# Optimizing a Trainium2 kernel written in Bass

```python
import numpy as np
import jax
import jax.numpy as jnp

def _softmax(x, axis=-1):
    return jax.nn.softmax(x, axis=axis)

def _gelu(x):
    return jax.nn.gelu(x, approximate=True)

def _silu(x):
    return jax.nn.silu(x)

def _sigmoid(x):
    return jax.nn.sigmoid(x)

def _layernorm(x, axis=-1, eps=1e-05):
    m = jnp.mean(x, axis=axis, keepdims=True)
    v = jnp.var(x, axis=axis, keepdims=True)
    return (x - m) / jnp.sqrt(v + eps)

def _scatter_add(tgt, idx, src, axis=0):
    return tgt.at[idx].add(src)

def _segment_sum(src, seg, n):
    return jax.ops.segment_sum(src, seg, n)
kernel_name = 'mk_decoder_postln_d1_seqx_r8_991e30'

def setup_inputs(seed: int=0):
    np.random.seed(seed)
    _w = jnp.asarray

    def _rec_inputs():
        import jax
        import jax.numpy as jnp
        _rk = jax.random.key(seed)
        x = -0.0003929 + 0.9999 * jax.random.normal(jax.random.fold_in(_rk, 1), (64, 128, 128), jnp.float32)
        _lenS = 128 - jax.random.randint(jax.random.fold_in(_rk, 7), (64,), 0, max(1, 128 // 4) + 1, jnp.int32)
        _lenS2 = 77 - jax.random.randint(jax.random.fold_in(_rk, 8), (64,), 0, max(1, 77 // 4) + 1, jnp.int32)
        _ctx_768P = jax.random.normal(jax.random.fold_in(_rk, 11), (64, 16, 96), jnp.float32)
        _ctx_768c = jax.random.dirichlet(jax.random.fold_in(_rk, 511), 0.3 * jnp.ones((16,), jnp.float32), (64, 77))
        _ctx_768t = jnp.einsum('bsk,bkd->bsd', _ctx_768c, _ctx_768P)
        _ctx_768t = _ctx_768t * jax.lax.rsqrt(jnp.mean(jnp.square(_ctx_768t)) + 1e-12) * 0.953939
        ctx_768 = 0.00095986 + 0.999812 * (_ctx_768t + 0.3 * jax.random.normal(jax.random.fold_in(_rk, 611), (64, 77, 96), jnp.float32))
        _validS = jnp.arange(128)[None, :] < _lenS[:, None]
        _validS2 = jnp.arange(77)[None, :] < _lenS2[:, None]
        _causal = jnp.tril(jnp.ones((128, 128), dtype=bool))
        mask_BxS2_bf1 = jnp.ones((64, 77), dtype=bool)
        return (x, ctx_768, mask_BxS2_bf1)
    x, ctx_768, mask_BxS2_bf1 = _rec_inputs()

    def _L0_attn_setup():
        import jax, jax.numpy as jnp
        import numpy as np
        SPS_AMPLIFY = 1.5
        SPS_DAMPEN = 0.3
        SPS_DEEP_QUESTION = 0.1
        SPS_EXCLAIM = 0.85
        SPS_QUESTION = 0.25
        SPS_SUPER_EXCLAIM = 0.95
        B, S, D = (4, 256, 128)
        NUM_HEADS = 16
        HEAD_DIM = D // NUM_HEADS
        SCALE = HEAD_DIM ** (-0.5)

        def sps_pro(x):
            xn = jax.nn.sigmoid(x)
            mult = jnp.where(xn > SPS_SUPER_EXCLAIM, 2.0, jnp.where(xn > SPS_EXCLAIM, SPS_AMPLIFY, jnp.where(xn < SPS_DEEP_QUESTION, 0.1, jnp.where(xn < SPS_QUESTION, SPS_DAMPEN, 1.0))))
            return x * mult
        key = jax.random.key(seed)
        k0, k1, k2, k3, k4 = jax.random.split(key, 5)
        s = 1.0 / np.sqrt(D)
        return {'x': jax.random.normal(k0, (B, S, D), dtype=jnp.float32), 'W_qkv': jax.random.uniform(k1, (D, 3 * D), dtype=jnp.float32, minval=-s, maxval=s), 'b_qkv': jax.random.uniform(k2, (3 * D,), dtype=jnp.float32, minval=-s, maxval=s), 'W_proj': jax.random.uniform(k3, (D, D), dtype=jnp.float32, minval=-s, maxval=s), 'b_proj': jax.random.uniform(k4, (D,), dtype=jnp.float32, minval=-s, maxval=s)}
    _L0_attn_all = _L0_attn_setup()
    _L0_attn_in = {k: v for k, v in _L0_attn_all.items() if k in ('W_qkv', 'b_qkv', 'W_proj', 'b_proj')}
    del _L0_attn_all

    def _L0_xattn_setup():
        import jax, jax.numpy as jnp
        import numpy as np
        DIM = 128
        CTX_DIM = 96
        HEADS = 16
        key = jax.random.key(seed)
        ks = jax.random.split(key, 7)
        B, N, M = (4, 512, 32)
        x = jax.random.normal(ks[0], (B, N, DIM), dtype=jnp.float32)
        context = jax.random.normal(ks[1], (B, M, CTX_DIM), dtype=jnp.float32)
        context_mask = jnp.ones((B, M), dtype=bool)
        s_d = 1.0 / np.sqrt(DIM)
        s_c = 1.0 / np.sqrt(CTX_DIM)
        Wq = jax.random.normal(ks[2], (DIM, DIM), dtype=jnp.float32) * s_d
        Wk = jax.random.normal(ks[3], (CTX_DIM, DIM), dtype=jnp.float32) * s_c
        Wv = jax.random.normal(ks[4], (CTX_DIM, DIM), dtype=jnp.float32) * s_c
        Wo = jax.random.normal(ks[5], (DIM, DIM), dtype=jnp.float32) * s_d
        return {'x': x, 'context': context, 'context_mask': context_mask, 'Wq': Wq, 'Wk': Wk, 'Wv': Wv, 'Wo': Wo}
    _L0_xattn_all = _L0_xattn_setup()
    _L0_xattn_in = {k: v for k, v in _L0_xattn_all.items() if k in ('Wq', 'Wk', 'Wv', 'Wo')}
    del _L0_xattn_all

    def _L0_ffn_setup():
        import jax, jax.numpy as jnp
        import numpy as np
        T, Z, D_DIM = (8, 256, 128)
        N_EXP, P_SLOT, H = (64, 32, 128)
        LN_EPS = 1e-05
        key = jax.random.key(seed)
        k = jax.random.split(key, 5)
        s = 0.02
        return {'x': jax.random.normal(k[0], (T, Z, D_DIM), dtype=jnp.float32), 'phi_w': jax.random.normal(k[1], (N_EXP * P_SLOT, D_DIM), dtype=jnp.float32) * s, 'phi_b': jax.random.normal(k[2], (N_EXP * P_SLOT,), dtype=jnp.float32) * s, 'expert_w': jax.random.normal(k[3], (N_EXP, D_DIM, H), dtype=jnp.float32) * s, 'expert_b': jax.random.normal(k[4], (N_EXP, H), dtype=jnp.float32) * s}
    _L0_ffn_all = _L0_ffn_setup()
    _L0_ffn_in = {k: v for k, v in _L0_ffn_all.items() if k in ('phi_w', 'phi_b', 'expert_w', 'expert_b')}
    del _L0_ffn_all
    return {'x': x, 'ctx_768': ctx_768, 'mask_BxS2_bf1': mask_BxS2_bf1, 'L0_attn_W_qkv': _L0_attn_in['W_qkv'], 'L0_attn_b_qkv': _L0_attn_in['b_qkv'], 'L0_attn_W_proj': _L0_attn_in['W_proj'], 'L0_attn_b_proj': _L0_attn_in['b_proj'], 'L0_xattn_Wq': _L0_xattn_in['Wq'], 'L0_xattn_Wk': _L0_xattn_in['Wk'], 'L0_xattn_Wv': _L0_xattn_in['Wv'], 'L0_xattn_Wo': _L0_xattn_in['Wo'], 'L0_ffn_phi_w': _L0_ffn_in['phi_w'], 'L0_ffn_phi_b': _L0_ffn_in['phi_b'], 'L0_ffn_expert_w': _L0_ffn_in['expert_w'], 'L0_ffn_expert_b': _L0_ffn_in['expert_b']}

def reference(x, ctx_768, mask_BxS2_bf1, L0_attn_W_qkv, L0_attn_b_qkv, L0_attn_W_proj, L0_attn_b_proj, L0_xattn_Wq, L0_xattn_Wk, L0_xattn_Wv, L0_xattn_Wo, L0_ffn_phi_w, L0_ffn_phi_b, L0_ffn_expert_w, L0_ffn_expert_b):
    import jax
    import jax.numpy as jnp

    def _L0_attn_ref(x, W_qkv, b_qkv, W_proj, b_proj):
        import jax, jax.numpy as jnp
        import numpy as np
        SPS_AMPLIFY = 1.5
        SPS_DAMPEN = 0.3
        SPS_DEEP_QUESTION = 0.1
        SPS_EXCLAIM = 0.85
        SPS_QUESTION = 0.25
        SPS_SUPER_EXCLAIM = 0.95
        B, S, D = (4, 256, 128)
        NUM_HEADS = 16
        HEAD_DIM = D // NUM_HEADS
        SCALE = HEAD_DIM ** (-0.5)

        def sps_pro(x):
            xn = jax.nn.sigmoid(x)
            mult = jnp.where(xn > SPS_SUPER_EXCLAIM, 2.0, jnp.where(xn > SPS_EXCLAIM, SPS_AMPLIFY, jnp.where(xn < SPS_DEEP_QUESTION, 0.1, jnp.where(xn < SPS_QUESTION, SPS_DAMPEN, 1.0))))
            return x * mult
        qkv = jnp.einsum('bsd,de->bse', x, W_qkv) + b_qkv
        q, k, v = jnp.split(qkv, 3, axis=-1)
        attn = jnp.einsum('bsd,btd->bst', q, k) * SCALE
        attn = sps_pro(attn)
        attn = jax.nn.softmax(attn, axis=-1)
        out = jnp.einsum('bst,btd->bsd', attn, v)
        out = jnp.einsum('bsd,de->bse', out, W_proj) + b_proj
        return out

    def _L0_xattn_ref(x, context, context_mask, Wq, Wk, Wv, Wo):
        import jax, jax.numpy as jnp
        import numpy as np
        DIM = 128
        CTX_DIM = 96
        HEADS = 16
        B, N, _ = x.shape
        M = context.shape[1]
        hd = DIM // HEADS
        scale = hd ** (-0.5)
        q = (x @ Wq).reshape(B, N, HEADS, hd).transpose(0, 2, 1, 3)
        k = (context @ Wk).reshape(B, M, HEADS, hd).transpose(0, 2, 1, 3)
        v = (context @ Wv).reshape(B, M, HEADS, hd).transpose(0, 2, 1, 3)
        scores = jnp.einsum('bhid,bhjd->bhij', q, k) * scale
        max_neg = -jnp.finfo(scores.dtype).max
        scores = jnp.where(context_mask[:, None, None, :], scores, max_neg)
        attn = jax.nn.softmax(scores, axis=-1)
        out = jnp.einsum('bhij,bhjd->bhid', attn, v)
        out = out.transpose(0, 2, 1, 3).reshape(B, N, DIM)
        return out @ Wo

    def _L0_ffn_ref(x, phi_w, phi_b, expert_w, expert_b):
        import jax, jax.numpy as jnp
        import numpy as np
        T, Z, D_DIM = (8, 256, 128)
        N_EXP, P_SLOT, H = (64, 32, 128)
        LN_EPS = 1e-05
        t, z, d = x.shape
        n = expert_w.shape[0]
        p = phi_w.shape[0] // n
        logits = (jnp.einsum('tzd,ed->tze', x, phi_w) + phi_b).reshape(t, z, n, p)
        D = jax.nn.softmax(logits, axis=3)
        C = jax.nn.softmax(logits, axis=2)
        X_tilde = jnp.einsum('tznp,tzd->npd', D, x)
        X_tilde = jnp.clip(X_tilde, -33000.0, 65000.0)
        mu = jnp.mean(X_tilde, axis=-1, keepdims=True)
        var = jnp.mean(jnp.square(X_tilde - mu), axis=-1, keepdims=True)
        X_tilde = (X_tilde - mu) * jax.lax.rsqrt(var + LN_EPS)
        X_tilde = jnp.tanh(X_tilde)
        Y_tilde = jnp.einsum('npd,ndH->npH', X_tilde, expert_w) + expert_b[:, None, :]
        Y = jnp.einsum('tznp,npH->tzH', C, Y_tilde)
        return Y
    x = _layernorm(x + _L0_attn_ref(x, L0_attn_W_qkv, L0_attn_b_qkv, L0_attn_W_proj, L0_attn_b_proj), axis=-1)
    x = _layernorm(x + _L0_xattn_ref(x, ctx_768, mask_BxS2_bf1, L0_xattn_Wq, L0_xattn_Wk, L0_xattn_Wv, L0_xattn_Wo), axis=-1)
    x = _layernorm(x + _L0_ffn_ref(x, L0_ffn_phi_w, L0_ffn_phi_b, L0_ffn_expert_w, L0_ffn_expert_b), axis=-1)
    return x

_drawn_inputs = setup_inputs


def setup_inputs(seed=0):
    import zlib

    import numpy as np

    out = dict(_drawn_inputs(seed))
    spreads = {}
    factors = {'L0_ffn_phi_w': 2.683, 'L0_ffn_phi_b': 30.356}
    for name, (base, spread) in spreads.items():
        noise = np.random.default_rng([zlib.crc32(name.encode()), seed]).standard_normal(out[name].shape)
        drawn = base * np.exp(spread * noise) if base else spread * noise
        out[name] = jnp.asarray(drawn.astype(out[name].dtype))
    for name, factor in factors.items():
        out[name] = (out[name] * factor).astype(out[name].dtype)
    return out
```

```python
from contextlib import ExitStack

import numpy as np

import concourse.bass as bass
from concourse import mybir

ALU = mybir.AluOpType
ACT = mybir.ActivationFunctionType
X = mybir.AxisListType.X
F32 = mybir.dt.float32
F32R = mybir.dt.float32r
F16 = mybir.dt.float16
BF16 = mybir.dt.bfloat16
U8 = mybir.dt.uint8

B, S, D = 64, 128, 128
TOKENS = B * S
J, JP, CD = 77, 78, 96
HEADS, HD = 16, 8
SCALE = float(HD) ** -0.5
EXPERTS, SLOTS = 64, 32
NP = EXPERTS * SLOTS
EPS = 1e-5
FILL = float(np.uint32(0x7F7F0000).view(np.float32))

T_01, T_025, T_085, T_095 = (float(np.float32(np.log(p / (1 - p)))) for p in (0.1, 0.25, 0.85, 0.95))

C_IDENT, C_GSUM, C_HEAD, C_END = 0, 128, 256, 260


def constants():
    k = np.arange(128)
    c = np.zeros((128, C_END), np.float32)
    c[:, C_IDENT:C_GSUM] = np.eye(128)
    c[:, C_GSUM:C_HEAD] = k[:, None] % 8 == k[None, :] % 8
    c[:, C_HEAD:C_END] = (k[:, None] % 32) // HD == np.arange(4)[None, :]
    return c


class Item:

    def __init__(self, i, c):
        self.known = isinstance(i, int)
        self.par = c % 2
        self.half = i + c // 2
        self.n = i * 2 + c

    def __sub__(self, s):
        return Item(self.half, self.par - s)

    def __add__(self, s):
        return Item(self.half, self.par + s)

    def within(self, n):
        return not self.known or 0 <= self.n < n

    def after(self, per, c):
        return self.n * per + c

    def turn(self, per, c):
        return self.half * per + c


def steps(eng, n, lag, step):
    lo = (lag + 3) // 2
    hi = n // 2
    for k in range(2 * lo):
        step(Item(k // 2, k % 2))
    with eng.Fori(lo, hi) as i:
        step(Item(i, 0))
        step(Item(i, 1))
    for k in range(2 * hi, n + lag):
        step(Item(k // 2, k % 2))


def reach(eng, sem, value):
    if not isinstance(value, int) or value > 0:
        eng.wait_ge(sem, value)


class Store:

    def __init__(self, nc, ctx, stage):
        self.nc, self.ctx, self.stage = nc, ctx, stage

    def sb(self, name, shape, dt=F32):
        return self.ctx.enter_context(self.nc.sbuf_tensor(f"{self.stage}_{name}", shape, dt))

    def ps(self, name, shape, dt=F32):
        return self.ctx.enter_context(self.nc.psum_tensor(f"{self.stage}_{name}", shape, dt))

    def sem(self, name):
        return self.ctx.enter_context(self.nc.semaphore(f"{self.stage}_{name}"))


def setup(nc, io, w):
    with ExitStack() as ctx:
        st = Store(nc, ctx, "setup")
        wT = st.sb("wT", [128, 3, 128])
        wproj = st.sb("wproj", [128, 128])
        bqkv = st.sb("bqkv", [128, 3])
        bproj = st.sb("bproj", [1, 128])
        brep = st.sb("brep", [128, 2, 128])
        ones = st.sb("ones", [128, 128])
        mask = st.sb("mask", [128, B * J], U8)
        pa = st.ps("pa", [128, 512])
        pb = st.ps("pb", [128, 512])
        loaded, mask_clear, mask_loaded, rep, folded, evac = (
            st.sem(n) for n in ("loaded", "mask_clear", "mask_loaded", "rep", "folded", "evac"))
        block = ctx.enter_context(nc.Block())
        loads = [(w.consts, io["consts"]), (wT, io["w_qkvT"].rearrange("(c e) d -> e c d", c=3)),
                 (wproj, io["w_proj"]), (bqkv, io["b_qkv"]), (bproj, io["b_proj"]), (w.xq, io["xq"]),
                 (w.xk, io["xk"]), (w.xv, io["xv"]), (w.xo, io["xo"])]
        LOADED = 16 * len(loads)
        ROWS = range(0, 128, 32)

        @block.sync
        def _(sync):
            for dst, src in loads:
                sync.dma_start(dst[:], src).then_inc(loaded, 16)
            sync.wait_ge(mask_clear, 1)
            for p in ROWS:
                sync.dma_start(mask[p:p + 1, :], io["mask"]).then_inc(mask_loaded, 16)

        @block.vector
        def _(dve):
            dve.memset(mask[:].bitcast(mybir.dt.uint32), 0).then_inc(mask_clear, 1)
            dve.memset(ones[:], 1.0).then_inc(rep, 1)
            dve.wait_ge(loaded, LOADED)
            dve.wait_ge(rep, 1)
            for n, c in enumerate((0, 2)):
                dve.tensor_scalar(brep[:, n, :], ones[:], bqkv[:, c:c + 1], None, ALU.mult).then_inc(rep, 1)
            dve.tensor_copy(w.ident16[:], w.ident)
            dve.memset(w.neg_half[:], -0.5)
            dve.memset(w.eps[:], EPS)
            dve.tensor_scalar(w.neg_ident[:], w.ident, -1.0, None, ALU.mult)
            dve.tensor_scalar(w.xqs[:], w.xq[:], SCALE, None, ALU.mult)
            dve.memset(w.ones16[:], 1.0)
            dve.wait_ge(mask_loaded, 16 * len(ROWS))
            dve.memset(w.fill[:].rearrange("a (b t) -> a b t", t=JP)[:, :, J], -FILL)
            dve.tensor_scalar(w.fill[:].rearrange("a (b t) -> a b t", t=JP)[:, :, 0:J],
                              mask[:].rearrange("a (b t) -> a b t", t=J), 1.0, FILL, ALU.subtract, ALU.mult)
            dve.wait_ge(folded, 1)
            dve.tensor_copy(w.m[:], pa[:, 0:128])
            dve.tensor_copy(w.w2[:], pa[:, 128:256])
            dve.tensor_copy(w.cvec[:], pb[:, 0:1])
            dve.tensor_copy(w.avec[:], pb[:, 1:2])
            dve.tensor_copy(w.beta[:], pb[:, 2:3])
            dve.tensor_copy(w.b2[:], pb[:, 128:256]).then_inc(evac, 1)

        @block.tensor
        def _(pe):
            pe.wait_ge(loaded, LOADED)
            pe.wait_ge(rep, 3)
            pe.matmul(pa[:, 0:128], wT[:, 0, :], wT[:, 1, :], start=True, stop=True)
            pe.matmul(pa[:, 128:256], wT[:, 2, :], wproj[:], start=True, stop=True)
            pe.matmul(pb[:, 0:1], wT[:, 1, :], bqkv[:, 0:1], start=True, stop=True)
            pe.matmul(pb[:, 1:2], wT[:, 0, :], bqkv[:, 1:2], start=True, stop=True)
            pe.matmul(pb[:, 2:3], brep[:, 0, :], bqkv[:, 1:2], start=True, stop=True)
            pe.matmul(pb[:, 128:256], brep[:, 1, :], wproj[:], start=True, stop=False)
            pe.matmul(pb[:, 128:256], ones[0:1, :], bproj[:], start=False, stop=True).then_inc(folded, 1)


def attention(nc, io, w):
    GB = 4
    GROUPS = B // GB
    x_in = io["x"].rearrange("(q b s) d -> q s b d", q=4, s=S)
    with ExitStack() as ctx:
        st = Store(nc, ctx, "attn")
        xTg = [st.sb(f"xTg{i}", [128, GB * 128]) for i in range(2)]
        uT = st.sb("uT", [128, 512])
        vp = [st.sb(f"vp{i}", [128, 512]) for i in range(2)]
        rb = st.sb("rb", [128, GB])
        a = [st.sb(f"a{i}", [128, 512]) for i in range(2)]
        band = [st.sb(f"band{i}", [128, 512]) for i in range(6)]
        f2 = [st.sb(f"f2{i}", [128, 512]) for i in range(2)]
        mx = st.sb("mx", [128, GB])
        nb = [st.sb(f"nb{i}", [128, GB]) for i in range(2)]
        pr = [st.sb(f"pr{i}", [128, 512]) for i in range(2)]
        sums = [st.sb(f"sums{i}", [128, GB]) for i in range(2)]
        pT = [st.sb(f"pT{i}", [128, 512]) for i in range(2)]
        rinv = st.sb("rinv", [128, GB])
        y = [st.sb(f"y{i}", [128, GB, 128]) for i in range(2)]
        stats = st.sb("stats", [128, GB, 6])
        mv = [st.sb(f"mv{i}", [128, GB, 2]) for i in range(2)]
        veps = st.sb("veps", [128, GB])
        rstd = [st.sb(f"rstd{i}", [128, GB]) for i in range(2)]
        x1 = [st.sb(f"x1{i}", [128, GB * 128]) for i in range(2)]
        psU, psV, psR, psS, psT, psO, psX = (st.ps(n, [128, 512]) for n in ("U", "V", "R", "S", "T", "O", "X"))
        xT_loaded = [st.sem("xT_loaded0"), st.sem("xT_loaded1")]
        x_loaded = [st.sem(f"x_loaded{q}") for q in range(4)]
        (u_made, v_made, s_made, uT_ready, v_ready, rb_ready, a_ready, f_ready, p_ready, pT_made, pT_ready,
         o_made, mv_ready, rstd_ready, x1_ready, x1T_made, x1T_kept, x1_kept, low_ready, band_done, f2_done,
         mx_done, y_chain, pool_chain) = (
            st.sem(n) for n in ("u_made", "v_made", "s_made", "uT_ready", "v_ready", "rb_ready", "a_ready",
                                "f_ready", "p_ready", "pT_made", "pT_ready", "o_made", "mv_ready",
                                "rstd_ready", "x1_ready", "x1T_made", "x1T_kept", "x1_kept", "low_ready",
                                "band_done", "f2_done", "mx_done", "y_chain", "pool_chain"))
        block = ctx.enter_context(nc.Block())

        @block.gpsimd
        def _(pool):
            for q in range(4):
                pool.dma_start(w.xres[:, q * 2048:(q + 1) * 2048].rearrange("s (b d) -> s b d", d=D), x_in[q])\
                    .then_inc(x_loaded[q], 16)

            def step(k):
                g = k - 1
                if g.within(GROUPS):
                    pool.wait_ge(band_done, g.after(3, 1))
                    pool.tensor_tensor(band[4][:], band[1][:], band[2][:], ALU.add).then_inc(low_ready, 1)
                g = k - 3
                if g.within(GROUPS):
                    pool.wait_ge(x1_ready, g.after(1, 1))
                    pool.tensor_copy(w.xres[:, bass.ds(g.n * 512, 512)], x1[g.par][:]).then_inc(x1_kept, 1)
                g = k - 2
                if g.within(GROUPS):
                    pool.wait_ge(mv_ready, g.after(1, 1))
                    pool.tensor_tensor(veps[:], mv[g.par][:, :, 1], w.eps[:, 0:GB], ALU.add).then_inc(pool_chain, 1)
                    pool.wait_ge(pool_chain, g.after(1, 1))
                    pool.tensor_tensor(rstd[g.par][:], veps[:], w.neg_half[:, 0:GB], ALU.pow).then_inc(rstd_ready, 1)
            steps(pool, GROUPS, 3, step)

        @block.sync
        def _(sync):
            def step(g):
                if not g.within(GROUPS):
                    return
                reach(sync, s_made, g.after(1, -1))
                sync.dma_start(xTg[g.par][:], io["xT"][:, bass.ds(g.n * 512, 512)]).then_inc(xT_loaded[g.par], 16)
            steps(sync, GROUPS, 0, step)

        @block.tensor
        def _(pe):
            def step(k):
                g = k - 2
                if g.within(GROUPS):
                    pe.wait_ge(p_ready, g.after(1, 1))
                    reach(pe, pT_ready, g.after(1, 0))
                    for b in range(GB):
                        c = slice(b * 128, (b + 1) * 128)
                        ins = pe.transpose(psT[:, c], pr[g.par][:, c], w.ident)
                    ins.then_inc(pT_made, 1)
                g = k
                if g.within(GROUPS):
                    pe.wait_ge(xT_loaded[g.par], g.turn(16, 16))
                    reach(pe, uT_ready, g.after(1, 0))
                    pe.matmul(psU[:], w.m[:], xTg[g.par][:], start=True, stop=True).then_inc(u_made, 1)
                g = k - 2
                if g.within(GROUPS):
                    pe.wait_ge(pT_ready, g.after(1, 1))
                    reach(pe, mv_ready, g.after(1, 0))
                    for b in range(GB):
                        c = slice(b * 128, (b + 1) * 128)
                        ins = pe.matmul(psO[:, c], pT[g.par][:, c], vp[g.par][:, c], start=True, stop=True)
                    ins.then_inc(o_made, 1)
                g = k
                if g.within(GROUPS):
                    reach(pe, v_ready, g.after(1, 0))
                    reach(pe, rb_ready, g.after(1, 0))
                    for b in range(GB):
                        xb = xTg[g.par][:, b * 128:(b + 1) * 128]
                        pe.matmul(psV[:, b * 128:(b + 1) * 128], xb, w.w2[:], start=True, stop=True)
                        ins = pe.matmul(psR[:, b:b + 1], xb, w.avec[:], start=True, stop=True)
                    ins.then_inc(v_made, 1)
                    pe.wait_ge(uT_ready, g.after(1, 1))
                    reach(pe, a_ready, g.after(1, 0))
                    for b in range(GB):
                        c = slice(b * 128, (b + 1) * 128)
                        ins = pe.matmul(psS[:, c], uT[:, c], xTg[g.par][:, c], start=True, stop=True)
                    ins.then_inc(s_made, 1)
                g = k - 3
                if g.within(GROUPS):
                    pe.wait_ge(x1_ready, g.after(1, 1))
                    reach(pe, x1T_kept, g.after(1, 0))
                    for b in range(GB):
                        c = slice(b * 128, (b + 1) * 128)
                        ins = pe.transpose(psX[:, c], x1[g.par][:, c], w.ident)
                    ins.then_inc(x1T_made, 1)
            steps(pe, GROUPS, 3, step)

        @block.scalar
        def _(act):
            def step(k):
                g = k - 2
                if g.within(GROUPS):
                    act.wait_ge(pT_made, g.after(1, 1))
                    reach(act, o_made, g.after(1, -1))
                    act.copy(pT[g.par][:], psT[:]).then_inc(pT_ready, 1)
                g = k
                if g.within(GROUPS):
                    act.wait_ge(u_made, g.after(1, 1))
                    reach(act, s_made, g.after(1, 0))
                    act.activation(uT[:], psU[:], ACT.Identity, bias=w.cvec[:]).then_inc(uT_ready, 1)
                g = k - 1
                if g.within(GROUPS):
                    act.wait_ge(f_ready, g.after(1, 1))
                    reach(act, pT_made, g.after(1, -1))
                    reach(act, mv_ready, g.after(1, -1))
                    for b in range(GB):
                        c = slice(b * 128, (b + 1) * 128)
                        ins = act.activation(pr[g.par][:, c], f2[g.par][:, c], ACT.Exp, bias=nb[g.par][:, b:b + 1],
                                             scale=0.5, accum_out=sums[g.par][:, b:b + 1])
                    ins.then_inc(p_ready, 1)
                g = k
                if g.within(GROUPS):
                    act.wait_ge(rb_ready, g.after(1, 1))
                    act.wait_ge(s_made, g.after(1, 1))
                    reach(act, f_ready, g.after(1, -1))
                    for b in range(GB):
                        c = slice(b * 128, (b + 1) * 128)
                        ins = act.activation(a[g.par][:, c], psS[:, c], ACT.Identity, bias=rb[:, b:b + 1],
                                             scale=SCALE)
                    ins.then_inc(a_ready, 1)
                g = k - 3
                if g.within(GROUPS):
                    act.wait_ge(x1T_made, g.after(1, 1))
                    act.copy(w.x1T[:, bass.ds(g.n * 512, 512)], psX[:]).then_inc(x1T_kept, 1)
            steps(act, GROUPS, 3, step)

        @block.vector
        def _(dve):
            for q in range(4):
                dve.wait_ge(x_loaded[q], 16)

            def step(k):
                g = k - 1
                if g.within(GROUPS):
                    dve.wait_ge(a_ready, g.after(1, 1))
                    reach(dve, f_ready, g.after(1, 0))
                    av = a[g.par][:]
                    dve.tensor_scalar(band[0][:], av, T_095, 2.0, ALU.is_gt, ALU.add)
                    dve.tensor_scalar(band[1][:], av, T_025, -1.4, ALU.is_lt, ALU.mult)
                    dve.tensor_scalar(band[2][:], av, T_01, -0.4, ALU.is_lt, ALU.mult).then_inc(band_done, 1)
                    dve.wait_ge(band_done, g.after(3, 1))
                    dve.scalar_tensor_tensor(out=band[3][:], in0=av, scalar=T_085, in1=band[0][:],
                                             op0=ALU.is_gt, op1=ALU.add).then_inc(band_done, 1)
                g = k - 3
                if g.within(GROUPS):
                    dve.wait_ge(rstd_ready, g.after(1, 1))
                    reach(dve, x1T_kept, g.after(1, -1))
                    reach(dve, x1_kept, g.after(1, -1))
                    for b in range(GB):
                        ins = dve.tensor_scalar(x1[g.par][:, b * 128:(b + 1) * 128], y[g.par][:, b, :],
                                                mv[g.par][:, b, 0:1], rstd[g.par][:, b:b + 1],
                                                ALU.subtract, ALU.mult)
                    ins.then_inc(x1_ready, 1)
                g = k - 1
                if g.within(GROUPS):
                    dve.wait_ge(band_done, g.after(3, 2))
                    dve.wait_ge(low_ready, g.after(1, 1))
                    dve.tensor_tensor(band[5][:], band[4][:], band[3][:], ALU.add).then_inc(band_done, 1)
                    dve.wait_ge(band_done, g.after(3, 3))
                    reach(dve, p_ready, g.after(1, -1))
                    dve.tensor_tensor(f2[g.par][:], band[5][:], av, ALU.mult).then_inc(f2_done, 1)
                    dve.wait_ge(f2_done, g.after(1, 1))
                    dve.tensor_reduce(mx[:], f2[g.par][:].rearrange("p (b t) -> p b t", b=GB), X, ALU.max)\
                       .then_inc(mx_done, 1)
                    dve.wait_ge(mx_done, g.after(1, 1))
                    dve.tensor_scalar(nb[g.par][:], mx[:], -0.5, None, ALU.mult).then_inc(f_ready, 1)
                g = k
                if g.within(GROUPS):
                    dve.wait_ge(v_made, g.after(1, 1))
                    reach(dve, a_ready, g.after(1, 0))
                    dve.tensor_scalar(rb[:], psR[:, 0:GB], w.beta[:], SCALE, ALU.add, ALU.mult).then_inc(rb_ready, 1)
                    reach(dve, o_made, g.after(1, -1))
                    dve.tensor_tensor(vp[g.par][:].rearrange("p (b e) -> p b e", b=GB),
                                      psV[:].rearrange("p (b e) -> p b e", b=GB),
                                      w.b2[:].unsqueeze(1).to_broadcast([128, GB, 128]), ALU.add).then_inc(v_ready, 1)
                g = k - 2
                if g.within(GROUPS):
                    dve.wait_ge(o_made, g.after(1, 1))
                    dve.wait_ge(p_ready, g.after(1, 1))
                    reach(dve, mv_ready, g.after(1, 0))
                    dve.reciprocal(rinv[:], sums[g.par][:]).then_inc(y_chain, 1)
                    dve.wait_ge(y_chain, g.after(3, 1))
                    reach(dve, x1_ready, g.after(1, -1))
                    for b in range(GB):
                        c = slice(b * 128, (b + 1) * 128)
                        ins = dve.scalar_tensor_tensor(out=y[g.par][:, b, :], in0=psO[:, c], scalar=rinv[:, b:b + 1],
                                                       in1=w.xres[:, bass.ds(g.n * 512 + b * 128, 128)],
                                                       op0=ALU.mult, op1=ALU.add)
                    ins.then_inc(y_chain, 1)
                    dve.wait_ge(y_chain, g.after(3, 2))
                    for b in range(GB):
                        ins = dve.bn_stats(stats[:, b, :], y[g.par][:, b, :])
                    ins.then_inc(y_chain, 1)
                    dve.wait_ge(y_chain, g.after(3, 3))
                    dve.memset(w.scratch[:], 0.0)
                    for b in range(GB):
                        ins = dve.bn_aggr(mv[g.par][:, b, :], stats[:, b, :])
                    ins.then_inc(mv_ready, 1)
            steps(dve, GROUPS, 3, step)


def attend_context(nc, io, w):
    PAIRS = B // 2
    HW = 4 * JP
    with ExitStack() as ctx:
        st = Store(nc, ctx, "cross")
        cg = [st.sb(f"cg{i}", [CD, 2 * JP]) for i in range(2)]
        qh = [st.sb(f"qh{i}", [128, 256], F32R) for i in range(2)]
        ql = [st.sb(f"ql{i}", [128, 256], F32R) for i in range(2)]
        fp = [st.sb(f"fp{i}", [128, 2, JP], BF16) for i in range(2)]
        kc = st.sb("kc", [128, 2 * JP])
        kb = st.sb("kb", [128, 2, 4, JP])
        kbh = [st.sb(f"kbh{i}", [128, 2, 4, JP], F32R) for i in range(2)]
        kbl = [st.sb(f"kbl{i}", [128, 2, 4, JP], F32R) for i in range(2)]
        v32 = st.sb("v32", [J, 256])
        vr = [st.sb(f"vr{i}", [J, 256]) for i in range(2)]
        vs = [st.sb(f"vs{i}", [J, 2, HEADS, 3, 9], BF16) for i in range(2)]
        mx = [st.sb(f"mx{i}", [128, 2, 4], F32R) for i in range(2)]
        p32 = [st.sb(f"p32{i}", [128, 2, HW]) for i in range(2)]
        ph = [st.sb(f"ph{i}", [128, 2, HW], F16) for i in range(2)]
        pl = [st.sb(f"pl{i}", [128, 2, HW], F16) for i in range(2)]
        pTh = [st.sb(f"pTh{i}", [J, 8, 128], F16) for i in range(2)]
        pTl = [st.sb(f"pTl{i}", [J, 8, 128], F16) for i in range(2)]
        o9 = st.sb("o9", [128, HEADS, 9])
        orec = st.sb("orec", [128, HEADS])
        on = st.sb("on", [128, 128])
        oT = st.sb("oT", [128, 128])
        y = [st.sb(f"y{i}", [128, 128]) for i in range(2)]
        stats = st.sb("stats", [128, 6])
        mv = [st.sb(f"mv{i}", [128, 2]) for i in range(2)]
        veps = st.sb("veps", [128, 1])
        rstd = [st.sb(f"rstd{i}", [128, 1]) for i in range(2)]
        xp = [st.sb(f"xp{i}", [128, 128]) for i in range(2)]
        psL = [st.ps(f"L{i}", [128, 2, 512]) for i in range(2)]
        psTh = st.ps("Th", [J, 8, 128], F16)
        psTl = st.ps("Tl", [J, 8, 128], F16)
        psA = st.ps("A", [128, 512])
        psM = st.ps("M", [128, 512])
        QUERY, KEY = slice(0, 256), slice(256, 256 + 2 * JP)
        c_loaded = [st.sem("c_loaded0"), st.sem("c_loaded1")]
        qk_made, qh_ready, ql_ready, kc_ready, kb_done, kbh_ready, kbl_ready, v_made, v32_ready, v_split, vs_ready = (
            st.sem(n) for n in ("qk_made", "qh_ready", "ql_ready", "kc_ready", "kb_done", "kbh_ready",
                                "kbl_ready", "v_made", "v32_ready", "v_split", "vs_ready"))
        s_made, mx_ready, shifted, ph_ready, p32_ready, pl_ready, t_made, pTh_ready, pTl_ready, av_made = (
            st.sem(n) for n in ("s_made", "mx_ready", "shifted", "ph_ready", "p32_ready", "pl_ready", "t_made",
                                "pTh_ready", "pTl_ready", "av_made"))
        o_sum, o_rec, on_ready, oT_made, oT_ready, pj_made, y_done, st_done, mv_ready, ve_done, rstd_ready, x2_ready, xT_made, xh_ready, xl_ready = (
            st.sem(n) for n in ("o_sum", "o_rec", "on_ready", "oT_made", "oT_ready", "pj_made", "y_done", "st_done",
                                "mv_ready", "ve_done", "rstd_ready", "x2_ready", "xT_made", "xh_ready", "xl_ready"))
        consts_set, fp_ready = st.sem("consts_set"), st.sem("fp_ready")
        block = ctx.enter_context(nc.Block())

        def earlier(r, j, s):
            return (r, j - s) if j >= s else (r - 1, j - s + 4)

        @block.sync
        def _(sync):
            def step(r):
                if r.within(PAIRS):
                    reach(sync, v_made, r.after(1, -1))
                    sync.dma_start(cg[r.par][:], io["ctxT"][:, bass.ds(r.n * 2 * JP, 2 * JP)])\
                        .then_inc(c_loaded[r.par], 16)
            steps(sync, PAIRS, 0, step)

        @block.tensor
        def _(pe):
            pe.wait_ge(consts_set, 1)

            def queries_keys(r, _):
                pe.wait_ge(c_loaded[r.par], r.turn(16, 16))
                pe.matmul(psM[:, QUERY], w.xqs[:], w.x1T[:, bass.ds(r.n * 256, 256)], start=True, stop=True)
                pe.matmul(psM[:, KEY], w.xk[:], cg[r.par][:], start=True, stop=True).then_inc(qk_made, 1)

            def own_values(r, _):
                for b in range(2):
                    ins = pe.matmul(psM[0:J, b * 128:(b + 1) * 128], cg[r.par][:, b * JP:b * JP + J], w.xv[:],
                                    start=True, stop=True)
                ins.then_inc(v_made, 1)

            def turn_out(r, b):
                pe.wait_ge(on_ready, r.after(2, b + 1))
                pe.transpose(psM[:, 0:128], on[:], w.ident).then_inc(oT_made, 1)

            def project(r, b):
                pe.wait_ge(oT_ready, r.after(2, b + 1))
                pe.matmul(psM[:, 0:128], oT[:], w.xo[:], start=True, stop=True).then_inc(pj_made, 1)

            def turn_x2(r, b):
                pe.wait_ge(x2_ready, r.after(2, b + 1))
                pe.transpose(psM[:, 0:128], xp[b][:], w.ident).then_inc(xT_made, 1)

            USES = [(queries_keys, ql_ready, 0, None), (project, y_done, 3, 1), (turn_out, oT_ready, 2, 0),
                    (own_values, v32_ready, 0, None), (project, y_done, 2, 0), (turn_x2, xl_ready, 3, 1),
                    (turn_out, oT_ready, 2, 1), (turn_x2, xl_ready, 2, 0)]

            def use_bank(k, n):
                make, _, lag, b = USES[n]
                if not (k - lag).within(PAIRS):
                    return
                for back in range(1, 17):
                    m = n - back
                    _, read, lag_m, b_m = USES[m % 8]
                    r = k - lag_m + m // 8
                    if r.within(PAIRS):
                        pe.wait_ge(read, r.after(1, 1) if b_m is None else r.after(2, b_m + 1))
                        break
                make(k - lag, b)

            def scores(r, j):
                if j == 0:
                    pe.wait_ge(fp_ready, r.after(1, 1))
                    pe.wait_ge(kbh_ready, r.after(1, 1))
                    pe.wait_ge(kbl_ready, r.after(1, 1))
                reach(pe, p32_ready, r.after(4, j - 1))
                b, bc = j // 2, slice(j // 2 * 128, j // 2 * 128 + 128)
                for i in range(2):
                    g = 32 * (2 * (j % 2) + i)
                    gr = slice(g, g + 32)
                    out = psL[j % 2][:, i, 0:HW]
                    kh_, kl_ = kbh[r.par][gr, b, :, :], kbl[r.par][gr, b, :, :]
                    pe.matmul(out, qh[r.par][gr, bc], kh_, start=True, stop=False)
                    pe.matmul(out, ql[r.par][gr, bc], kh_, start=False, stop=False)
                    pe.matmul(out, qh[r.par][gr, bc], kl_, start=False, stop=False)
                    fill = fp[r.par][g:g + 1, b, :].unsqueeze(1).to_broadcast([1, 4, JP])
                    ins = pe.matmul(out, w.ones16[g:g + 1, :], fill, start=False, stop=True)
                ins.then_inc(s_made, 1)

            def shift(r, j):
                pe.wait_ge(mx_ready, r.after(4, j + 1))
                for i in range(2):
                    ins = pe.matmul(psL[j % 2][:, i, 0:HW], w.neg_ident[:],
                                    mx[j % 2][:, i, :].unsqueeze(2).to_broadcast([128, 4, JP]),
                                    start=False, stop=True, skip_group_check=True)
                ins.then_inc(shifted, 1)

            def turn(r, j):
                pe.wait_ge(ph_ready, r.after(4, j + 1))
                pe.wait_ge(pl_ready, r.after(4, j + 1))
                reach(pe, pTh_ready, r.after(4, j))
                reach(pe, pTl_ready, r.after(4, j))
                for h in range(8):
                    c = slice(h % 4 * JP, h % 4 * JP + J)
                    pe.transpose(psTh[:, h, :], ph[j % 2][:, h // 4, c], w.ident16[:])
                    ins = pe.transpose(psTl[:, h, :], pl[j % 2][:, h // 4, c], w.ident16[:])
                ins.then_inc(t_made, 1)

            def values(r, j):
                if j == 0:
                    pe.wait_ge(vs_ready, r.after(1, 1))
                if j % 2 == 0:
                    reach(pe, o_sum, r.after(2, j // 2))
                pe.wait_ge(pTh_ready, r.after(4, j + 1))
                pe.wait_ge(pTl_ready, r.after(4, j + 1))
                for h in range(8):
                    head = 8 * (j % 2) + h
                    v = vs[r.par][:, j // 2, head, :, :]
                    pe.matmul(psA[:, head * 27:head * 27 + 27], pTh[j % 2][:, h, :], v, start=True, stop=True)
                    ins = pe.matmul(psA[:, head * 27:head * 27 + 18], pTl[j % 2][:, h, :], v[:, 0:2, :],
                                    start=False, stop=True, skip_group_check=True)
                ins.then_inc(av_made, 1)

            def step(k):
                r = k - 1
                for j in range(4):
                    if r.within(PAIRS):
                        scores(r, j)
                    use_bank(k, 2 * j)
                    r3, j3 = earlier(r, j, 3)
                    if r3.within(PAIRS):
                        values(r3, j3)
                    r2, j2 = earlier(r, j, 2)
                    if r2.within(PAIRS):
                        turn(r2, j2)
                    use_bank(k, 2 * j + 1)
                    if r.within(PAIRS):
                        shift(r, j)
            steps(pe, PAIRS, 3, step)

        @block.scalar
        def _(act):
            def keep_out(r, b):
                act.wait_ge(oT_made, r.after(2, b + 1))
                reach(act, pj_made, r.after(2, b))
                act.copy(oT[:], psM[:, 0:128]).then_inc(oT_ready, 1)

            def keep_high(r, b):
                act.wait_ge(xT_made, r.after(2, b + 1))
                act.copy(w.xh[:, bass.ds(r.n * 256 + b * 128, 128)], psM[:, 0:128]).then_inc(xh_ready, 1)

            def step(k):
                r = k - 1
                for j in range(4):
                    if j == 0 and k.within(PAIRS):
                        act.wait_ge(qk_made, k.after(1, 1))
                        reach(act, shifted, (k - 1).after(4, 0))
                        reach(act, kb_done, k.after(1, 0))
                        act.copy(kc[:], psM[:, KEY]).then_inc(kc_ready, 1)
                        act.copy(qh[k.par][:], psM[:, QUERY]).then_inc(qh_ready, 1)
                    if j == 2 and k.within(PAIRS):
                        act.copy(fp[k.par][:], w.fill[:, bass.ds(k.n * 2 * JP, 2 * JP)]
                                 .rearrange("p (b t) -> p b t", b=2)).then_inc(fp_ready, 1)
                    if j % 2 and (k - 2).within(PAIRS):
                        keep_out(k - 2, j // 2)
                    r2, j2 = earlier(r, j, 2)
                    if r2.within(PAIRS):
                        act.wait_ge(t_made, r2.after(4, j2 + 1))
                        reach(act, av_made, r2.after(4, j2 - 1))
                        act.copy(pTl[j % 2][:], psTl[:]).then_inc(pTl_ready, 1)
                    if j == 1 and k.within(PAIRS):
                        act.wait_ge(v_made, k.after(1, 1))
                        reach(act, v_split, k.after(4, -2))
                        act.copy(v32[:], psM[0:J, 0:256]).then_inc(v32_ready, 1)
                    if j == 2 and (k - 3).within(PAIRS):
                        keep_high(k - 3, 1)
                    if j == 3 and (k - 2).within(PAIRS):
                        keep_high(k - 2, 0)
                    if r.within(PAIRS):
                        act.wait_ge(shifted, r.after(4, j + 1))
                        reach(act, t_made, r.after(4, j - 1))
                        reach(act, pl_ready, r.after(4, j - 1))
                        act.activation(ph[j % 2][:], psL[j % 2][:, :, 0:HW], ACT.Exp).then_inc(ph_ready, 1)
                        act.activation(p32[j % 2][:], psL[j % 2][:, :, 0:HW], ACT.Exp).then_inc(p32_ready, 1)
            steps(act, PAIRS, 3, step)

        @block.vector
        def _(dve):
            for i in range(2):
                dve.memset(xp[i][:, 127:128], 1.0)
                dve.memset(vs[i][:, :, :, 0, 8], 1.0)
                ins = dve.memset(vs[i][:, :, :, 1:3, 8], 0.0)
            ins.then_inc(consts_set, 1)
            dve.wait_ge(consts_set, 1)

            def part(r, c):
                return vs[r.par][:, :, :, c, 0:8]

            def as_heads(t):
                return t[:].rearrange("j (b h e) -> j b h e", b=2, h=HEADS)

            def split_first(r):
                dve.wait_ge(v32_ready, r.after(1, 1))
                reach(dve, av_made, (r - 1).after(4, 0))
                dve.tensor_copy(part(r, 0), as_heads(v32)).then_inc(v_split, 1)
                dve.wait_ge(v_split, r.after(4, 1))
                dve.tensor_tensor(as_heads(vr[0]), as_heads(v32), part(r, 0), ALU.subtract).then_inc(v_split, 1)

            def split_rest(r):
                dve.wait_ge(v_split, r.after(4, 2))
                dve.tensor_copy(part(r, 1), as_heads(vr[0])).then_inc(v_split, 1)
                dve.wait_ge(v_split, r.after(4, 3))
                reach(dve, vs_ready, r.after(1, 0))
                dve.tensor_tensor(as_heads(vr[1]), as_heads(vr[0]), part(r, 1), ALU.subtract).then_inc(v_split, 1)
                dve.wait_ge(v_split, r.after(4, 4))
                dve.tensor_copy(part(r, 2), as_heads(vr[1])).then_inc(vs_ready, 1)

            def combine(r, b):
                dve.wait_ge(av_made, r.after(4, 2 * b + 2))
                reach(dve, on_ready, r.after(2, b))
                dve.tensor_reduce(o9[:], psA[:, 0:432].rearrange("p (h c e) -> p h e c", h=HEADS, c=3), X, ALU.add)\
                    .then_inc(o_sum, 1)
                dve.wait_ge(o_sum, r.after(2, b + 1))
                dve.reciprocal(orec[:], o9[:, :, 8]).then_inc(o_rec, 1)
                dve.wait_ge(o_rec, r.after(2, b + 1))
                reach(dve, oT_made, r.after(2, b))
                dve.tensor_tensor(on[:].rearrange("p (h e) -> p h e", h=HEADS), o9[:, :, 0:8],
                                  orec[:].unsqueeze(2).to_broadcast([128, HEADS, 8]), ALU.mult).then_inc(on_ready, 1)

            def statistics(r, b):
                dve.wait_ge(pj_made, r.after(2, b + 1))
                dve.tensor_tensor(y[b][:], psM[:, 0:128], w.xres[:, bass.ds(r.n * 256 + b * 128, 128)], ALU.add)\
                    .then_inc(y_done, 1)
                dve.wait_ge(y_done, r.after(2, b + 1))
                dve.bn_stats(stats[:], y[b][:]).then_inc(st_done, 1)
                dve.wait_ge(st_done, r.after(2, b + 1))
                dve.memset(w.scratch[:], 0.0)
                dve.bn_aggr(mv[b][:], stats[:]).then_inc(mv_ready, 1)

            def normalise(r, b):
                dve.wait_ge(rstd_ready, r.after(2, b + 1))
                reach(dve, xT_made, (r - 1).after(2, b + 1))
                dve.tensor_scalar(w.xres[:, bass.ds(r.n * 256 + b * 128, 128)], y[b][:], mv[b][:, 0:1], rstd[b][:],
                                  ALU.subtract, ALU.mult)
                dve.tensor_scalar(xp[b][:, 0:127], y[b][:, 0:127], mv[b][:, 0:1], rstd[b][:],
                                  ALU.subtract, ALU.mult).then_inc(x2_ready, 1)

            def low_part(r, b):
                at = bass.ds(r.n * 256 + b * 128, 128)
                dve.wait_ge(xh_ready, r.after(2, b + 1))
                dve.tensor_tensor(w.xl[:, at], psM[:, 0:128], w.xh[:, at], ALU.subtract).then_inc(xl_ready, 1)

            def step(k):
                r = k - 1
                for j in range(4):
                    if r.within(PAIRS):
                        dve.wait_ge(s_made, r.after(4, j + 1))
                        reach(dve, shifted, r.after(4, j - 1))
                        dve.tensor_reduce(mx[j % 2][:], psL[j % 2][:, :, 0:HW].rearrange("p i (h t) -> p i h t", h=4),
                                          X, ALU.max).then_inc(mx_ready, 1)
                    if j == 0 and k.within(PAIRS):
                        dve.wait_ge(qh_ready, k.after(1, 1))
                        dve.tensor_tensor(ql[k.par][:], psM[:, QUERY], qh[k.par][:], ALU.subtract).then_inc(ql_ready, 1)
                    if j == 1 and k.within(PAIRS):
                        dve.wait_ge(kb_done, k.after(1, 1))
                        dve.tensor_copy(kbh[k.par][:], kb[:]).then_inc(kbh_ready, 1)
                    if j == 2 and (k - 2).within(PAIRS):
                        statistics(k - 2, 0)
                    if j == 3 and (k - 2).within(PAIRS):
                        normalise(k - 2, 0)
                    if j % 2 == 0 and (k - 2).within(PAIRS):
                        combine(k - 2, j // 2)
                    r2, j2 = earlier(r, j, 2)
                    if r2.within(PAIRS):
                        dve.wait_ge(t_made, r2.after(4, j2 + 1))
                        reach(dve, av_made, r2.after(4, j2 - 1))
                        dve.tensor_copy(pTh[j % 2][:], psTh[:]).then_inc(pTh_ready, 1)
                    if j == 0 and (k - 3).within(PAIRS):
                        statistics(k - 3, 1)
                    if j == 1 and (k - 3).within(PAIRS):
                        normalise(k - 3, 1)
                    if j == 2 and (k - 3).within(PAIRS):
                        low_part(k - 3, 1)
                    if j == 3 and (k - 2).within(PAIRS):
                        low_part(k - 2, 0)
                    if j == 3 and k.within(PAIRS):
                        split_first(k)
                    if j == 1 and r.within(PAIRS):
                        split_rest(r)
            steps(dve, PAIRS, 3, step)

        @block.gpsimd
        def _(pool):
            def step(k):
                r = k - 1
                for j in range(4):
                    if j == 0 and k.within(PAIRS):
                        pool.wait_ge(kc_ready, k.after(1, 1))
                        reach(pool, kbl_ready, k.after(1, 0))
                        pool.tensor_tensor(
                            kb[:], kc[:].rearrange("p (b t) -> p b t", b=2).unsqueeze(2).to_broadcast([128, 2, 4, JP]),
                            w.head.unsqueeze(1).unsqueeze(3).to_broadcast([128, 2, 4, JP]), ALU.mult).then_inc(kb_done, 1)
                    if j == 1 and k.within(PAIRS):
                        pool.wait_ge(kbh_ready, k.after(1, 1))
                        pool.tensor_tensor(kbl[k.par][:], kb[:], kbh[k.par][:], ALU.subtract).then_inc(kbl_ready, 1)
                    if j % 2 == 0:
                        rp, bp = (k - 2, 0) if j else (k - 3, 1)
                        if rp.within(PAIRS):
                            pool.wait_ge(mv_ready, rp.after(2, bp + 1))
                            pool.tensor_tensor(veps[:], mv[bp][:, 1:2], w.eps[:, 0:1], ALU.add).then_inc(ve_done, 1)
                            pool.wait_ge(ve_done, rp.after(2, bp + 1))
                            pool.tensor_tensor(rstd[bp][:], veps[:], w.neg_half[:, 0:1], ALU.pow).then_inc(rstd_ready, 1)
                    if r.within(PAIRS):
                        pool.wait_ge(p32_ready, r.after(4, j + 1))
                        reach(pool, t_made, r.after(4, j - 1))
                        pool.tensor_tensor(pl[j % 2][:], p32[j % 2][:], ph[j % 2][:], ALU.subtract).then_inc(pl_ready, 1)
            steps(pool, PAIRS, 3, step)


def prepare_slots(nc, io, w):
    with ExitStack() as ctx:
        st = Store(nc, ctx, "prep")
        phi = st.sb("phi", [128, 16, 128])
        bias = st.sb("bias", [128, 16])
        diff = st.sb("diff", [128, 16, 128])
        psW = st.ps("W", [128, NP])
        loaded, diff_done, w_made, wh_done = (
            st.sem(n) for n in ("loaded", "diff_done", "w_made", "wh_done"))
        block = ctx.enter_context(nc.Block())

        def by_quarter(t, c):
            return t[:].rearrange("d (q c g p) -> d c g q p", q=4, c=4, g=16)[:, c]

        def by_expert(t, c):
            return t[:, c * 512:(c + 1) * 512].rearrange("d (g q p) -> d g q p", g=16, q=4)

        @block.sync
        def _(sync):
            sync.dma_start(phi[:], io["phi"].rearrange("(c r) d -> r c d", r=128)).then_inc(loaded, 16)
            sync.dma_start(bias[:], io["phi_b"]).then_inc(loaded, 16)

        @block.vector
        def _(dve):
            dve.wait_ge(loaded, 32)
            dve.tensor_tensor(diff[:, :, 0:127], phi[:, :, 0:127], phi[:, :, 127:128].to_broadcast([128, 16, 127]),
                              ALU.subtract)
            dve.tensor_copy(diff[:, :, 127], bias[:]).then_inc(diff_done, 1)
            for c in range(4):
                b = slice(c * 512, (c + 1) * 512)
                dve.wait_ge(wh_done, c + 1)
                dve.tensor_tensor(w.w1l[:, b], psW[:, b], w.w1h[:, b], ALU.subtract)
                dve.tensor_tensor(by_quarter(w.w2l, c), by_expert(psW, c), by_quarter(w.w2h, c), ALU.subtract)

        @block.tensor
        def _(pe):
            pe.wait_ge(diff_done, 1)
            for c in range(16):
                ins = pe.transpose(psW[:, c * 128:(c + 1) * 128], diff[:, c, :], w.ident)
                if c % 4 == 3:
                    ins.then_inc(w_made, 1)

        @block.scalar
        def _(act):
            for c in range(4):
                b = slice(c * 512, (c + 1) * 512)
                act.wait_ge(w_made, c + 1)
                act.copy(w.w1h[:, b], psW[:, b])
                act.copy(by_quarter(w.w2h, c), by_expert(psW, c)).then_inc(wh_done, 1)


def gather_slots(nc, w, psX):
    TILES = TOKENS // 128
    with ExitStack() as ctx:
        st = Store(nc, ctx, "gather")
        xh = [st.sb(f"xh{i}", [128, 128], F32R) for i in range(2)]
        xl = [st.sb(f"xl{i}", [128, 128], F32R) for i in range(2)]
        x2 = [st.sb(f"x2{i}", [128, 128]) for i in range(2)]
        mx = [st.sb(f"mx{i}", [128, 2, 16], F32R) for i in range(2)]
        e = [st.sb(f"e{i}", [128, 2, 16, 32]) for i in range(2)]
        rsum = [st.sb(f"rsum{i}", [128, 32]) for i in range(2)]
        rinv = [st.sb(f"rinv{i}", [128, 32]) for i in range(2)]
        dd = [st.sb(f"d{i}", [128, 2, 512]) for i in range(2)]
        psL = [st.ps(f"L{i}", [128, 2, 512]) for i in range(2)]
        x_ready, x2_ready = st.sem("x_ready"), st.sem("x2_ready")
        l_made, mx_ready, shifted, e_ready, sum_done, rinv_ready, d_ready, x_made = (
            st.sem(n) for n in ("l_made", "mx_ready", "shifted", "e_ready", "sum_done", "rinv_ready", "d_ready",
                                "x_made"))
        block = ctx.enter_context(nc.Block())

        def earlier(t, j, s):
            return (t, j - s) if j >= s else (t - (s - j + 1) // 2, (j - s) % 2)

        @block.tensor
        def _(pe):
            def logits(t, j):
                pe.wait_ge(x_ready, t.after(1, 1))
                reach(pe, e_ready, t.after(2, j - 1))
                for n, (xs, ws) in enumerate(((xh, w.w1h), (xl, w.w1h), (xh, w.w1l))):
                    for i in range(2):
                        c = (2 * j + i) * 512
                        ins = pe.matmul(psL[j][:, i, :], xs[t.par][:], ws[:, c:c + 512], start=n == 0, stop=n == 2)
                ins.then_inc(l_made, 1)

            def gather(t, j):
                if j == 0:
                    pe.wait_ge(x2_ready, t.after(1, 1))
                pe.wait_ge(d_ready, t.after(2, j + 1))
                for i in range(2):
                    ins = pe.matmul(psX[:, 2 * j + i, :], x2[t.par][:], dd[j][:, i, :], start=t.known and t.n == 0,
                                    stop=t.known and t.n == TILES - 1)
                ins.then_inc(x_made, 1)

            def shift(t, j):
                pe.wait_ge(mx_ready, t.after(2, j + 1))
                for i in range(2):
                    ins = pe.matmul(psL[j][:, i, :], w.neg_ident[:],
                                    mx[j][:, i, :].unsqueeze(2).to_broadcast([128, 16, 32]), start=False, stop=True,
                                    skip_group_check=True)
                ins.then_inc(shifted, 1)

            def step(t):
                for j in range(2):
                    if t.within(TILES):
                        logits(t, j)
                    t3, j3 = earlier(t, j, 3)
                    if t3.within(TILES):
                        gather(t3, j3)
                    if t.within(TILES):
                        shift(t, j)
            steps(pe, TILES, 2, step)

        @block.scalar
        def _(act):
            def copies(t):
                at = bass.ds(t.n * 128, 128)
                reach(act, l_made, t.after(2, -2))
                act.copy(xh[t.par][:], w.xh[:, at].bitcast(F32))
                act.copy(xl[t.par][:], w.xl[:, at].bitcast(F32)).then_inc(x_ready, 1)

            def step(t):
                for j in range(2):
                    if j == 0 and t.within(TILES):
                        copies(t)
                    if j == 1 and t.within(TILES):
                        reach(act, x_made, t.after(2, -2))
                        act.copy(x2[t.par][:], w.xres[:, bass.ds(t.n * 128, 128)]).then_inc(x2_ready, 1)
                    tu, ju = earlier(t, j, 1)
                    if tu.within(TILES):
                        act.wait_ge(shifted, tu.after(2, ju + 1))
                        reach(act, d_ready, tu.after(2, ju - 1))
                        act.activation(e[ju][:], psL[ju][:].rearrange("p i (n s) -> p i n s", n=16), ACT.Exp)\
                            .then_inc(e_ready, 1)
            steps(act, TILES, 2, step)

        @block.vector
        def _(dve):
            def step(t):
                for j in range(2):
                    if t.within(TILES):
                        dve.wait_ge(l_made, t.after(2, j + 1))
                        reach(dve, shifted, t.after(2, j - 1))
                        dve.tensor_reduce(mx[j][:], psL[j][:].rearrange("p i (n s) -> p i n s", n=16), X, ALU.max)\
                            .then_inc(mx_ready, 1)
                    tu, ju = earlier(t, j, 1)
                    if tu.within(TILES):
                        dve.wait_ge(e_ready, tu.after(2, ju + 1))
                        reach(dve, rinv_ready, tu.after(2, ju - 1))
                        dve.tensor_reduce(rsum[ju][:].rearrange("p (i n) -> p i n", i=2), e[ju][:], X, ALU.add)\
                            .then_inc(sum_done, 1)
                        dve.wait_ge(sum_done, tu.after(2, ju + 1))
                        reach(dve, d_ready, tu.after(2, ju - 1))
                        dve.reciprocal(rinv[ju][:], rsum[ju][:]).then_inc(rinv_ready, 1)
            steps(dve, TILES, 2, step)

        @block.gpsimd
        def _(pool):
            def step(t):
                for j in range(2):
                    tu, ju = earlier(t, j, 1)
                    if tu.within(TILES):
                        pool.wait_ge(rinv_ready, tu.after(2, ju + 1))
                        reach(pool, x_made, tu.after(2, ju - 1))
                        pool.tensor_tensor(
                            dd[ju][:].rearrange("p i (n s) -> p i n s", n=16), e[ju][:],
                            rinv[ju][:].rearrange("p (i n) -> p i n", i=2).unsqueeze(3).to_broadcast([128, 2, 16, 32]),
                            ALU.mult).then_inc(d_ready, 1)
            steps(pool, TILES, 2, step)


def run_experts(nc, io, w, psX, y_dram):
    with ExitStack() as ctx:
        st = Store(nc, ctx, "expert")
        we = st.sb("we", [128, EXPERTS, 128])
        be = st.sb("be", [1, EXPERTS * 128])
        ones = st.sb("ones", [1, 32])
        xt = st.sb("xt", [128, NP])
        stats = st.sb("stats", [128, 16, 6])
        mv = st.sb("mv", [128, 16, 2])
        veps = st.sb("veps", [128, 16])
        rstd = st.sb("rstd", [128, 16])
        z = st.sb("z", [128, 16, 128])
        zT = xt
        y = z
        psT = st.ps("T", [128, 16, 128])
        psY = psX
        (we_loaded, be_loaded, ones_set, xt_ready, t_made, st_done, mv_ready, ve_done, rstd_ready, n_ready, z_ready,
         zT_made, zT_ready, y_made, y_ready, y_stored, y_loaded) = (
            st.sem(n) for n in ("we_loaded", "be_loaded", "ones_set", "xt_ready", "t_made", "st_done", "mv_ready",
                                "ve_done", "rstd_ready", "n_ready", "z_ready", "zT_made", "zT_ready", "y_made",
                                "y_ready", "y_stored", "y_loaded"))
        block = ctx.enter_context(nc.Block())

        @block.sync
        def _(sync):
            sync.dma_start(we[:], io["expert_w"].rearrange("n d h -> d n h")).then_inc(we_loaded, 16)
            sync.dma_start(be[:], io["expert_b"]).then_inc(be_loaded, 16)
            sync.wait_ge(y_ready, 4)
            sync.dma_start(y_dram.rearrange("(c r) h -> r c h", r=128), y[:]).then_inc(y_stored, 16)
            sync.wait_ge(y_stored, 16)
            order = y_dram.rearrange("(c g q p) h -> q c g p h", c=4, g=16, q=4)
            for q in range(4):
                for c in range(4):
                    sync.dma_start(w.yk[:, q * 4 + c, :], order[q, c]).then_inc(y_loaded, 16)
            sync.wait_ge(y_loaded, 256)

        @block.vector
        def _(dve):
            dve.memset(ones[:], 1.0).then_inc(ones_set, 1)
            for c in range(4):
                dve.tensor_scalar(xt[:, c * 512:(c + 1) * 512], psX[:, c, :], 65000.0, -33000.0, ALU.min, ALU.max)\
                    .then_inc(xt_ready, 1)
            for c in range(16):
                dve.wait_ge(t_made, c // 4 + 1)
                ins = dve.bn_stats(stats[:, c, :], psT[:, c, :])
            ins.then_inc(st_done, 1)
            dve.wait_ge(st_done, 1)
            dve.memset(w.scratch[:], 0.0)
            for c in range(16):
                ins = dve.bn_aggr(mv[:, c, :], stats[:, c, :])
            ins.then_inc(mv_ready, 1)
            dve.wait_ge(rstd_ready, 1)
            for c in range(16):
                ins = dve.tensor_scalar(z[:, c, :], psT[:, c, :], mv[:, c, 0:1], rstd[:, c:c + 1], ALU.subtract, ALU.mult)
                if c % 4 == 3:
                    ins.then_inc(n_ready, 1)
            for c in range(4):
                dve.wait_ge(zT_made, c + 1)
                dve.tensor_copy(zT[:, c * 512:(c + 1) * 512], psT[:, 4 * c:4 * c + 4, :]).then_inc(zT_ready, 1)

        @block.gpsimd
        def _(pool):
            pool.wait_ge(mv_ready, 1)
            pool.tensor_tensor(veps[:], mv[:, :, 1], w.eps[:, 0:16], ALU.add).then_inc(ve_done, 1)
            pool.wait_ge(ve_done, 1)
            pool.tensor_tensor(rstd[:], veps[:], w.neg_half[:, 0:16], ALU.pow).then_inc(rstd_ready, 1)

        @block.tensor
        def _(pe):
            for c in range(16):
                pe.wait_ge(xt_ready, c // 4 + 1)
                ins = pe.transpose(psT[:, c, :], xt[:, c * 128:(c + 1) * 128], w.ident)
                if c % 4 == 3:
                    ins.then_inc(t_made, 1)
            for c in range(16):
                pe.wait_ge(z_ready, c // 4 + 1)
                ins = pe.transpose(psT[:, c, :], z[:, c, :], w.ident)
                if c % 4 == 3:
                    ins.then_inc(zT_made, 1)
            pe.wait_ge(we_loaded, 16)
            pe.wait_ge(be_loaded, 16)
            pe.wait_ge(ones_set, 1)
            for n in range(EXPERTS):
                pe.wait_ge(zT_ready, n // 16 + 1)
                r = n % 4 * 32
                out = psY[r:r + 32, n // 16, n // 4 % 4 * 128:(n // 4 % 4 + 1) * 128]
                pe.matmul(out, zT[:, n * 32:(n + 1) * 32], we[:, n, :], start=True, stop=False)
                ins = pe.matmul(out, ones[:], be[:, n * 128:(n + 1) * 128], start=False, stop=True)
                if n % 16 == 15:
                    ins.then_inc(y_made, 1)

        @block.scalar
        def _(act):
            for c in range(4):
                act.wait_ge(n_ready, c + 1)
                act.activation(z[:, 4 * c:4 * c + 4, :], z[:, 4 * c:4 * c + 4, :], ACT.Tanh).then_inc(z_ready, 1)
            for c in range(4):
                act.wait_ge(y_made, c + 1)
                act.copy(y[:, 4 * c:4 * c + 4, :], psY[:, c, :]).then_inc(y_ready, 1)


def mix_slots(nc, w, out):
    TILES = TOKENS // 256
    with ExitStack() as ctx:
        st = Store(nc, ctx, "mix")
        mg = [st.sb(f"mg{i}", [128, 256]) for i in range(2)]
        m8 = st.sb("m8", [128, 2, 8])
        me = [st.sb(f"me{i}", [128, 2, 16, 8], F32R) for i in range(2)]
        e = [st.sb(f"e{i}", [128, 4, 256]) for i in range(2)]
        sg = [st.sb(f"sg{i}", [128, 256]) for i in range(2)]
        rinv = [st.sb(f"rinv{i}", [128, 256]) for i in range(2)]
        cc = [st.sb(f"c{i}", [128, 4, 256]) for i in range(2)]
        yT = st.sb("yT", [128, 256])
        y = [st.sb(f"y{i}", [128, 2, 128]) for i in range(2)]
        stats = st.sb("stats", [128, 2, 6])
        mv = [st.sb(f"mv{i}", [128, 2, 2]) for i in range(2)]
        veps = st.sb("veps", [128, 2])
        rstd = [st.sb(f"rstd{i}", [128, 2]) for i in range(2)]
        res = [st.sb(f"res{i}", [128, 2, 128]) for i in range(2)]
        psL = [st.ps(f"L{i}", [128, 2, 512]) for i in range(2)]
        psG = st.ps("G", [128, 2, 128])
        psS = st.ps("S", [128, 512])
        psY = st.ps("Y", [128, 256])
        psF = st.ps("F", [128, 2, 128])
        (l_made, mg_ready, g_made, m8_done, me_ready, shifted, e_ready, sg_ready, s_made, rinv_ready, c_ready,
         y_made) = (
            st.sem(n) for n in ("l_made", "mg_ready", "g_made", "m8_done", "me_ready", "shifted", "e_ready",
                                "sg_ready", "s_made", "rinv_ready", "c_ready", "y_made"))
        yT_ready, f_made, y_done, st_done, mv_ready, ve_done, rstd_ready, res_ready = (
            st.sem(n) for n in ("yT_ready", "f_made", "y_done", "st_done", "mv_ready", "ve_done", "rstd_ready",
                                "res_ready"))
        stored = [st.sem("stored0"), st.sem("stored1")]
        block = ctx.enter_context(nc.Block())

        def earlier(t, j, s):
            return (t, j - s) if j >= s else (t - 1, j - s + 4)

        @block.sync
        def _(sync):
            def step(k):
                t = k - 2
                if t.within(TILES):
                    sync.wait_ge(res_ready, t.after(1, 1))
                    sync.dma_start(out[bass.ds(t.n * 256, 256), :].rearrange("(b s) d -> s b d", b=2), res[t.par][:])\
                        .then_inc(stored[t.par], 16)
            steps(sync, TILES, 2, step)
            for i in range(2):
                sync.wait_ge(stored[i], 16 * (TILES // 2))

        @block.tensor
        def _(pe):
            def logits(t, j):
                reach(pe, e_ready, t.after(4, j - 1))
                at = bass.ds(t.n * 256, 256)
                for c in range(4):
                    o = psL[j % 2][:, c // 2, c % 2 * 256:(c % 2 + 1) * 256]
                    k = slice((4 * j + c) * 128, (4 * j + c + 1) * 128)
                    pe.matmul(o, w.w2h[:, k], w.xh[:, at], start=(c % 2 == 0), stop=False, skip_group_check=True)
                    pe.matmul(o, w.w2h[:, k], w.xl[:, at], start=False, stop=False, skip_group_check=True)
                    ins = pe.matmul(o, w.w2l[:, k], w.xh[:, at], start=False, stop=True, skip_group_check=True)
                ins.then_inc(l_made, 1)

            def spread(t, j):
                pe.wait_ge(c_ready, t.after(4, j + 1))
                if j == 0:
                    reach(pe, yT_ready, t.after(1, 0))
                for c in range(4):
                    ins = pe.matmul(psY[:], w.yk[:, 4 * j + c, :], cc[j % 2][:, c, :],
                                    start=(j == 0 and c == 0), stop=(j == 3 and c == 3))
                ins.then_inc(y_made, 1)

            def turn_max(t, j):
                pe.wait_ge(mg_ready, t.after(4, j + 1))
                reach(pe, m8_done, t.after(4, j))
                for b in range(2):
                    ins = pe.transpose(psG[:, b, :], mg[j % 2][:, b * 128:(b + 1) * 128], w.ident)
                ins.then_inc(g_made, 1)

            def sum_experts(t, j):
                pe.wait_ge(sg_ready, t.after(4, j + 1))
                reach(pe, rinv_ready, t.after(4, j))
                pe.matmul(psS[:, 0:256], w.gsum, sg[j % 2][:], start=True, stop=True).then_inc(s_made, 1)

            def shift(t, j):
                pe.wait_ge(me_ready, t.after(4, j + 1))
                for b in range(2):
                    for i in range(2):
                        o = psL[j % 2][:, i, :].rearrange("p (c t) -> p c t", c=2)[:, :, b * 128:(b + 1) * 128]
                        ins = pe.matmul(o, me[j % 2][:, b, :, :], w.neg_ident[:].unsqueeze(1).to_broadcast([128, 2, 128]),
                                        start=False, stop=True, skip_group_check=True)
                ins.then_inc(shifted, 1)

            def step(k):
                for j in range(4):
                    if k.within(TILES):
                        logits(k, j)
                    t3, j3 = earlier(k, j, 3)
                    if t3.within(TILES):
                        spread(t3, j3)
                    if k.within(TILES):
                        turn_max(k, j)
                    t1, j1 = earlier(k, j, 1)
                    if t1.within(TILES):
                        sum_experts(t1, j1)
                    if k.within(TILES):
                        shift(k, j)
                    if j == 3 and (k - 1).within(TILES):
                        t = k - 1
                        pe.wait_ge(yT_ready, t.after(1, 1))
                        reach(pe, y_done, t.after(1, 0))
                        for b in range(2):
                            ins = pe.transpose(psF[:, b, :], yT[:, b * 128:(b + 1) * 128], w.ident)
                        ins.then_inc(f_made, 1)
            steps(pe, TILES, 2, step)

        @block.scalar
        def _(act):
            def step(k):
                for j in range(4):
                    if k.within(TILES):
                        act.wait_ge(shifted, k.after(4, j + 1))
                        reach(act, c_ready, k.after(4, j - 1))
                        reach(act, sg_ready, k.after(4, j - 1))
                        act.activation(e[j % 2][:], psL[j % 2][:].rearrange("p i (c t) -> p (i c) t", c=2), ACT.Exp)\
                            .then_inc(e_ready, 1)
                    if j == 2 and (k - 1).within(TILES):
                        t = k - 1
                        act.wait_ge(y_made, t.after(4, 4))
                        reach(act, f_made, t.after(1, 0))
                        act.copy(yT[:], psY[:]).then_inc(yT_ready, 1)
            steps(act, TILES, 2, step)

        @block.vector
        def _(dve):
            def step(k):
                for j in range(4):
                    if k.within(TILES):
                        dve.wait_ge(l_made, k.after(4, j + 1))
                        reach(dve, g_made, k.after(4, j - 1))
                        dve.tensor_reduce(mg[j % 2][:], psL[j % 2][:].rearrange("p i (c t) -> p t (i c)", c=2), X,
                                          ALU.max).then_inc(mg_ready, 1)
                    t1, j1 = earlier(k, j, 1)
                    if t1.within(TILES):
                        dve.wait_ge(e_ready, t1.after(4, j1 + 1))
                        reach(dve, s_made, t1.after(4, j1 - 1))
                        dve.tensor_reduce(sg[j1 % 2][:], e[j1 % 2][:].rearrange("p c t -> p t c"), X, ALU.add)\
                            .then_inc(sg_ready, 1)
                    if k.within(TILES):
                        dve.wait_ge(g_made, k.after(4, j + 1))
                        reach(dve, me_ready, k.after(4, j))
                        dve.tensor_reduce(m8[:], psG[:].rearrange("t b (g p) -> t b p g", g=16), X, ALU.max)\
                            .then_inc(m8_done, 1)
                        dve.wait_ge(m8_done, k.after(4, j + 1))
                        reach(dve, shifted, k.after(4, j - 1))
                        dve.tensor_copy(me[j % 2][:], m8[:].unsqueeze(2).to_broadcast([128, 2, 16, 8])).then_inc(me_ready, 1)
                    if t1.within(TILES):
                        dve.wait_ge(s_made, t1.after(4, j1 + 1))
                        reach(dve, c_ready, t1.after(4, j1 - 1))
                        dve.reciprocal(rinv[j1 % 2][:], psS[:, 0:256]).then_inc(rinv_ready, 1)
                    t = k - 2
                    if j == 0 and t.within(TILES):
                        dve.wait_ge(f_made, t.after(1, 1))
                        reach(dve, res_ready, t.after(1, -1))
                        dve.tensor_tensor(y[t.par][:], psF[:], w.xres[:, bass.ds(t.n * 256, 256)]
                                          .rearrange("s (b d) -> s b d", b=2), ALU.add).then_inc(y_done, 1)
                        dve.wait_ge(y_done, t.after(1, 1))
                        for b in range(2):
                            ins = dve.bn_stats(stats[:, b, :], y[t.par][:, b, :])
                        ins.then_inc(st_done, 1)
                        dve.wait_ge(st_done, t.after(1, 1))
                        dve.memset(w.scratch[:], 0.0)
                        for b in range(2):
                            ins = dve.bn_aggr(mv[t.par][:, b, :], stats[:, b, :])
                        ins.then_inc(mv_ready, 1)
                    if j == 1 and t.within(TILES):
                        dve.wait_ge(rstd_ready, t.after(1, 1))
                        if not (t.known and t.n < 2):
                            dve.wait_ge(stored[t.par], t.turn(16, 0))
                        for b in range(2):
                            ins = dve.tensor_scalar(res[t.par][:, b, :], y[t.par][:, b, :], mv[t.par][:, b, 0:1],
                                                    rstd[t.par][:, b:b + 1], ALU.subtract, ALU.mult)
                        ins.then_inc(res_ready, 1)
            steps(dve, TILES, 2, step)

        @block.gpsimd
        def _(pool):
            def step(k):
                for j in range(4):
                    t1, j1 = earlier(k, j, 1)
                    if t1.within(TILES):
                        pool.wait_ge(rinv_ready, t1.after(4, j1 + 1))
                        reach(pool, y_made, t1.after(4, j1 - 1))
                        pool.tensor_tensor(cc[j1 % 2][:], e[j1 % 2][:],
                                           rinv[j1 % 2][:].unsqueeze(1).to_broadcast([128, 4, 256]), ALU.mult)\
                            .then_inc(c_ready, 1)
                    t = k - 2
                    if j == 0 and t.within(TILES):
                        pool.wait_ge(mv_ready, t.after(1, 1))
                        pool.tensor_tensor(veps[:], mv[t.par][:, :, 1], w.eps[:, 0:2], ALU.add).then_inc(ve_done, 1)
                        pool.wait_ge(ve_done, t.after(1, 1))
                        pool.tensor_tensor(rstd[t.par][:], veps[:], w.neg_half[:, 0:2], ALU.pow).then_inc(rstd_ready, 1)
            steps(pool, TILES, 2, step)


class Weights:
    pass


def decoder_block(nc, io, out, y_dram):
    with ExitStack() as ctx:
        st = Store(nc, ctx, "kept")
        w = Weights()
        w.xres = st.sb("xres", [128, TOKENS])
        w.xh = st.sb("xh", [128, TOKENS], F32R)
        w.xl = st.sb("xl", [128, TOKENS], F32R)
        w.consts = st.sb("consts", [128, C_END])
        w.ident = w.consts[:, C_IDENT:C_GSUM]
        w.gsum = w.consts[:, C_GSUM:C_HEAD]
        w.head = w.consts[:, C_HEAD:C_END]
        w.ident16 = st.sb("ident16", [128, 128], F16)
        w.neg_ident = st.sb("neg_ident", [128, 128], F32R)
        w.neg_half = st.sb("neg_half", [128, 16])
        w.eps = st.sb("eps", [128, 16])
        w.scratch = st.sb("scratch", [128, 1])
        with ExitStack() as first:
            sf = Store(nc, first, "first")
            w.x1T = sf.sb("x1T", [128, TOKENS])
            w.m, w.w2, w.b2 = sf.sb("m", [128, 128]), sf.sb("w2", [128, 128]), sf.sb("b2", [128, 128])
            w.cvec, w.avec, w.beta = sf.sb("cvec", [128, 1]), sf.sb("avec", [128, 1]), sf.sb("beta", [128, 1])
            w.xq, w.xqs, w.xo = sf.sb("xq", [128, 128]), sf.sb("xqs", [128, 128]), sf.sb("xo", [128, 128])
            w.xk, w.xv = sf.sb("xk", [CD, 128]), sf.sb("xv", [CD, 128])
            w.fill = sf.sb("fill", [128, B * JP], BF16)
            w.ones16 = sf.sb("ones16", [128, 128], BF16)
            setup(nc, io, w)
            attention(nc, io, w)
            attend_context(nc, io, w)
        w.yk = st.sb("yk", [128, 16, 128])
        w.w2h, w.w2l = st.sb("w2h", [128, NP], F32R), st.sb("w2l", [128, NP], F32R)
        with ExitStack() as banks:
            psX = Store(nc, banks, "slots").ps("X", [128, 4, 512])
            with ExitStack() as second:
                ss = Store(nc, second, "second")
                w.w1h, w.w1l = ss.sb("w1h", [128, NP], F32R), ss.sb("w1l", [128, NP], F32R)
                prepare_slots(nc, io, w)
                gather_slots(nc, w, psX)
            run_experts(nc, io, w, psX, y_dram)
        mix_slots(nc, w, out)


def kernel(**inputs):
    import concourse.bacc as bacc
    from concourse.bass_utils import run_bass_kernel_spmd

    get = lambda name: np.asarray(inputs[name])
    x = get("x").reshape(TOKENS, D)
    context = np.zeros((B, JP, CD), np.float32)
    context[:, :J] = get("ctx_768")
    host = {
        "x": x, "xT": x.T, "ctxT": context.reshape(B * JP, CD).T, "mask": get("mask_BxS2_bf1").reshape(1, B * J),
        "w_qkvT": get("L0_attn_W_qkv").T, "b_qkv": get("L0_attn_b_qkv").reshape(3, D).T,
        "w_proj": get("L0_attn_W_proj"), "b_proj": get("L0_attn_b_proj").reshape(1, D),
        "xq": get("L0_xattn_Wq"), "xk": get("L0_xattn_Wk"), "xv": get("L0_xattn_Wv"), "xo": get("L0_xattn_Wo"),
        "phi": get("L0_ffn_phi_w"), "phi_b": get("L0_ffn_phi_b").reshape(16, 128).T,
        "expert_w": get("L0_ffn_expert_w"), "expert_b": get("L0_ffn_expert_b").reshape(1, EXPERTS * D),
        "consts": constants(),
    }
    nc = bacc.Bacc("TRN2", target_bir_lowering=False, num_devices=1)
    arrays, io = {}, {}
    for name, a in host.items():
        a = np.ascontiguousarray(a)
        arrays[f"in_{name}"] = a
        io[name] = nc.dram_tensor(f"in_{name}", a.shape, mybir.dt.from_np(a.dtype), kind="ExternalInput").ap()
    out = nc.dram_tensor("out_0", (TOKENS, D), F32, kind="ExternalOutput").ap()
    y_dram = nc.dram_tensor("y_slots", (NP, D), F32, kind="Internal").ap()
    decoder_block(nc, io, out, y_dram)
    result = run_bass_kernel_spmd(nc, [arrays], core_ids=[0])
    return result.results[0]["out_0"].reshape(B, S, D)
```

```python
from contextlib import ExitStack

import numpy as np

import concourse.bass as bass
from concourse import mybir

ALU = mybir.AluOpType
ACT = mybir.ActivationFunctionType
X = mybir.AxisListType.X
F32 = mybir.dt.float32
F32R = mybir.dt.float32r
F16 = mybir.dt.float16
BF16 = mybir.dt.bfloat16
U8 = mybir.dt.uint8

B, S, D = 64, 128, 128
TOKENS = B * S
J, JP, CD = 77, 78, 96
HEADS, HD = 16, 8
SCALE = float(HD) ** -0.5
EXPERTS, SLOTS = 64, 32
NP = EXPERTS * SLOTS
EPS = 1e-5
FILL = float(np.uint32(0x7F7F0000).view(np.float32))

T_01, T_025, T_085, T_095 = (float(np.float32(np.log(p / (1 - p)))) for p in (0.1, 0.25, 0.85, 0.95))

C_IDENT, C_HEAD, C_END = 0, 128, 132


def constants():
    k = np.arange(128)
    c = np.zeros((128, C_END), np.float32)
    c[:, C_IDENT:C_HEAD] = np.eye(128)
    c[:, C_HEAD:C_END] = (k[:, None] % 32) // HD == np.arange(4)[None, :]
    return c


class Item:

    def __init__(self, i, c):
        self.known = isinstance(i, int)
        self.par = c % 2
        self.half = i + c // 2
        self.n = i * 2 + c

    def __sub__(self, s):
        return Item(self.half, self.par - s)

    def __add__(self, s):
        return Item(self.half, self.par + s)

    def within(self, n):
        return not self.known or 0 <= self.n < n

    def after(self, per, c):
        return self.n * per + c

    def turn(self, per, c):
        return self.half * per + c


def steps(eng, n, lag, step):
    lo = (lag + 3) // 2
    hi = n // 2
    for k in range(2 * lo):
        step(Item(k // 2, k % 2))
    with eng.Fori(lo, hi) as i:
        step(Item(i, 0))
        step(Item(i, 1))
    for k in range(2 * hi, n + lag):
        step(Item(k // 2, k % 2))


def reach(eng, sem, value):
    if not isinstance(value, int) or value > 0:
        eng.wait_ge(sem, value)


class Store:

    def __init__(self, nc, ctx, stage):
        self.nc, self.ctx, self.stage = nc, ctx, stage

    def sb(self, name, shape, dt=F32):
        return self.ctx.enter_context(self.nc.sbuf_tensor(f"{self.stage}_{name}", shape, dt))

    def ps(self, name, shape, dt=F32):
        return self.ctx.enter_context(self.nc.psum_tensor(f"{self.stage}_{name}", shape, dt))

    def sem(self, name):
        return self.ctx.enter_context(self.nc.semaphore(f"{self.stage}_{name}"))


def setup(nc, io, w):
    with ExitStack() as ctx:
        st = Store(nc, ctx, "setup")
        wT = st.sb("wT", [128, 3, 128])
        wproj = st.sb("wproj", [128, 128])
        bqkv = st.sb("bqkv", [128, 3])
        bproj = st.sb("bproj", [1, 128])
        brep = st.sb("brep", [128, 2, 128])
        ones = st.sb("ones", [128, 128])
        mask = st.sb("mask", [128, B * J], U8)
        pa = st.ps("pa", [128, 512])
        pb = st.ps("pb", [128, 512])
        loaded, mask_clear, mask_loaded, rep, folded, evac = (
            st.sem(n) for n in ("loaded", "mask_clear", "mask_loaded", "rep", "folded", "evac"))
        block = ctx.enter_context(nc.Block())
        loads = [(w.consts, io["consts"]), (wT, io["w_qkvT"].rearrange("(c e) d -> e c d", c=3)),
                 (wproj, io["w_proj"]), (bqkv, io["b_qkv"]), (bproj, io["b_proj"]), (w.xq, io["xq"]),
                 (w.xk, io["xk"]), (w.xv, io["xv"]), (w.xo, io["xo"])]
        LOADED = 16 * len(loads)
        ROWS = range(0, 128, 32)

        @block.sync
        def _(sync):
            for dst, src in loads:
                sync.dma_start(dst[:], src).then_inc(loaded, 16)
            sync.wait_ge(mask_clear, 1)
            for p in ROWS:
                sync.dma_start(mask[p:p + 1, :], io["mask"]).then_inc(mask_loaded, 16)

        @block.vector
        def _(dve):
            dve.memset(mask[:].bitcast(mybir.dt.uint32), 0).then_inc(mask_clear, 1)
            dve.memset(ones[:], 1.0).then_inc(rep, 1)
            dve.wait_ge(loaded, LOADED)
            dve.wait_ge(rep, 1)
            for n, c in enumerate((0, 2)):
                dve.tensor_scalar(brep[:, n, :], ones[:], bqkv[:, c:c + 1], None, ALU.mult).then_inc(rep, 1)
            dve.tensor_copy(w.ident16[:], w.ident)
            dve.memset(w.neg_half[:], -0.5)
            dve.memset(w.eps[:], EPS)
            dve.tensor_scalar(w.neg_ident[:], w.ident, -1.0, None, ALU.mult)
            dve.tensor_scalar(w.xqs[:], w.xq[:], SCALE, None, ALU.mult)
            dve.memset(w.ones16[:], 1.0)
            dve.wait_ge(mask_loaded, 16 * len(ROWS))
            dve.memset(w.fill[:].rearrange("a (b t) -> a b t", t=JP)[:, :, J], -FILL)
            dve.tensor_scalar(w.fill[:].rearrange("a (b t) -> a b t", t=JP)[:, :, 0:J],
                              mask[:].rearrange("a (b t) -> a b t", t=J), 1.0, FILL, ALU.subtract, ALU.mult)
            dve.wait_ge(folded, 1)
            dve.tensor_copy(w.m[:], pa[:, 0:128])
            dve.tensor_copy(w.w2[:], pa[:, 128:256])
            dve.tensor_copy(w.cvec[:], pb[:, 0:1])
            dve.tensor_copy(w.avec[:], pb[:, 1:2])
            dve.tensor_copy(w.beta[:], pb[:, 2:3])
            dve.tensor_copy(w.b2[:], pb[:, 128:256]).then_inc(evac, 1)

        @block.tensor
        def _(pe):
            pe.wait_ge(loaded, LOADED)
            pe.wait_ge(rep, 3)
            pe.matmul(pa[:, 0:128], wT[:, 0, :], wT[:, 1, :], start=True, stop=True)
            pe.matmul(pa[:, 128:256], wT[:, 2, :], wproj[:], start=True, stop=True)
            pe.matmul(pb[:, 0:1], wT[:, 1, :], bqkv[:, 0:1], start=True, stop=True)
            pe.matmul(pb[:, 1:2], wT[:, 0, :], bqkv[:, 1:2], start=True, stop=True)
            pe.matmul(pb[:, 2:3], brep[:, 0, :], bqkv[:, 1:2], start=True, stop=True)
            pe.matmul(pb[:, 128:256], brep[:, 1, :], wproj[:], start=True, stop=False)
            pe.matmul(pb[:, 128:256], ones[0:1, :], bproj[:], start=False, stop=True).then_inc(folded, 1)


def attention(nc, io, w):
    GB = 4
    GROUPS = B // GB
    x_in = io["x"].rearrange("(q b s) d -> q s b d", q=4, s=S)
    with ExitStack() as ctx:
        st = Store(nc, ctx, "attn")
        xTg = [st.sb(f"xTg{i}", [128, GB * 128]) for i in range(2)]
        uT = st.sb("uT", [128, 512])
        vp = [st.sb(f"vp{i}", [128, 512]) for i in range(2)]
        rb = st.sb("rb", [128, GB])
        a = [st.sb(f"a{i}", [128, 512]) for i in range(2)]
        band = [st.sb(f"band{i}", [128, 512]) for i in range(6)]
        f2 = [st.sb(f"f2{i}", [128, 512]) for i in range(2)]
        mx = st.sb("mx", [128, GB])
        nb = [st.sb(f"nb{i}", [128, GB]) for i in range(2)]
        pr = [st.sb(f"pr{i}", [128, 512]) for i in range(2)]
        sums = [st.sb(f"sums{i}", [128, GB]) for i in range(2)]
        pT = [st.sb(f"pT{i}", [128, 512]) for i in range(2)]
        rinv = st.sb("rinv", [128, GB])
        y = [st.sb(f"y{i}", [128, GB, 128]) for i in range(2)]
        stats = st.sb("stats", [128, GB, 6])
        mv = [st.sb(f"mv{i}", [128, GB, 2]) for i in range(2)]
        veps = st.sb("veps", [128, GB])
        rstd = [st.sb(f"rstd{i}", [128, GB]) for i in range(2)]
        x1 = [st.sb(f"x1{i}", [128, GB * 128]) for i in range(2)]
        psU, psV, psR, psS, psT, psO, psX = (st.ps(n, [128, 512]) for n in ("U", "V", "R", "S", "T", "O", "X"))
        xT_loaded = [st.sem("xT_loaded0"), st.sem("xT_loaded1")]
        x_loaded = [st.sem(f"x_loaded{q}") for q in range(4)]
        (u_made, v_made, s_made, uT_ready, v_ready, rb_ready, a_ready, f_ready, p_ready, pT_made, pT_ready,
         o_made, mv_ready, rstd_ready, x1_ready, x1T_made, x1T_kept, x1_kept, low_ready, band_done, f2_done,
         mx_done, y_chain, pool_chain) = (
            st.sem(n) for n in ("u_made", "v_made", "s_made", "uT_ready", "v_ready", "rb_ready", "a_ready",
                                "f_ready", "p_ready", "pT_made", "pT_ready", "o_made", "mv_ready",
                                "rstd_ready", "x1_ready", "x1T_made", "x1T_kept", "x1_kept", "low_ready",
                                "band_done", "f2_done", "mx_done", "y_chain", "pool_chain"))
        block = ctx.enter_context(nc.Block())

        @block.gpsimd
        def _(pool):
            for q in range(4):
                pool.dma_start(w.xres[:, q * 2048:(q + 1) * 2048].rearrange("s (b d) -> s b d", d=D), x_in[q])\
                    .then_inc(x_loaded[q], 16)

            def step(k):
                g = k - 1
                if g.within(GROUPS):
                    pool.wait_ge(band_done, g.after(3, 1))
                    pool.tensor_tensor(band[4][:], band[1][:], band[2][:], ALU.add).then_inc(low_ready, 1)
                g = k - 3
                if g.within(GROUPS):
                    pool.wait_ge(x1_ready, g.after(1, 1))
                    pool.tensor_copy(w.xres[:, bass.ds(g.n * 512, 512)], x1[g.par][:]).then_inc(x1_kept, 1)
                g = k - 2
                if g.within(GROUPS):
                    pool.wait_ge(mv_ready, g.after(1, 1))
                    pool.tensor_tensor(veps[:], mv[g.par][:, :, 1], w.eps[:, 0:GB], ALU.add).then_inc(pool_chain, 1)
                    pool.wait_ge(pool_chain, g.after(1, 1))
                    pool.tensor_tensor(rstd[g.par][:], veps[:], w.neg_half[:, 0:GB], ALU.pow).then_inc(rstd_ready, 1)
            steps(pool, GROUPS, 3, step)

        @block.sync
        def _(sync):
            def step(g):
                if not g.within(GROUPS):
                    return
                reach(sync, s_made, g.after(1, -1))
                sync.dma_start(xTg[g.par][:], io["xT"][:, bass.ds(g.n * 512, 512)]).then_inc(xT_loaded[g.par], 16)
            steps(sync, GROUPS, 0, step)

        @block.tensor
        def _(pe):
            def step(k):
                g = k - 2
                if g.within(GROUPS):
                    pe.wait_ge(p_ready, g.after(1, 1))
                    reach(pe, pT_ready, g.after(1, 0))
                    for b in range(GB):
                        c = slice(b * 128, (b + 1) * 128)
                        ins = pe.transpose(psT[:, c], pr[g.par][:, c], w.ident)
                    ins.then_inc(pT_made, 1)
                g = k
                if g.within(GROUPS):
                    pe.wait_ge(xT_loaded[g.par], g.turn(16, 16))
                    reach(pe, uT_ready, g.after(1, 0))
                    pe.matmul(psU[:], w.m[:], xTg[g.par][:], start=True, stop=True).then_inc(u_made, 1)
                g = k - 2
                if g.within(GROUPS):
                    pe.wait_ge(pT_ready, g.after(1, 1))
                    reach(pe, mv_ready, g.after(1, 0))
                    for b in range(GB):
                        c = slice(b * 128, (b + 1) * 128)
                        ins = pe.matmul(psO[:, c], pT[g.par][:, c], vp[g.par][:, c], start=True, stop=True)
                    ins.then_inc(o_made, 1)
                g = k
                if g.within(GROUPS):
                    reach(pe, v_ready, g.after(1, 0))
                    reach(pe, rb_ready, g.after(1, 0))
                    for b in range(GB):
                        xb = xTg[g.par][:, b * 128:(b + 1) * 128]
                        pe.matmul(psV[:, b * 128:(b + 1) * 128], xb, w.w2[:], start=True, stop=True)
                        ins = pe.matmul(psR[:, b:b + 1], xb, w.avec[:], start=True, stop=True)
                    ins.then_inc(v_made, 1)
                    pe.wait_ge(uT_ready, g.after(1, 1))
                    reach(pe, a_ready, g.after(1, 0))
                    for b in range(GB):
                        c = slice(b * 128, (b + 1) * 128)
                        ins = pe.matmul(psS[:, c], uT[:, c], xTg[g.par][:, c], start=True, stop=True)
                    ins.then_inc(s_made, 1)
                g = k - 3
                if g.within(GROUPS):
                    pe.wait_ge(x1_ready, g.after(1, 1))
                    reach(pe, x1T_kept, g.after(1, 0))
                    for b in range(GB):
                        c = slice(b * 128, (b + 1) * 128)
                        ins = pe.transpose(psX[:, c], x1[g.par][:, c], w.ident)
                    ins.then_inc(x1T_made, 1)
            steps(pe, GROUPS, 3, step)

        @block.scalar
        def _(act):
            def step(k):
                g = k - 2
                if g.within(GROUPS):
                    act.wait_ge(pT_made, g.after(1, 1))
                    reach(act, o_made, g.after(1, -1))
                    act.copy(pT[g.par][:], psT[:]).then_inc(pT_ready, 1)
                g = k
                if g.within(GROUPS):
                    act.wait_ge(u_made, g.after(1, 1))
                    reach(act, s_made, g.after(1, 0))
                    act.activation(uT[:], psU[:], ACT.Identity, bias=w.cvec[:]).then_inc(uT_ready, 1)
                g = k - 1
                if g.within(GROUPS):
                    act.wait_ge(f_ready, g.after(1, 1))
                    reach(act, pT_made, g.after(1, -1))
                    reach(act, mv_ready, g.after(1, -1))
                    for b in range(GB):
                        c = slice(b * 128, (b + 1) * 128)
                        ins = act.activation(pr[g.par][:, c], f2[g.par][:, c], ACT.Exp, bias=nb[g.par][:, b:b + 1],
                                             scale=0.5, accum_out=sums[g.par][:, b:b + 1])
                    ins.then_inc(p_ready, 1)
                g = k
                if g.within(GROUPS):
                    act.wait_ge(rb_ready, g.after(1, 1))
                    act.wait_ge(s_made, g.after(1, 1))
                    reach(act, f_ready, g.after(1, -1))
                    for b in range(GB):
                        c = slice(b * 128, (b + 1) * 128)
                        ins = act.activation(a[g.par][:, c], psS[:, c], ACT.Identity, bias=rb[:, b:b + 1],
                                             scale=SCALE)
                    ins.then_inc(a_ready, 1)
                g = k - 3
                if g.within(GROUPS):
                    act.wait_ge(x1T_made, g.after(1, 1))
                    act.copy(w.x1T[:, bass.ds(g.n * 512, 512)], psX[:]).then_inc(x1T_kept, 1)
            steps(act, GROUPS, 3, step)

        @block.vector
        def _(dve):
            for q in range(4):
                dve.wait_ge(x_loaded[q], 16)

            def step(k):
                g = k - 1
                if g.within(GROUPS):
                    dve.wait_ge(a_ready, g.after(1, 1))
                    reach(dve, f_ready, g.after(1, 0))
                    av = a[g.par][:]
                    dve.tensor_scalar(band[0][:], av, T_095, 2.0, ALU.is_gt, ALU.add)
                    dve.tensor_scalar(band[1][:], av, T_025, -1.4, ALU.is_lt, ALU.mult)
                    dve.tensor_scalar(band[2][:], av, T_01, -0.4, ALU.is_lt, ALU.mult).then_inc(band_done, 1)
                    dve.wait_ge(band_done, g.after(3, 1))
                    dve.scalar_tensor_tensor(out=band[3][:], in0=av, scalar=T_085, in1=band[0][:],
                                             op0=ALU.is_gt, op1=ALU.add).then_inc(band_done, 1)
                g = k - 3
                if g.within(GROUPS):
                    dve.wait_ge(rstd_ready, g.after(1, 1))
                    reach(dve, x1T_kept, g.after(1, -1))
                    reach(dve, x1_kept, g.after(1, -1))
                    for b in range(GB):
                        ins = dve.tensor_scalar(x1[g.par][:, b * 128:(b + 1) * 128], y[g.par][:, b, :],
                                                mv[g.par][:, b, 0:1], rstd[g.par][:, b:b + 1],
                                                ALU.subtract, ALU.mult)
                    ins.then_inc(x1_ready, 1)
                g = k - 1
                if g.within(GROUPS):
                    dve.wait_ge(band_done, g.after(3, 2))
                    dve.wait_ge(low_ready, g.after(1, 1))
                    dve.tensor_tensor(band[5][:], band[4][:], band[3][:], ALU.add).then_inc(band_done, 1)
                    dve.wait_ge(band_done, g.after(3, 3))
                    reach(dve, p_ready, g.after(1, -1))
                    dve.tensor_tensor(f2[g.par][:], band[5][:], av, ALU.mult).then_inc(f2_done, 1)
                    dve.wait_ge(f2_done, g.after(1, 1))
                    dve.tensor_reduce(mx[:], f2[g.par][:].rearrange("p (b t) -> p b t", b=GB), X, ALU.max)\
                       .then_inc(mx_done, 1)
                    dve.wait_ge(mx_done, g.after(1, 1))
                    dve.tensor_scalar(nb[g.par][:], mx[:], -0.5, None, ALU.mult).then_inc(f_ready, 1)
                g = k
                if g.within(GROUPS):
                    dve.wait_ge(v_made, g.after(1, 1))
                    reach(dve, a_ready, g.after(1, 0))
                    dve.tensor_scalar(rb[:], psR[:, 0:GB], w.beta[:], SCALE, ALU.add, ALU.mult).then_inc(rb_ready, 1)
                    reach(dve, o_made, g.after(1, -1))
                    dve.tensor_tensor(vp[g.par][:].rearrange("p (b e) -> p b e", b=GB),
                                      psV[:].rearrange("p (b e) -> p b e", b=GB),
                                      w.b2[:].unsqueeze(1).to_broadcast([128, GB, 128]), ALU.add).then_inc(v_ready, 1)
                g = k - 2
                if g.within(GROUPS):
                    dve.wait_ge(o_made, g.after(1, 1))
                    dve.wait_ge(p_ready, g.after(1, 1))
                    reach(dve, mv_ready, g.after(1, 0))
                    dve.reciprocal(rinv[:], sums[g.par][:]).then_inc(y_chain, 1)
                    dve.wait_ge(y_chain, g.after(3, 1))
                    reach(dve, x1_ready, g.after(1, -1))
                    for b in range(GB):
                        c = slice(b * 128, (b + 1) * 128)
                        ins = dve.scalar_tensor_tensor(out=y[g.par][:, b, :], in0=psO[:, c], scalar=rinv[:, b:b + 1],
                                                       in1=w.xres[:, bass.ds(g.n * 512 + b * 128, 128)],
                                                       op0=ALU.mult, op1=ALU.add)
                    ins.then_inc(y_chain, 1)
                    dve.wait_ge(y_chain, g.after(3, 2))
                    for b in range(GB):
                        ins = dve.bn_stats(stats[:, b, :], y[g.par][:, b, :])
                    ins.then_inc(y_chain, 1)
                    dve.wait_ge(y_chain, g.after(3, 3))
                    dve.memset(w.scratch[:], 0.0)
                    for b in range(GB):
                        ins = dve.bn_aggr(mv[g.par][:, b, :], stats[:, b, :])
                    ins.then_inc(mv_ready, 1)
            steps(dve, GROUPS, 3, step)


def attend_context(nc, io, w):
    PAIRS = B // 2
    HW = 4 * JP
    with ExitStack() as ctx:
        st = Store(nc, ctx, "cross")
        cg = [st.sb(f"cg{i}", [CD, 2 * JP]) for i in range(2)]
        qh = [st.sb(f"qh{i}", [128, 256], F32R) for i in range(2)]
        ql = [st.sb(f"ql{i}", [128, 256], F32R) for i in range(2)]
        fp = [st.sb(f"fp{i}", [128, 2, JP], BF16) for i in range(2)]
        kc = st.sb("kc", [128, 2 * JP])
        kb = st.sb("kb", [128, 2, 4, JP])
        kbh = [st.sb(f"kbh{i}", [128, 2, 4, JP], F32R) for i in range(2)]
        kbl = [st.sb(f"kbl{i}", [128, 2, 4, JP], F32R) for i in range(2)]
        v32 = st.sb("v32", [J, 256])
        vr = [st.sb(f"vr{i}", [J, 256]) for i in range(2)]
        vs = [st.sb(f"vs{i}", [J, 2, HEADS, 3, 9], BF16) for i in range(2)]
        mx = [st.sb(f"mx{i}", [128, 2, 4], F32R) for i in range(2)]
        p32 = [st.sb(f"p32{i}", [128, 2, HW]) for i in range(2)]
        ph = [st.sb(f"ph{i}", [128, 2, HW], F16) for i in range(2)]
        pl = [st.sb(f"pl{i}", [128, 2, HW], F16) for i in range(2)]
        pTh = [st.sb(f"pTh{i}", [J, 8, 128], F16) for i in range(2)]
        pTl = [st.sb(f"pTl{i}", [J, 8, 128], F16) for i in range(2)]
        o9 = st.sb("o9", [128, HEADS, 9])
        orec = st.sb("orec", [128, HEADS])
        on = st.sb("on", [128, 128])
        oT = st.sb("oT", [128, 128])
        y = [st.sb(f"y{i}", [128, 128]) for i in range(2)]
        stats = st.sb("stats", [128, 6])
        mv = [st.sb(f"mv{i}", [128, 2]) for i in range(2)]
        veps = st.sb("veps", [128, 1])
        rstd = [st.sb(f"rstd{i}", [128, 1]) for i in range(2)]
        xp = [st.sb(f"xp{i}", [128, 128]) for i in range(2)]
        psL = [st.ps(f"L{i}", [128, 2, 512]) for i in range(2)]
        psTh = st.ps("Th", [J, 8, 128], F16)
        psTl = st.ps("Tl", [J, 8, 128], F16)
        psA = st.ps("A", [128, 512])
        psM = st.ps("M", [128, 512])
        QUERY, KEY = slice(0, 256), slice(256, 256 + 2 * JP)
        c_loaded = [st.sem("c_loaded0"), st.sem("c_loaded1")]
        qk_made, qh_ready, ql_ready, kc_ready, kb_done, kbh_ready, kbl_ready, v_made, v32_ready, v_split, vs_ready = (
            st.sem(n) for n in ("qk_made", "qh_ready", "ql_ready", "kc_ready", "kb_done", "kbh_ready",
                                "kbl_ready", "v_made", "v32_ready", "v_split", "vs_ready"))
        s_made, mx_ready, shifted, ph_ready, p32_ready, pl_ready, t_made, pTh_ready, pTl_ready, av_made = (
            st.sem(n) for n in ("s_made", "mx_ready", "shifted", "ph_ready", "p32_ready", "pl_ready", "t_made",
                                "pTh_ready", "pTl_ready", "av_made"))
        o_sum, o_rec, on_ready, oT_made, oT_ready, pj_made, y_done, st_done, mv_ready, ve_done, rstd_ready, x2_ready, xT_made, xh_ready, xl_ready = (
            st.sem(n) for n in ("o_sum", "o_rec", "on_ready", "oT_made", "oT_ready", "pj_made", "y_done", "st_done",
                                "mv_ready", "ve_done", "rstd_ready", "x2_ready", "xT_made", "xh_ready", "xl_ready"))
        consts_set, fp_ready = st.sem("consts_set"), st.sem("fp_ready")
        block = ctx.enter_context(nc.Block())

        def earlier(r, j, s):
            return (r, j - s) if j >= s else (r - 1, j - s + 4)

        @block.sync
        def _(sync):
            sync.dma_start(w.phi[:], io["phi"].rearrange("(c r) d -> r c d", r=128)).then_inc(w.phi_loaded, 16)
            sync.dma_start(w.bias[:], io["phi_b"]).then_inc(w.phi_loaded, 16)

            def step(r):
                if r.within(PAIRS):
                    reach(sync, v_made, r.after(1, -1))
                    sync.dma_start(cg[r.par][:], io["ctxT"][:, bass.ds(r.n * 2 * JP, 2 * JP)])\
                        .then_inc(c_loaded[r.par], 16)
            steps(sync, PAIRS, 0, step)

        @block.tensor
        def _(pe):
            pe.wait_ge(consts_set, 1)

            def queries_keys(r, _):
                pe.wait_ge(c_loaded[r.par], r.turn(16, 16))
                pe.matmul(psM[:, QUERY], w.xqs[:], w.x1T[:, bass.ds(r.n * 256, 256)], start=True, stop=True)
                pe.matmul(psM[:, KEY], w.xk[:], cg[r.par][:], start=True, stop=True).then_inc(qk_made, 1)

            def own_values(r, _):
                for b in range(2):
                    ins = pe.matmul(psM[0:J, b * 128:(b + 1) * 128], cg[r.par][:, b * JP:b * JP + J], w.xv[:],
                                    start=True, stop=True)
                ins.then_inc(v_made, 1)

            def turn_out(r, b):
                pe.wait_ge(on_ready, r.after(2, b + 1))
                pe.transpose(psM[:, 0:128], on[:], w.ident).then_inc(oT_made, 1)

            def project(r, b):
                pe.wait_ge(oT_ready, r.after(2, b + 1))
                pe.matmul(psM[:, 0:128], oT[:], w.xo[:], start=True, stop=True).then_inc(pj_made, 1)

            def turn_x2(r, b):
                pe.wait_ge(x2_ready, r.after(2, b + 1))
                pe.transpose(psM[:, 0:128], xp[b][:], w.ident).then_inc(xT_made, 1)

            USES = [(queries_keys, ql_ready, 0, None), (project, y_done, 3, 1), (own_values, v32_ready, 0, None),
                    (turn_out, oT_ready, 2, 0), (project, y_done, 2, 0), (turn_x2, xl_ready, 3, 1),
                    (turn_x2, xl_ready, 2, 0), (turn_out, oT_ready, 2, 1)]

            def use_bank(k, n):
                make, _, lag, b = USES[n]
                if not (k - lag).within(PAIRS):
                    return
                for back in range(1, 17):
                    m = n - back
                    _, read, lag_m, b_m = USES[m % 8]
                    r = k - lag_m + m // 8
                    if r.within(PAIRS):
                        pe.wait_ge(read, r.after(1, 1) if b_m is None else r.after(2, b_m + 1))
                        break
                make(k - lag, b)

            def scores(r, j):
                if j == 0:
                    pe.wait_ge(fp_ready, r.after(1, 1))
                    pe.wait_ge(kbh_ready, r.after(1, 1))
                    pe.wait_ge(kbl_ready, r.after(1, 1))
                reach(pe, p32_ready, r.after(4, j - 1))
                b, bc = j // 2, slice(j // 2 * 128, j // 2 * 128 + 128)
                for i in range(2):
                    g = 32 * (2 * (j % 2) + i)
                    gr = slice(g, g + 32)
                    out = psL[j % 2][:, i, 0:HW]
                    kh_, kl_ = kbh[r.par][gr, b, :, :], kbl[r.par][gr, b, :, :]
                    pe.matmul(out, qh[r.par][gr, bc], kh_, start=True, stop=False)
                    pe.matmul(out, ql[r.par][gr, bc], kh_, start=False, stop=False)
                    pe.matmul(out, qh[r.par][gr, bc], kl_, start=False, stop=False)
                    fill = fp[r.par][g:g + 1, b, :].unsqueeze(1).to_broadcast([1, 4, JP])
                    ins = pe.matmul(out, w.ones16[g:g + 1, :], fill, start=False, stop=True)
                ins.then_inc(s_made, 1)

            def shift(r, j):
                pe.wait_ge(mx_ready, r.after(4, j + 1))
                for i in range(2):
                    ins = pe.matmul(psL[j % 2][:, i, 0:HW], w.neg_ident[:],
                                    mx[j % 2][:, i, :].unsqueeze(2).to_broadcast([128, 4, JP]),
                                    start=False, stop=True, skip_group_check=True)
                ins.then_inc(shifted, 1)

            def turn(r, j):
                pe.wait_ge(ph_ready, r.after(4, j + 1))
                pe.wait_ge(pl_ready, r.after(4, j + 1))
                reach(pe, pTh_ready, r.after(4, j))
                reach(pe, pTl_ready, r.after(4, j))
                for h in range(8):
                    c = slice(h % 4 * JP, h % 4 * JP + J)
                    pe.transpose(psTh[:, h, :], ph[j % 2][:, h // 4, c], w.ident16[:])
                    ins = pe.transpose(psTl[:, h, :], pl[j % 2][:, h // 4, c], w.ident16[:])
                ins.then_inc(t_made, 1)

            def values(r, j):
                if j == 0:
                    pe.wait_ge(vs_ready, r.after(1, 1))
                if j % 2 == 0:
                    reach(pe, o_sum, r.after(2, j // 2))
                pe.wait_ge(pTh_ready, r.after(4, j + 1))
                pe.wait_ge(pTl_ready, r.after(4, j + 1))
                for h in range(8):
                    head = 8 * (j % 2) + h
                    v = vs[r.par][:, j // 2, head, :, :]
                    pe.matmul(psA[:, head * 27:head * 27 + 27], pTh[j % 2][:, h, :], v, start=True, stop=True)
                    ins = pe.matmul(psA[:, head * 27:head * 27 + 18], pTl[j % 2][:, h, :], v[:, 0:2, :],
                                    start=False, stop=True, skip_group_check=True)
                ins.then_inc(av_made, 1)

            def step(k):
                r = k - 1
                for j in range(4):
                    if r.within(PAIRS):
                        scores(r, j)
                    r3, j3 = earlier(r, j, 3)
                    if r3.within(PAIRS):
                        values(r3, j3)
                    use_bank(k, 2 * j)
                    r2, j2 = earlier(r, j, 2)
                    if r2.within(PAIRS):
                        turn(r2, j2)
                    if r.within(PAIRS):
                        shift(r, j)
                    use_bank(k, 2 * j + 1)
            steps(pe, PAIRS, 3, step)

        @block.scalar
        def _(act):
            def keep_out(r, b):
                act.wait_ge(oT_made, r.after(2, b + 1))
                reach(act, pj_made, r.after(2, b))
                act.copy(oT[:], psM[:, 0:128]).then_inc(oT_ready, 1)

            def keep_high(r, b):
                act.wait_ge(xT_made, r.after(2, b + 1))
                act.copy(w.xh[:, bass.ds(r.n * 256 + b * 128, 128)], psM[:, 0:128]).then_inc(xh_ready, 1)

            def step(k):
                r = k - 1
                for j in range(4):
                    if j == 0 and k.within(PAIRS):
                        act.wait_ge(qk_made, k.after(1, 1))
                        reach(act, shifted, (k - 1).after(4, 0))
                        reach(act, kb_done, k.after(1, 0))
                        act.copy(kc[:], psM[:, KEY]).then_inc(kc_ready, 1)
                        act.copy(qh[k.par][:], psM[:, QUERY]).then_inc(qh_ready, 1)
                    if j == 2 and k.within(PAIRS):
                        act.copy(fp[k.par][:], w.fill[:, bass.ds(k.n * 2 * JP, 2 * JP)]
                                 .rearrange("p (b t) -> p b t", b=2)).then_inc(fp_ready, 1)
                    if j == 1 and k.within(PAIRS):
                        act.wait_ge(v_made, k.after(1, 1))
                        reach(act, v_split, k.after(4, -2))
                        act.copy(v32[:], psM[0:J, 0:256]).then_inc(v32_ready, 1)
                    if j == 3 and (k - 2).within(PAIRS):
                        keep_high(k - 2, 0)
                    r2, j2 = earlier(r, j, 2)
                    if r2.within(PAIRS):
                        act.wait_ge(t_made, r2.after(4, j2 + 1))
                        reach(act, av_made, r2.after(4, j2 - 1))
                        act.copy(pTl[j % 2][:], psTl[:]).then_inc(pTl_ready, 1)
                    if j == 2 and (k - 3).within(PAIRS):
                        keep_high(k - 3, 1)
                    if j % 2 and (k - 2).within(PAIRS):
                        keep_out(k - 2, j // 2)
                    if r.within(PAIRS):
                        act.wait_ge(shifted, r.after(4, j + 1))
                        reach(act, t_made, r.after(4, j - 1))
                        reach(act, pl_ready, r.after(4, j - 1))
                        act.activation(ph[j % 2][:], psL[j % 2][:, :, 0:HW], ACT.Exp).then_inc(ph_ready, 1)
                        act.activation(p32[j % 2][:], psL[j % 2][:, :, 0:HW], ACT.Exp).then_inc(p32_ready, 1)
            steps(act, PAIRS, 3, step)

        @block.vector
        def _(dve):
            for i in range(2):
                dve.memset(xp[i][:, 127:128], 1.0)
                dve.memset(vs[i][:, :, :, 0, 8], 1.0)
                ins = dve.memset(vs[i][:, :, :, 1:3, 8], 0.0)
            ins.then_inc(consts_set, 1)
            dve.wait_ge(consts_set, 1)

            def part(r, c):
                return vs[r.par][:, :, :, c, 0:8]

            def as_heads(t):
                return t[:].rearrange("j (b h e) -> j b h e", b=2, h=HEADS)

            def split_first(r):
                dve.wait_ge(v32_ready, r.after(1, 1))
                reach(dve, av_made, (r - 1).after(4, 0))
                dve.tensor_copy(part(r, 0), as_heads(v32)).then_inc(v_split, 1)
                dve.wait_ge(v_split, r.after(4, 1))
                dve.tensor_tensor(as_heads(vr[0]), as_heads(v32), part(r, 0), ALU.subtract).then_inc(v_split, 1)

            def split_rest(r):
                dve.wait_ge(v_split, r.after(4, 2))
                dve.tensor_copy(part(r, 1), as_heads(vr[0])).then_inc(v_split, 1)
                dve.wait_ge(v_split, r.after(4, 3))
                reach(dve, vs_ready, r.after(1, 0))
                dve.tensor_tensor(as_heads(vr[1]), as_heads(vr[0]), part(r, 1), ALU.subtract).then_inc(v_split, 1)
                dve.wait_ge(v_split, r.after(4, 4))
                dve.tensor_copy(part(r, 2), as_heads(vr[1])).then_inc(vs_ready, 1)

            def sum_parts(r, b):
                dve.wait_ge(av_made, r.after(4, 2 * b + 2))
                reach(dve, on_ready, r.after(2, b))
                dve.tensor_reduce(o9[:], psA[:, 0:432].rearrange("p (h c e) -> p h e c", h=HEADS, c=3), X, ALU.add)\
                    .then_inc(o_sum, 1)

            def divide(r, b):
                dve.wait_ge(o_sum, r.after(2, b + 1))
                dve.reciprocal(orec[:], o9[:, :, 8]).then_inc(o_rec, 1)
                dve.wait_ge(o_rec, r.after(2, b + 1))
                reach(dve, oT_made, r.after(2, b))
                dve.tensor_tensor(on[:].rearrange("p (h e) -> p h e", h=HEADS), o9[:, :, 0:8],
                                  orec[:].unsqueeze(2).to_broadcast([128, HEADS, 8]), ALU.mult).then_inc(on_ready, 1)

            def add_residual(r, b):
                dve.wait_ge(pj_made, r.after(2, b + 1))
                dve.tensor_tensor(y[b][:], psM[:, 0:128], w.xres[:, bass.ds(r.n * 256 + b * 128, 128)], ALU.add)\
                    .then_inc(y_done, 1)

            def statistics(r, b):
                dve.wait_ge(y_done, r.after(2, b + 1))
                dve.bn_stats(stats[:], y[b][:]).then_inc(st_done, 1)
                dve.wait_ge(st_done, r.after(2, b + 1))
                dve.memset(w.scratch[:], 0.0)
                dve.bn_aggr(mv[b][:], stats[:]).then_inc(mv_ready, 1)

            def normalise(r, b):
                dve.wait_ge(rstd_ready, r.after(2, b + 1))
                reach(dve, xT_made, (r - 1).after(2, b + 1))
                dve.tensor_scalar(xp[b][:, 0:127], y[b][:, 0:127], mv[b][:, 0:1], rstd[b][:],
                                  ALU.subtract, ALU.mult).then_inc(x2_ready, 1)

            def keep_residual(r, b):
                dve.tensor_scalar(w.xres[:, bass.ds(r.n * 256 + b * 128, 128)], y[b][:], mv[b][:, 0:1], rstd[b][:],
                                  ALU.subtract, ALU.mult)

            def low_part(r, b):
                at = bass.ds(r.n * 256 + b * 128, 128)
                dve.wait_ge(xh_ready, r.after(2, b + 1))
                dve.tensor_tensor(w.xl[:, at], psM[:, 0:128], w.xh[:, at], ALU.subtract).then_inc(xl_ready, 1)

            def step(k):
                r = k - 1
                for j in range(4):
                    if r.within(PAIRS):
                        dve.wait_ge(s_made, r.after(4, j + 1))
                        reach(dve, shifted, r.after(4, j - 1))
                        dve.tensor_reduce(mx[j % 2][:], psL[j % 2][:, :, 0:HW].rearrange("p i (h t) -> p i h t", h=4),
                                          X, ALU.max).then_inc(mx_ready, 1)
                    if j == 0 and k.within(PAIRS):
                        dve.wait_ge(qh_ready, k.after(1, 1))
                        dve.tensor_tensor(ql[k.par][:], psM[:, QUERY], qh[k.par][:], ALU.subtract).then_inc(ql_ready, 1)
                    if j % 2 and (k - 2).within(PAIRS):
                        if j == 3:
                            keep_residual(k - 2, 0)
                            low_part(k - 2, 0)
                        divide(k - 2, j // 2)
                    if j == 1 and (k - 3).within(PAIRS):
                        statistics(k - 3, 1)
                    if j == 1 and k.within(PAIRS):
                        dve.wait_ge(kb_done, k.after(1, 1))
                        dve.tensor_copy(kbh[k.par][:], kb[:]).then_inc(kbh_ready, 1)
                    if j == 2 and (k - 2).within(PAIRS):
                        add_residual(k - 2, 0)
                        sum_parts(k - 2, 1)
                        statistics(k - 2, 0)
                    r2, j2 = earlier(r, j, 2)
                    if r2.within(PAIRS):
                        dve.wait_ge(t_made, r2.after(4, j2 + 1))
                        reach(dve, av_made, r2.after(4, j2 - 1))
                        dve.tensor_copy(pTh[j % 2][:], psTh[:]).then_inc(pTh_ready, 1)
                    if j == 2 and (k - 3).within(PAIRS):
                        low_part(k - 3, 1)
                    if j == 0 and (k - 2).within(PAIRS):
                        sum_parts(k - 2, 0)
                    if j == 0 and (k - 3).within(PAIRS):
                        add_residual(k - 3, 1)
                    if j == 0 and r.within(PAIRS):
                        split_rest(r)
                    if j == 1 and (k - 3).within(PAIRS):
                        normalise(k - 3, 1)
                        keep_residual(k - 3, 1)
                    if j == 2 and (k - 2).within(PAIRS):
                        normalise(k - 2, 0)
                    if j == 3 and k.within(PAIRS):
                        split_first(k)
            steps(dve, PAIRS, 3, step)

        @block.gpsimd
        def _(pool):
            def inverse_deviation(r, b):
                pool.wait_ge(mv_ready, r.after(2, b + 1))
                pool.tensor_tensor(veps[:], mv[b][:, 1:2], w.eps[:, 0:1], ALU.add).then_inc(ve_done, 1)
                pool.wait_ge(ve_done, r.after(2, b + 1))
                pool.tensor_tensor(rstd[b][:], veps[:], w.neg_half[:, 0:1], ALU.pow).then_inc(rstd_ready, 1)

            def step(k):
                r = k - 1
                for j in range(4):
                    if j == 0 and k.within(PAIRS):
                        pool.wait_ge(kc_ready, k.after(1, 1))
                        reach(pool, kbl_ready, k.after(1, 0))
                        pool.tensor_tensor(
                            kb[:], kc[:].rearrange("p (b t) -> p b t", b=2).unsqueeze(2).to_broadcast([128, 2, 4, JP]),
                            w.head.unsqueeze(1).unsqueeze(3).to_broadcast([128, 2, 4, JP]), ALU.mult).then_inc(kb_done, 1)
                    if j == 1 and (k - 3).within(PAIRS):
                        inverse_deviation(k - 3, 1)
                    if j == 2 and (k - 2).within(PAIRS):
                        inverse_deviation(k - 2, 0)
                    if j == 2 and k.within(PAIRS):
                        pool.wait_ge(kbh_ready, k.after(1, 1))
                        pool.tensor_tensor(kbl[k.par][:], kb[:], kbh[k.par][:], ALU.subtract).then_inc(kbl_ready, 1)
                    if r.within(PAIRS):
                        pool.wait_ge(p32_ready, r.after(4, j + 1))
                        reach(pool, t_made, r.after(4, j - 1))
                        pool.tensor_tensor(pl[j % 2][:], p32[j % 2][:], ph[j % 2][:], ALU.subtract).then_inc(pl_ready, 1)
            steps(pool, PAIRS, 3, step)


def prepare_slots(nc, w):
    with ExitStack() as ctx:
        st = Store(nc, ctx, "prep")
        diff = st.sb("diff", [128, 16, 128])
        psW = st.ps("W", [128, NP])
        diff_done, w_made, wh_done = (st.sem(n) for n in ("diff_done", "w_made", "wh_done"))
        block = ctx.enter_context(nc.Block())

        def by_quarter(t, c):
            return t[:].rearrange("d (q c g p) -> d c g q p", q=4, c=4, g=16)[:, c]

        def by_expert(t, c):
            return t[:, c * 512:(c + 1) * 512].rearrange("d (g q p) -> d g q p", g=16, q=4)

        @block.vector
        def _(dve):
            dve.wait_ge(w.phi_loaded, 32)
            dve.tensor_copy(diff[:, :, 127], w.bias[:])
            for c in range(4):
                p = slice(4 * c, 4 * c + 4)
                dve.tensor_tensor(diff[:, p, 0:127], w.phi[:, p, 0:127], w.phi[:, p, 127:128].to_broadcast([128, 4, 127]),
                                  ALU.subtract).then_inc(diff_done, 1)
            for c in range(4):
                b = slice(c * 512, (c + 1) * 512)
                dve.wait_ge(wh_done, c + 1)
                dve.tensor_tensor(w.w1l[:, b], psW[:, b], w.w1h[:, b], ALU.subtract)
                dve.tensor_tensor(by_quarter(w.w2l, c), by_expert(psW, c), by_quarter(w.w2h, c), ALU.subtract)

        @block.tensor
        def _(pe):
            for c in range(16):
                pe.wait_ge(diff_done, c // 4 + 1)
                ins = pe.transpose(psW[:, c * 128:(c + 1) * 128], diff[:, c, :], w.ident)
                if c % 4 == 3:
                    ins.then_inc(w_made, 1)

        @block.scalar
        def _(act):
            for c in range(4):
                b = slice(c * 512, (c + 1) * 512)
                act.wait_ge(w_made, c + 1)
                act.copy(w.w1h[:, b], psW[:, b])
                act.copy(by_quarter(w.w2h, c), by_expert(psW, c)).then_inc(wh_done, 1)


def gather_slots(nc, io, w, psX):
    TILES = TOKENS // 128
    with ExitStack() as ctx:
        st = Store(nc, ctx, "gather")
        xh = [st.sb(f"xh{i}", [128, 128], F32R) for i in range(2)]
        xl = [st.sb(f"xl{i}", [128, 128], F32R) for i in range(2)]
        x2 = [st.sb(f"x2{i}", [128, 128]) for i in range(2)]
        mx = [st.sb(f"mx{i}", [128, 2, 16], F32R) for i in range(2)]
        e = [st.sb(f"e{i}", [128, 2, 16, 32]) for i in range(2)]
        rsum = [st.sb(f"rsum{i}", [128, 32]) for i in range(2)]
        rinv = [st.sb(f"rinv{i}", [128, 32]) for i in range(2)]
        dd = [st.sb(f"d{i}", [128, 2, 512]) for i in range(2)]
        psL = [st.ps(f"L{i}", [128, 2, 512]) for i in range(2)]
        x_ready, x2_ready = st.sem("x_ready"), st.sem("x2_ready")
        l_made, mx_ready, shifted, e_ready, sum_done, rinv_ready, d_ready, x_made = (
            st.sem(n) for n in ("l_made", "mx_ready", "shifted", "e_ready", "sum_done", "rinv_ready", "d_ready",
                                "x_made"))
        block = ctx.enter_context(nc.Block())

        def earlier(t, j, s):
            return (t, j - s) if j >= s else (t - (s - j + 1) // 2, (j - s) % 2)

        @block.sync
        def _(sync):
            sync.dma_start(w.we[:], io["expert_w"].rearrange("n d h -> d n h")).then_inc(w.we_loaded, 16)
            sync.dma_start(w.beT[:], io["expert_bT"]).then_inc(w.be_loaded, 16)

        @block.tensor
        def _(pe):
            def logits(t, j):
                pe.wait_ge(x_ready, t.after(1, 1))
                reach(pe, e_ready, t.after(2, j - 1))
                for n, (xs, ws) in enumerate(((xh, w.w1h), (xl, w.w1h), (xh, w.w1l))):
                    for i in range(2):
                        c = (2 * j + i) * 512
                        ins = pe.matmul(psL[j][:, i, :], xs[t.par][:], ws[:, c:c + 512], start=n == 0, stop=n == 2)
                ins.then_inc(l_made, 1)

            def gather(t, j):
                if j == 0:
                    pe.wait_ge(x2_ready, t.after(1, 1))
                pe.wait_ge(d_ready, t.after(2, j + 1))
                for i in range(2):
                    ins = pe.matmul(psX[:, 2 * j + i, :], x2[t.par][:], dd[j][:, i, :], start=t.known and t.n == 0,
                                    stop=t.known and t.n == TILES - 1)
                ins.then_inc(x_made, 1)

            def shift(t, j):
                pe.wait_ge(mx_ready, t.after(2, j + 1))
                for i in range(2):
                    ins = pe.matmul(psL[j][:, i, :], w.neg_ident[:],
                                    mx[j][:, i, :].unsqueeze(2).to_broadcast([128, 16, 32]), start=False, stop=True,
                                    skip_group_check=True)
                ins.then_inc(shifted, 1)

            def step(t):
                for j in range(2):
                    if t.within(TILES):
                        logits(t, j)
                    t3, j3 = earlier(t, j, 3)
                    if t3.within(TILES):
                        gather(t3, j3)
                    if t.within(TILES):
                        shift(t, j)
            steps(pe, TILES, 2, step)

        @block.scalar
        def _(act):
            def copies(t):
                at = bass.ds(t.n * 128, 128)
                reach(act, l_made, t.after(2, -2))
                act.copy(xh[t.par][:], w.xh[:, at].bitcast(F32))
                act.copy(xl[t.par][:], w.xl[:, at].bitcast(F32)).then_inc(x_ready, 1)

            def step(t):
                for j in range(2):
                    if j == 0 and t.within(TILES):
                        copies(t)
                    if j == 1 and t.within(TILES):
                        reach(act, x_made, t.after(2, -2))
                        act.copy(x2[t.par][:], w.xres[:, bass.ds(t.n * 128, 128)]).then_inc(x2_ready, 1)
                    tu, ju = earlier(t, j, 1)
                    if tu.within(TILES):
                        act.wait_ge(shifted, tu.after(2, ju + 1))
                        reach(act, d_ready, tu.after(2, ju - 1))
                        act.activation(e[ju][:], psL[ju][:].rearrange("p i (n s) -> p i n s", n=16), ACT.Exp)\
                            .then_inc(e_ready, 1)
            steps(act, TILES, 2, step)

        @block.vector
        def _(dve):
            def step(t):
                for j in range(2):
                    if t.within(TILES):
                        dve.wait_ge(l_made, t.after(2, j + 1))
                        reach(dve, shifted, t.after(2, j - 1))
                        dve.tensor_reduce(mx[j][:], psL[j][:].rearrange("p i (n s) -> p i n s", n=16), X, ALU.max)\
                            .then_inc(mx_ready, 1)
                    tu, ju = earlier(t, j, 1)
                    if tu.within(TILES):
                        dve.wait_ge(e_ready, tu.after(2, ju + 1))
                        reach(dve, rinv_ready, tu.after(2, ju - 1))
                        dve.tensor_reduce(rsum[ju][:].rearrange("p (i n) -> p i n", i=2), e[ju][:], X, ALU.add)\
                            .then_inc(sum_done, 1)
                        dve.wait_ge(sum_done, tu.after(2, ju + 1))
                        reach(dve, d_ready, tu.after(2, ju - 1))
                        dve.reciprocal(rinv[ju][:], rsum[ju][:]).then_inc(rinv_ready, 1)
            steps(dve, TILES, 2, step)

        @block.gpsimd
        def _(pool):
            def step(t):
                for j in range(2):
                    tu, ju = earlier(t, j, 1)
                    if tu.within(TILES):
                        pool.wait_ge(rinv_ready, tu.after(2, ju + 1))
                        reach(pool, x_made, tu.after(2, ju - 1))
                        pool.tensor_tensor(
                            dd[ju][:].rearrange("p i (n s) -> p i n s", n=16), e[ju][:],
                            rinv[ju][:].rearrange("p (i n) -> p i n", i=2).unsqueeze(3).to_broadcast([128, 2, 16, 32]),
                            ALU.mult).then_inc(d_ready, 1)
            steps(pool, TILES, 2, step)


def run_experts(nc, w, psX):
    with ExitStack() as ctx:
        st = Store(nc, ctx, "expert")
        xt = st.sb("xt", [128, 4, 512])
        stats = st.sb("stats", [128, 16, 6])
        mv = st.sb("mv", [128, 16, 2])
        veps = st.sb("veps", [128, 16])
        rstd = st.sb("rstd", [128, 16])
        n = st.sb("n", [128, 16, 128])
        z = st.sb("z", [128, 16, 128])
        zT = st.sb("zT", [128, 4, 512])
        y = n
        yT = xt
        psT = st.ps("T", [128, 16, 128])
        psY = psX
        (xt_ready, t_made, st_done, mv_ready, ve_done, rstd_ready, n_ready, z_ready, zT_made, zT_ready, y_made,
         y_ready, yT_made, yT_ready, yk_made) = (
            st.sem(n) for n in ("xt_ready", "t_made", "st_done", "mv_ready", "ve_done", "rstd_ready", "n_ready",
                                "z_ready", "zT_made", "zT_ready", "y_made", "y_ready", "yT_made", "yT_ready", "yk_made"))
        block = ctx.enter_context(nc.Block())
        PARTS = [range(4 * c, 4 * c + 4) for c in range(4)]

        @block.vector
        def _(dve):
            for c in range(4):
                dve.tensor_scalar(xt[:, c, :], psX[:, c, :], 65000.0, -33000.0, ALU.min, ALU.max).then_inc(xt_ready, 1)
            def statistics(c):
                dve.wait_ge(t_made, c + 1)
                for k in PARTS[c]:
                    ins = dve.bn_stats(stats[:, k, :], psT[:, k, :])
                ins.then_inc(st_done, 1)
                dve.wait_ge(st_done, c + 1)
                dve.memset(w.scratch[:], 0.0)
                for k in PARTS[c]:
                    ins = dve.bn_aggr(mv[:, k, :], stats[:, k, :])
                ins.then_inc(mv_ready, 1)

            def normalise(c):
                dve.wait_ge(rstd_ready, c + 1)
                for k in PARTS[c]:
                    ins = dve.tensor_scalar(n[:, k, :], psT[:, k, :], mv[:, k, 0:1], rstd[:, k:k + 1],
                                            ALU.subtract, ALU.mult)
                ins.then_inc(n_ready, 1)

            for c in range(4):
                statistics(c)
                if c > 0:
                    normalise(c - 1)
            normalise(3)
            dve.wait_ge(w.be_loaded, 16)
            for c in range(4):
                dve.wait_ge(yT_made, c + 1)
                bias = w.beT[:, 16 * c:16 * c + 16].unsqueeze(1).unsqueeze(3).to_broadcast([128, 4, 16, 8])
                dve.tensor_tensor(yT[:, c, :].rearrange("h (q g p) -> h q g p", q=4, g=16),
                                  psT[:, 4 * c:4 * c + 4, :].rearrange("h k (g q p) -> h q (k g) p", q=4, p=8), bias,
                                  ALU.add).then_inc(yT_ready, 1)

        @block.gpsimd
        def _(pool):
            for c in range(4):
                p = slice(4 * c, 4 * c + 4)
                pool.wait_ge(mv_ready, c + 1)
                pool.tensor_tensor(veps[:, p], mv[:, p, 1], w.eps[:, p], ALU.add).then_inc(ve_done, 1)
                pool.wait_ge(ve_done, c + 1)
                pool.tensor_tensor(rstd[:, p], veps[:, p], w.neg_half[:, p], ALU.pow).then_inc(rstd_ready, 1)

        @block.tensor
        def _(pe):
            def products(c):
                pe.wait_ge(zT_ready, c + 1)
                for g in range(16):
                    out = psY[g % 4 * 32:g % 4 * 32 + 32, c, g // 4 * 128:(g // 4 + 1) * 128]
                    ins = pe.matmul(out, zT[:, c, g * 32:(g + 1) * 32], w.we[:, 16 * c + g, :], start=True, stop=True)
                ins.then_inc(y_made, 1)

            def turn_products(c):
                pe.wait_ge(y_ready, c + 1)
                for k in PARTS[c]:
                    ins = pe.transpose(psT[:, k, :], y[:, k, :], w.ident)
                ins.then_inc(yT_made, 1)

            def turn_ordered(c):
                pe.wait_ge(yT_ready, c + 1)
                for q in range(4):
                    ins = pe.transpose(psT[:, 4 * c + q, :], yT[:, c, q * 128:(q + 1) * 128], w.ident)
                ins.then_inc(yk_made, 1)

            for c in range(4):
                pe.wait_ge(xt_ready, c + 1)
                for k in PARTS[c]:
                    ins = pe.transpose(psT[:, k, :], xt[:, c, k % 4 * 128:(k % 4 + 1) * 128], w.ident)
                ins.then_inc(t_made, 1)
            pe.wait_ge(w.we_loaded, 16)
            for c in range(4):
                pe.wait_ge(z_ready, c + 1)
                for k in PARTS[c]:
                    ins = pe.transpose(psT[:, k, :], z[:, k, :], w.ident)
                ins.then_inc(zT_made, 1)
                if c > 0:
                    products(c - 1)
                if c > 1:
                    turn_products(c - 2)
            products(3)
            turn_products(2)
            turn_ordered(0)
            turn_ordered(1)
            turn_products(3)
            turn_ordered(2)
            turn_ordered(3)

        @block.scalar
        def _(act):
            def keep_products(c):
                act.wait_ge(y_made, c + 1)
                act.copy(y[:, 4 * c:4 * c + 4, :], psY[:, c, :].rearrange("s (k h) -> s k h", k=4)).then_inc(y_ready, 1)

            for c in range(4):
                p = slice(4 * c, 4 * c + 4)
                act.wait_ge(n_ready, c + 1)
                act.activation(z[:, p, :], n[:, p, :], ACT.Tanh).then_inc(z_ready, 1)
                act.wait_ge(zT_made, c + 1)
                act.copy(zT[:, c, :], psT[:, p, :].rearrange("d k s -> d (k s)")).then_inc(zT_ready, 1)
                if c > 1:
                    keep_products(c - 2)
            keep_products(2)
            keep_products(3)
            for c in range(4):
                act.wait_ge(yk_made, c + 1)
                act.copy(w.yk[:].rearrange("s (q c) h -> s q c h", q=4)[:, :, c, :], psT[:, 4 * c:4 * c + 4, :])


def mix_slots(nc, w, out):
    TILES = TOKENS // 256
    with ExitStack() as ctx:
        st = Store(nc, ctx, "mix")
        mg = [st.sb(f"mg{i}", [128, 256]) for i in range(2)]
        m8 = st.sb("m8", [128, 2, 8])
        me = [st.sb(f"me{i}", [128, 2, 16, 8], F32R) for i in range(2)]
        e = [st.sb(f"e{i}", [128, 4, 256]) for i in range(4)]
        sg = [st.sb(f"sg{i}", [128, 256]) for i in range(2)]
        s8 = st.sb("s8", [128, 2, 8])
        r8 = st.sb("r8", [128, 2, 8])
        re = [st.sb(f"re{i}", [128, 2, 16, 8]) for i in range(2)]
        rinv = [st.sb(f"rinv{i}", [128, 256]) for i in range(2)]
        cc = [st.sb(f"c{i}", [128, 4, 256]) for i in range(2)]
        yT = st.sb("yT", [128, 256])
        y = [st.sb(f"y{i}", [128, 2, 128]) for i in range(2)]
        stats = st.sb("stats", [128, 2, 6])
        mv = [st.sb(f"mv{i}", [128, 2, 2]) for i in range(2)]
        veps = st.sb("veps", [128, 2])
        rstd = [st.sb(f"rstd{i}", [128, 2]) for i in range(2)]
        res = [st.sb(f"res{i}", [128, 2, 128]) for i in range(2)]
        psL = [st.ps(f"L{i}", [128, 2, 512]) for i in range(2)]
        psG = st.ps("G", [128, 4, 128])
        psR = st.ps("R", [128, 512])
        psY = st.ps("Y", [128, 256])
        psF = st.ps("F", [128, 2, 128])
        (l_made, mg_ready, g_made, m8_ready, me_ready, shifted, e_ready, sg_ready, sums_made, s8_done, r8_ready,
         re_ready, r_made,
         rinv_ready, c_ready, y_made) = (
            st.sem(n) for n in ("l_made", "mg_ready", "g_made", "m8_ready", "me_ready", "shifted", "e_ready", "sg_ready",
                                "sums_made", "s8_done", "r8_ready", "re_ready", "r_made", "rinv_ready", "c_ready", "y_made"))
        yT_ready, f_made, y_done, st_done, mv_ready, ve_done, rstd_ready, res_ready = (
            st.sem(n) for n in ("yT_ready", "f_made", "y_done", "st_done", "mv_ready", "ve_done", "rstd_ready",
                                "res_ready"))
        stored = [st.sem("stored0"), st.sem("stored1")]
        block = ctx.enter_context(nc.Block())

        def earlier(t, j, s):
            return (t, j - s) if j >= s else (t - 1, j - s + 4)

        @block.sync
        def _(sync):
            def step(k):
                t = k - 2
                if t.within(TILES):
                    sync.wait_ge(res_ready, t.after(1, 1))
                    sync.dma_start(out[bass.ds(t.n * 256, 256), :].rearrange("(b s) d -> s b d", b=2), res[t.par][:])\
                        .then_inc(stored[t.par], 16)
            steps(sync, TILES, 2, step)
            for i in range(2):
                sync.wait_ge(stored[i], 16 * (TILES // 2))

        @block.tensor
        def _(pe):
            def logits(t, j):
                reach(pe, e_ready, t.after(4, j - 1))
                at = bass.ds(t.n * 256, 256)
                for c in range(4):
                    o = psL[j % 2][:, c // 2, c % 2 * 256:(c % 2 + 1) * 256]
                    k = slice((4 * j + c) * 128, (4 * j + c + 1) * 128)
                    pe.matmul(o, w.w2h[:, k], w.xh[:, at], start=(c % 2 == 0), stop=False, skip_group_check=True)
                    pe.matmul(o, w.w2h[:, k], w.xl[:, at], start=False, stop=False, skip_group_check=True)
                    ins = pe.matmul(o, w.w2l[:, k], w.xh[:, at], start=False, stop=True, skip_group_check=True)
                ins.then_inc(l_made, 1)

            def shift(t, j):
                pe.wait_ge(me_ready, t.after(4, j + 1))
                for b in range(2):
                    for i in range(2):
                        o = psL[j % 2][:, i, :].rearrange("p (c t) -> p c t", c=2)[:, :, b * 128:(b + 1) * 128]
                        ins = pe.matmul(o, me[j % 2][:, b, :, :],
                                        w.neg_ident[:].unsqueeze(1).to_broadcast([128, 2, 128]),
                                        start=False, stop=True, skip_group_check=True)
                ins.then_inc(shifted, 1)

            def repeat_inverses(t, j):
                pe.wait_ge(re_ready, t.after(4, j + 1))
                reach(pe, rinv_ready, t.after(4, j))
                for b in range(2):
                    ins = pe.transpose(psR[:, b * 128:(b + 1) * 128], re[j % 2][:, b, :, :], w.ident)
                ins.then_inc(r_made, 1)

            def spread(t, j, half):
                if half == 0:
                    pe.wait_ge(c_ready, t.after(4, j + 1))
                    if j == 0:
                        reach(pe, yT_ready, t.after(1, 0))
                for c in range(2 * half, 2 * half + 2):
                    ins = pe.matmul(psY[:], w.yk[:, 4 * j + c, :], cc[j % 2][:, c, :],
                                    start=(j == 0 and c == 0), stop=(j == 3 and c == 3))
                if half == 1:
                    ins.then_inc(y_made, 1)

            def turn_max(t, j):
                pe.wait_ge(mg_ready, t.after(4, j + 1))
                for b in range(2):
                    ins = pe.transpose(psG[:, b, :], mg[j % 2][:, b * 128:(b + 1) * 128], w.ident)
                ins.then_inc(g_made, 1)

            def turn_sums(t, j):
                pe.wait_ge(sg_ready, t.after(4, j + 1))
                for b in range(2):
                    ins = pe.transpose(psG[:, 2 + b, :], sg[j % 2][:, b * 128:(b + 1) * 128], w.ident)
                ins.then_inc(sums_made, 1)

            def step(k):
                for j in range(4):
                    if k.within(TILES):
                        logits(k, j)
                    t = k - 2
                    if j == 0 and t.within(TILES):
                        pe.wait_ge(yT_ready, t.after(1, 1))
                        reach(pe, y_done, t.after(1, 0))
                        for b in range(2):
                            ins = pe.transpose(psF[:, b, :], yT[:, b * 128:(b + 1) * 128], w.ident)
                        ins.then_inc(f_made, 1)
                    t1, j1 = earlier(k, j, 1)
                    if t1.within(TILES):
                        shift(t1, j1)
                    if (k - 1).within(TILES):
                        spread(k - 1, j, 0)
                    t3, j3 = earlier(k, j, 3)
                    if t3.within(TILES):
                        repeat_inverses(t3, j3)
                    if (k - 1).within(TILES):
                        spread(k - 1, j, 1)
                    if t1.within(TILES):
                        pe.wait_ge(m8_ready, t1.after(4, j1 + 1))
                    if t3.within(TILES):
                        pe.wait_ge(s8_done, t3.after(4, j3 + 1))
                    if k.within(TILES):
                        turn_max(k, j)
                    t2, j2 = earlier(k, j, 2)
                    if t2.within(TILES):
                        turn_sums(t2, j2)
            steps(pe, TILES, 2, step)

        @block.scalar
        def _(act):
            def step(k):
                for j in range(4):
                    t = k - 2
                    if j == 0 and t.within(TILES):
                        act.wait_ge(y_made, t.after(4, 4))
                        reach(act, f_made, t.after(1, 0))
                        act.copy(yT[:], psY[:]).then_inc(yT_ready, 1)
                    t1, j1 = earlier(k, j, 1)
                    t3, j3 = earlier(k, j, 3)
                    if t1.within(TILES):
                        act.wait_ge(m8_ready, t1.after(4, j1 + 1))
                        reach(act, shifted, t1.after(4, j1 - 1))
                        act.copy(me[j1 % 2][:], m8[:].unsqueeze(2).to_broadcast([128, 2, 16, 8])).then_inc(me_ready, 1)
                    if t3.within(TILES):
                        act.wait_ge(r8_ready, t3.after(4, j3 + 1))
                        reach(act, r_made, t3.after(4, j3 - 1))
                        act.copy(re[j3 % 2][:], r8[:].unsqueeze(2).to_broadcast([128, 2, 16, 8])).then_inc(re_ready, 1)
                    if t1.within(TILES):
                        act.wait_ge(shifted, t1.after(4, j1 + 1))
                        reach(act, c_ready, t1.after(4, j1 - 3))
                        act.activation(e[j1][:], psL[j1 % 2][:].rearrange("p i (c t) -> p (i c) t", c=2), ACT.Exp)\
                            .then_inc(e_ready, 1)
                    if t3.within(TILES):
                        act.wait_ge(r_made, t3.after(4, j3 + 1))
                        reach(act, c_ready, t3.after(4, j3 - 1))
                        act.copy(rinv[j3 % 2][:], psR[:, 0:256]).then_inc(rinv_ready, 1)
            steps(act, TILES, 2, step)

        @block.vector
        def _(dve):
            def step(k):
                for j in range(4):
                    if k.within(TILES):
                        dve.wait_ge(l_made, k.after(4, j + 1))
                        reach(dve, g_made, k.after(4, j - 1))
                        dve.tensor_reduce(mg[j % 2][:], psL[j % 2][:].rearrange("p i (c t) -> p t (i c)", c=2), X,
                                          ALU.max).then_inc(mg_ready, 1)
                    t1, j1 = earlier(k, j, 1)
                    if t1.within(TILES):
                        dve.wait_ge(e_ready, t1.after(4, j1 + 1))
                        reach(dve, sums_made, t1.after(4, j1 - 1))
                        dve.tensor_reduce(sg[j1 % 2][:], e[j1][:].rearrange("p c t -> p t c"), X, ALU.add)\
                            .then_inc(sg_ready, 1)
                    t2, j2 = earlier(k, j, 2)
                    if t2.within(TILES):
                        dve.wait_ge(sums_made, t2.after(4, j2 + 1))
                    if k.within(TILES):
                        dve.wait_ge(g_made, k.after(4, j + 1))
                        reach(dve, me_ready, k.after(4, j))
                        dve.tensor_reduce(m8[:], psG[:, 0:2, :].rearrange("t b (g p) -> t b p g", g=16), X,
                                          ALU.max).then_inc(m8_ready, 1)
                    if t2.within(TILES):
                        reach(dve, r8_ready, t2.after(4, j2))
                        dve.tensor_reduce(s8[:], psG[:, 2:4, :].rearrange("t b (g p) -> t b p g", g=16), X, ALU.add)\
                            .then_inc(s8_done, 1)
                        dve.wait_ge(s8_done, t2.after(4, j2 + 1))
                        reach(dve, re_ready, t2.after(4, j2))
                        dve.reciprocal(r8[:], s8[:]).then_inc(r8_ready, 1)
                    t = k - 2
                    if j == 1 and t.within(TILES):
                        dve.wait_ge(f_made, t.after(1, 1))
                        reach(dve, res_ready, t.after(1, -1))
                        dve.tensor_tensor(y[t.par][:], psF[:], w.xres[:, bass.ds(t.n * 256, 256)]
                                          .rearrange("s (b d) -> s b d", b=2), ALU.add).then_inc(y_done, 1)
                        dve.wait_ge(y_done, t.after(1, 1))
                        for b in range(2):
                            ins = dve.bn_stats(stats[:, b, :], y[t.par][:, b, :])
                        ins.then_inc(st_done, 1)
                        dve.wait_ge(st_done, t.after(1, 1))
                        dve.memset(w.scratch[:], 0.0)
                        for b in range(2):
                            ins = dve.bn_aggr(mv[t.par][:, b, :], stats[:, b, :])
                        ins.then_inc(mv_ready, 1)
                    if j == 3 and t.within(TILES):
                        dve.wait_ge(rstd_ready, t.after(1, 1))
                        if not (t.known and t.n < 2):
                            dve.wait_ge(stored[t.par], t.turn(16, 0))
                        for b in range(2):
                            ins = dve.tensor_scalar(res[t.par][:, b, :], y[t.par][:, b, :], mv[t.par][:, b, 0:1],
                                                    rstd[t.par][:, b:b + 1], ALU.subtract, ALU.mult)
                        ins.then_inc(res_ready, 1)
            steps(dve, TILES, 2, step)

        @block.gpsimd
        def _(pool):
            def step(k):
                for j in range(4):
                    t3, j3 = earlier(k, j, 3)
                    if t3.within(TILES):
                        pool.wait_ge(rinv_ready, t3.after(4, j3 + 1))
                        reach(pool, y_made, t3.after(4, j3 - 1))
                        pool.tensor_tensor(cc[j3 % 2][:], e[j3][:],
                                           rinv[j3 % 2][:].unsqueeze(1).to_broadcast([128, 4, 256]), ALU.mult)\
                            .then_inc(c_ready, 1)
                    t = k - 2
                    if j == 1 and t.within(TILES):
                        pool.wait_ge(mv_ready, t.after(1, 1))
                        pool.tensor_tensor(veps[:], mv[t.par][:, :, 1], w.eps[:, 0:2], ALU.add).then_inc(ve_done, 1)
                        pool.wait_ge(ve_done, t.after(1, 1))
                        pool.tensor_tensor(rstd[t.par][:], veps[:], w.neg_half[:, 0:2], ALU.pow).then_inc(rstd_ready, 1)
            steps(pool, TILES, 2, step)


class Weights:
    pass


def decoder_block(nc, io, out):
    with ExitStack() as ctx:
        st = Store(nc, ctx, "kept")
        w = Weights()
        w.xres = st.sb("xres", [128, TOKENS])
        w.xh = st.sb("xh", [128, TOKENS], F32R)
        w.xl = st.sb("xl", [128, TOKENS], F32R)
        w.consts = st.sb("consts", [128, C_END])
        w.ident = w.consts[:, C_IDENT:C_HEAD]
        w.head = w.consts[:, C_HEAD:C_END]
        w.ident16 = st.sb("ident16", [128, 128], F16)
        w.neg_ident = st.sb("neg_ident", [128, 128], F32R)
        w.neg_half = st.sb("neg_half", [128, 16])
        w.eps = st.sb("eps", [128, 16])
        w.scratch = st.sb("scratch", [128, 1])
        w.phi_loaded, w.we_loaded, w.be_loaded = (st.sem(n) for n in ("phi_loaded", "we_loaded", "be_loaded"))
        w.phi = st.sb("phi", [128, 16, 128])
        w.bias = st.sb("bias", [128, 16])
        with ExitStack() as first:
            sf = Store(nc, first, "first")
            w.x1T = sf.sb("x1T", [128, TOKENS])
            w.m, w.w2, w.b2 = sf.sb("m", [128, 128]), sf.sb("w2", [128, 128]), sf.sb("b2", [128, 128])
            w.cvec, w.avec, w.beta = sf.sb("cvec", [128, 1]), sf.sb("avec", [128, 1]), sf.sb("beta", [128, 1])
            w.xq, w.xqs, w.xo = sf.sb("xq", [128, 128]), sf.sb("xqs", [128, 128]), sf.sb("xo", [128, 128])
            w.xk, w.xv = sf.sb("xk", [CD, 128]), sf.sb("xv", [CD, 128])
            w.fill = sf.sb("fill", [128, B * JP], BF16)
            w.ones16 = sf.sb("ones16", [128, 128], BF16)
            setup(nc, io, w)
            attention(nc, io, w)
            attend_context(nc, io, w)
        w.yk = st.sb("yk", [128, 16, 128])
        w.w2h, w.w2l = st.sb("w2h", [128, NP], F32R), st.sb("w2l", [128, NP], F32R)
        with ExitStack() as banks:
            sl = Store(nc, banks, "slots")
            psX = sl.ps("X", [128, 4, 512])
            w.we = sl.sb("we", [128, EXPERTS, 128])
            w.beT = sl.sb("beT", [128, EXPERTS])
            with ExitStack() as second:
                ss = Store(nc, second, "second")
                w.w1h, w.w1l = ss.sb("w1h", [128, NP], F32R), ss.sb("w1l", [128, NP], F32R)
                prepare_slots(nc, w)
                gather_slots(nc, io, w, psX)
            run_experts(nc, w, psX)
        mix_slots(nc, w, out)


def kernel(**inputs):
    import concourse.bacc as bacc
    from concourse.bass_utils import run_bass_kernel_spmd

    get = lambda name: np.asarray(inputs[name])
    x = get("x").reshape(TOKENS, D)
    context = np.zeros((B, JP, CD), np.float32)
    context[:, :J] = get("ctx_768")
    host = {
        "x": x, "xT": x.T, "ctxT": context.reshape(B * JP, CD).T, "mask": get("mask_BxS2_bf1").reshape(1, B * J),
        "w_qkvT": get("L0_attn_W_qkv").T, "b_qkv": get("L0_attn_b_qkv").reshape(3, D).T,
        "w_proj": get("L0_attn_W_proj"), "b_proj": get("L0_attn_b_proj").reshape(1, D),
        "xq": get("L0_xattn_Wq"), "xk": get("L0_xattn_Wk"), "xv": get("L0_xattn_Wv"), "xo": get("L0_xattn_Wo"),
        "phi": get("L0_ffn_phi_w"), "phi_b": get("L0_ffn_phi_b").reshape(16, 128).T,
        "expert_w": get("L0_ffn_expert_w"), "expert_bT": get("L0_ffn_expert_b").T,
        "consts": constants(),
    }
    nc = bacc.Bacc("TRN2", target_bir_lowering=False, num_devices=1)
    arrays, io = {}, {}
    for name, a in host.items():
        a = np.ascontiguousarray(a)
        arrays[f"in_{name}"] = a
        io[name] = nc.dram_tensor(f"in_{name}", a.shape, mybir.dt.from_np(a.dtype), kind="ExternalInput").ap()
    out = nc.dram_tensor("out_0", (TOKENS, D), F32, kind="ExternalOutput").ap()
    decoder_block(nc, io, out)
    result = run_bass_kernel_spmd(nc, [arrays], core_ids=[0])
    return result.results[0]["out_0"].reshape(B, S, D)
```

```python
from contextlib import ExitStack

import numpy as np

import concourse.bass as bass
from concourse import mybir

ALU = mybir.AluOpType
ACT = mybir.ActivationFunctionType
X = mybir.AxisListType.X
F32 = mybir.dt.float32
F32R = mybir.dt.float32r
F16 = mybir.dt.float16
BF16 = mybir.dt.bfloat16
U8 = mybir.dt.uint8

B, S, D = 64, 128, 128
TOKENS = B * S
J, JP, CD = 77, 78, 96
HEADS, HD = 16, 8
SCALE = float(HD) ** -0.5
EXPERTS, SLOTS = 64, 32
NP = EXPERTS * SLOTS
EPS = 1e-5
FILL = float(np.uint32(0x7F7F0000).view(np.float32))

T_01, T_025, T_085, T_095 = (float(np.float32(np.log(p / (1 - p)))) for p in (0.1, 0.25, 0.85, 0.95))

ROWS = range(0, 128, 32)

C_IDENT, C_HEAD, C_END = 0, 128, 132


def constants():
    k = np.arange(128)
    c = np.zeros((128, C_END), np.float32)
    c[:, C_IDENT:C_HEAD] = np.eye(128)
    c[:, C_HEAD:C_END] = (k[:, None] % 32) // HD == np.arange(4)[None, :]
    return c


class Item:

    def __init__(self, i, c):
        self.known = isinstance(i, int)
        self.par = c % 2
        self.half = i + c // 2
        self.n = i * 2 + c

    def __sub__(self, s):
        return Item(self.half, self.par - s)

    def __add__(self, s):
        return Item(self.half, self.par + s)

    def within(self, n):
        return not self.known or 0 <= self.n < n

    def after(self, per, c):
        return self.n * per + c

    def turn(self, per, c):
        return self.half * per + c


def steps(eng, n, lag, step, ahead=0, unroll=4):
    lo = (lag + 3) // 2
    hi = lo + (n - ahead - 2 * lo) // unroll * (unroll // 2)
    for k in range(2 * lo):
        step(Item(k // 2, k % 2))
    with eng.Fori(0, (hi - lo) // (unroll // 2)) as i:
        for c in range(unroll):
            step(Item(i * (unroll // 2) + lo, c))
    for k in range(2 * hi, n + lag):
        step(Item(k // 2, k % 2))


def reach(eng, sem, value):
    if not isinstance(value, int) or value > 0:
        eng.wait_ge(sem, value)


class Store:

    def __init__(self, nc, ctx, stage):
        self.nc, self.ctx, self.stage = nc, ctx, stage

    def sb(self, name, shape, dt=F32):
        return self.ctx.enter_context(self.nc.sbuf_tensor(f"{self.stage}_{name}", shape, dt))

    def ps(self, name, shape, dt=F32):
        return self.ctx.enter_context(self.nc.psum_tensor(f"{self.stage}_{name}", shape, dt))

    def sem(self, name):
        return self.ctx.enter_context(self.nc.semaphore(f"{self.stage}_{name}"))


def setup(nc, io, w):
    with ExitStack() as ctx:
        st = Store(nc, ctx, "setup")
        wT = st.sb("wT", [128, 3, 128])
        wproj = st.sb("wproj", [128, 128])
        bqkv = st.sb("bqkv", [128, 3])
        bproj = st.sb("bproj", [1, 128])
        brep = st.sb("brep", [128, 2, 128])
        ones = st.sb("ones", [128, 128])
        warm = st.sb("warm", [128, 1])
        pa = st.ps("pa", [128, 512])
        pb = st.ps("pb", [128, 512])
        loaded, cross_loaded, mask_clear, rep, folded = (
            st.sem(n) for n in ("loaded", "cross_loaded", "mask_clear", "rep", "folded"))
        block = ctx.enter_context(nc.Block())
        loads = [(wT, io["w_qkvT"].rearrange("(c e) d -> e c d", c=3)), (wproj, io["w_proj"]), (bqkv, io["b_qkv"]),
                 (bproj, io["b_proj"]), (w.consts, io["consts"])]
        cross_loads = [(w.xq, io["xq"]), (w.xk, io["xk"]), (w.xv, io["xv"]), (w.xo, io["xo"])]

        @block.sync
        def _(sync):
            for dst, src in loads:
                sync.dma_start(dst[:], src).then_inc(loaded, 16)
            sync.wait_ge(mask_clear, 1)
            for p in ROWS:
                sync.dma_start(w.mask[p:p + 1, :], io["mask"]).then_inc(w.mask_loaded, 16)

        @block.scalar
        def _(act):
            for dst, src in cross_loads:
                act.dma_start(dst[:], src).then_inc(cross_loaded, 16)
            act.wait_ge(rep, 1)
            act.activation(warm[:], ones[:, 0:1], ACT.Exp)

        @block.vector
        def _(dve):
            dve.memset(ones[:], 1.0).then_inc(rep, 1)
            dve.memset(w.mask[:].bitcast(mybir.dt.uint32), 0).then_inc(mask_clear, 1)
            dve.memset(w.neg_half[:], -0.5)
            dve.memset(w.eps[:], EPS)
            dve.memset(w.ones16[:], 1.0)
            dve.wait_ge(loaded, 16 * len(loads))
            dve.wait_ge(rep, 1)
            for n, c in enumerate((0, 2)):
                dve.tensor_scalar(brep[:, n, :], ones[:], bqkv[:, c:c + 1], None, ALU.mult).then_inc(rep, 1)
            dve.tensor_copy(w.ident16[:], w.ident)
            dve.tensor_scalar(w.neg_ident[:], w.ident, -1.0, None, ALU.mult)
            dve.wait_ge(cross_loaded, 16 * len(cross_loads))
            dve.tensor_scalar(w.xqs[:], w.xq[:], SCALE, None, ALU.mult)
            dve.wait_ge(folded, 1)
            dve.tensor_copy(w.m[:], pa[:, 0:128])
            dve.tensor_copy(w.w2[:], pa[:, 128:256])
            dve.tensor_copy(w.cvec[:], pb[:, 0:1])
            dve.tensor_copy(w.avec[:], pb[:, 1:2])
            dve.tensor_copy(w.beta[:], pb[:, 2:3])
            dve.tensor_copy(w.b2[:], pb[:, 128:256])

        @block.tensor
        def _(pe):
            pe.wait_ge(loaded, 16 * len(loads))
            pe.wait_ge(rep, 3)
            pe.matmul(pa[:, 0:128], wT[:, 0, :], wT[:, 1, :], start=True, stop=True)
            pe.matmul(pa[:, 128:256], wT[:, 2, :], wproj[:], start=True, stop=True)
            pe.matmul(pb[:, 0:1], wT[:, 1, :], bqkv[:, 0:1], start=True, stop=True)
            pe.matmul(pb[:, 1:2], wT[:, 0, :], bqkv[:, 1:2], start=True, stop=True)
            pe.matmul(pb[:, 2:3], brep[:, 0, :], bqkv[:, 1:2], start=True, stop=True)
            pe.matmul(pb[:, 128:256], brep[:, 1, :], wproj[:], start=True, stop=False)
            pe.matmul(pb[:, 128:256], ones[0:1, :], bproj[:], start=False, stop=True).then_inc(folded, 1)


def attention(nc, io, w):
    GB = 4
    GROUPS = B // GB
    x_in = io["x"].rearrange("(q b s) d -> q s b d", q=4, s=S)
    with ExitStack() as ctx:
        st = Store(nc, ctx, "attn")
        xTg = [st.sb(f"xTg{i}", [128, GB * 128]) for i in range(2)]
        uT = st.sb("uT", [128, 512])
        vp = [st.sb(f"vp{i}", [128, 512]) for i in range(2)]
        rb = st.sb("rb", [128, GB])
        a = [st.sb(f"a{i}", [128, 512]) for i in range(2)]
        band = [st.sb(f"band{i}", [128, 512]) for i in range(6)]
        f2 = [st.sb(f"f2{i}", [128, 512]) for i in range(2)]
        mx = st.sb("mx", [128, GB])
        nb = [st.sb(f"nb{i}", [128, GB]) for i in range(2)]
        pr = [st.sb(f"pr{i}", [128, 512]) for i in range(2)]
        sums = [st.sb(f"sums{i}", [128, GB]) for i in range(2)]
        pT = [st.sb(f"pT{i}", [128, 512]) for i in range(2)]
        rinv = st.sb("rinv", [128, GB])
        y = [st.sb(f"y{i}", [128, GB, 128]) for i in range(2)]
        stats = st.sb("stats", [128, GB, 6])
        mv = [st.sb(f"mv{i}", [128, GB, 2]) for i in range(2)]
        veps = st.sb("veps", [128, GB])
        rstd = [st.sb(f"rstd{i}", [128, GB]) for i in range(2)]
        x1 = [st.sb(f"x1{i}", [128, GB * 128]) for i in range(2)]
        psU, psV, psR, psS, psT, psO, psX = (st.ps(n, [128, 512]) for n in ("U", "V", "R", "S", "T", "O", "X"))
        xT_loaded = [st.sem("xT_loaded0"), st.sem("xT_loaded1")]
        x_loaded = [st.sem(f"x_loaded{q}") for q in range(4)]
        (u_made, v_made, s_made, uT_ready, v_ready, rb_ready, a_ready, f_ready, p_ready, pT_made, pT_ready,
         o_made, mv_ready, rstd_ready, x1_ready, x1T_made, x1T_kept, x1_kept, low_ready, band_done, f2_done,
         mx_done, y_chain, pool_chain) = (
            st.sem(n) for n in ("u_made", "v_made", "s_made", "uT_ready", "v_ready", "rb_ready", "a_ready",
                                "f_ready", "p_ready", "pT_made", "pT_ready", "o_made", "mv_ready",
                                "rstd_ready", "x1_ready", "x1T_made", "x1T_kept", "x1_kept", "low_ready",
                                "band_done", "f2_done", "mx_done", "y_chain", "pool_chain"))
        block = ctx.enter_context(nc.Block())

        @block.gpsimd
        def _(pool):
            for q in range(4):
                pool.dma_start(w.xres[:, q * 2048:(q + 1) * 2048].rearrange("s (b d) -> s b d", d=D), x_in[q])\
                    .then_inc(x_loaded[q], 16)

            def step(k):
                g = k - 1
                if g.within(GROUPS):
                    pool.wait_ge(band_done, g.after(3, 1))
                    pool.tensor_tensor(band[4][:], band[1][:], band[2][:], ALU.add).then_inc(low_ready, 1)
                g = k - 3
                if g.within(GROUPS):
                    pool.wait_ge(x1_ready, g.after(1, 1))
                    pool.tensor_copy(w.xres[:, bass.ds(g.n * 512, 512)], x1[g.par][:]).then_inc(x1_kept, 1)
                g = k - 2
                if g.within(GROUPS):
                    pool.wait_ge(mv_ready, g.after(1, 1))
                    pool.tensor_tensor(veps[:], mv[g.par][:, :, 1], w.eps[:, 0:GB], ALU.add).then_inc(pool_chain, 1)
                    pool.wait_ge(pool_chain, g.after(1, 1))
                    pool.tensor_tensor(rstd[g.par][:], veps[:], w.neg_half[:, 0:GB], ALU.pow).then_inc(rstd_ready, 1)
            steps(pool, GROUPS, 3, step)

        @block.sync
        def _(sync):
            def step(g):
                if not g.within(GROUPS):
                    return
                reach(sync, s_made, g.after(1, -1))
                sync.dma_start(xTg[g.par][:], io["xT"][:, bass.ds(g.n * 512, 512)]).then_inc(xT_loaded[g.par], 16)
            steps(sync, GROUPS, 0, step)

        @block.tensor
        def _(pe):
            def step(k):
                g = k
                if g.within(GROUPS):
                    pe.wait_ge(xT_loaded[g.par], g.turn(16, 16))
                    reach(pe, uT_ready, g.after(1, 0))
                    pe.matmul(psU[:], w.m[:], xTg[g.par][:], start=True, stop=True).then_inc(u_made, 1)
                    reach(pe, v_ready, g.after(1, 0))
                    reach(pe, rb_ready, g.after(1, 0))
                    for b in range(GB):
                        xb = xTg[g.par][:, b * 128:(b + 1) * 128]
                        pe.matmul(psV[:, b * 128:(b + 1) * 128], xb, w.w2[:], start=True, stop=True)
                        ins = pe.matmul(psR[:, b:b + 1], xb, w.avec[:], start=True, stop=True)
                    ins.then_inc(v_made, 1)
                g = k - 2
                if g.within(GROUPS):
                    pe.wait_ge(p_ready, g.after(1, 1))
                    reach(pe, pT_ready, g.after(1, 0))
                    for b in range(GB):
                        c = slice(b * 128, (b + 1) * 128)
                        ins = pe.transpose(psT[:, c], pr[g.par][:, c], w.ident)
                    ins.then_inc(pT_made, 1)
                    pe.wait_ge(pT_ready, g.after(1, 1))
                    reach(pe, mv_ready, g.after(1, 0))
                    for b in range(GB):
                        c = slice(b * 128, (b + 1) * 128)
                        ins = pe.matmul(psO[:, c], pT[g.par][:, c], vp[g.par][:, c], start=True, stop=True)
                    ins.then_inc(o_made, 1)
                g = k
                if g.within(GROUPS):
                    pe.wait_ge(uT_ready, g.after(1, 1))
                    reach(pe, a_ready, g.after(1, 0))
                    for b in range(GB):
                        c = slice(b * 128, (b + 1) * 128)
                        ins = pe.matmul(psS[:, c], uT[:, c], xTg[g.par][:, c], start=True, stop=True)
                    ins.then_inc(s_made, 1)
                g = k - 3
                if g.within(GROUPS):
                    pe.wait_ge(x1_ready, g.after(1, 1))
                    reach(pe, x1T_kept, g.after(1, 0))
                    for b in range(GB):
                        c = slice(b * 128, (b + 1) * 128)
                        ins = pe.transpose(psX[:, c], x1[g.par][:, c], w.ident)
                    ins.then_inc(x1T_made, 1)
            steps(pe, GROUPS, 3, step)

        @block.scalar
        def _(act):
            def step(k):
                g = k
                if g.within(GROUPS):
                    act.wait_ge(u_made, g.after(1, 1))
                    reach(act, s_made, g.after(1, 0))
                    act.activation(uT[:], psU[:], ACT.Identity, bias=w.cvec[:]).then_inc(uT_ready, 1)
                g = k - 2
                if g.within(GROUPS):
                    act.wait_ge(pT_made, g.after(1, 1))
                    reach(act, o_made, g.after(1, -1))
                    act.copy(pT[g.par][:], psT[:]).then_inc(pT_ready, 1)
                g = k
                if g.within(GROUPS):
                    act.wait_ge(rb_ready, g.after(1, 1))
                    act.wait_ge(s_made, g.after(1, 1))
                    reach(act, f_ready, g.after(1, -1))
                    for b in range(GB):
                        c = slice(b * 128, (b + 1) * 128)
                        ins = act.activation(a[g.par][:, c], psS[:, c], ACT.Identity, bias=rb[:, b:b + 1],
                                             scale=SCALE)
                    ins.then_inc(a_ready, 1)
                g = k - 1
                if g.within(GROUPS):
                    act.wait_ge(f_ready, g.after(1, 1))
                    reach(act, pT_made, g.after(1, -1))
                    reach(act, mv_ready, g.after(1, -1))
                    for b in range(GB):
                        c = slice(b * 128, (b + 1) * 128)
                        ins = act.activation(pr[g.par][:, c], f2[g.par][:, c], ACT.Exp, bias=nb[g.par][:, b:b + 1],
                                             scale=0.5, accum_out=sums[g.par][:, b:b + 1])
                    ins.then_inc(p_ready, 1)
                g = k - 3
                if g.within(GROUPS):
                    act.wait_ge(x1T_made, g.after(1, 1))
                    act.copy(w.x1T[:, bass.ds(g.n * 512, 512)], psX[:]).then_inc(x1T_kept, 1)
            steps(act, GROUPS, 3, step)

        @block.vector
        def _(dve):
            dve.wait_ge(w.mask_loaded, 16 * len(ROWS))
            dve.memset(w.fill[:].rearrange("a (b t) -> a b t", t=JP)[:, :, J], -FILL)
            dve.tensor_scalar(w.fill[:].rearrange("a (b t) -> a b t", t=JP)[:, :, 0:J],
                              w.mask[:].rearrange("a (b t) -> a b t", t=J), 1.0, FILL, ALU.subtract, ALU.mult)

            def step(k):
                g = k - 1
                if g.within(GROUPS):
                    dve.wait_ge(a_ready, g.after(1, 1))
                    reach(dve, f_ready, g.after(1, 0))
                    av = a[g.par][:]
                    dve.tensor_scalar(band[0][:], av, T_095, 2.0, ALU.is_gt, ALU.add)
                    dve.tensor_scalar(band[1][:], av, T_025, -1.4, ALU.is_lt, ALU.mult)
                    dve.tensor_scalar(band[2][:], av, T_01, -0.4, ALU.is_lt, ALU.mult).then_inc(band_done, 1)
                g = k - 3
                if g.within(GROUPS):
                    dve.wait_ge(rstd_ready, g.after(1, 1))
                    reach(dve, x1T_kept, g.after(1, -1))
                    reach(dve, x1_kept, g.after(1, -1))
                    for b in range(GB):
                        ins = dve.tensor_scalar(x1[g.par][:, b * 128:(b + 1) * 128], y[g.par][:, b, :],
                                                mv[g.par][:, b, 0:1], rstd[g.par][:, b:b + 1],
                                                ALU.subtract, ALU.mult)
                    ins.then_inc(x1_ready, 1)
                g = k - 1
                if g.within(GROUPS):
                    dve.wait_ge(band_done, g.after(3, 1))
                    dve.scalar_tensor_tensor(out=band[3][:], in0=av, scalar=T_085, in1=band[0][:],
                                             op0=ALU.is_gt, op1=ALU.add).then_inc(band_done, 1)
                g = k
                if g.within(GROUPS):
                    dve.wait_ge(v_made, g.after(1, 1))
                    reach(dve, a_ready, g.after(1, 0))
                    dve.tensor_scalar(rb[:], psR[:, 0:GB], w.beta[:], SCALE, ALU.add, ALU.mult).then_inc(rb_ready, 1)
                g = k - 1
                if g.within(GROUPS):
                    dve.wait_ge(band_done, g.after(3, 2))
                    dve.wait_ge(low_ready, g.after(1, 1))
                    dve.tensor_tensor(band[5][:], band[4][:], band[3][:], ALU.add).then_inc(band_done, 1)
                    dve.wait_ge(band_done, g.after(3, 3))
                    reach(dve, p_ready, g.after(1, -1))
                    dve.tensor_tensor(f2[g.par][:], band[5][:], av, ALU.mult).then_inc(f2_done, 1)
                    dve.wait_ge(f2_done, g.after(1, 1))
                    dve.tensor_reduce(mx[:], f2[g.par][:].rearrange("p (b t) -> p b t", b=GB), X, ALU.max)\
                       .then_inc(mx_done, 1)
                g = k - 2
                if g.within(GROUPS):
                    dve.wait_ge(p_ready, g.after(1, 1))
                    reach(dve, mv_ready, g.after(1, 0))
                    dve.reciprocal(rinv[:], sums[g.par][:]).then_inc(y_chain, 1)
                g = k - 1
                if g.within(GROUPS):
                    dve.wait_ge(mx_done, g.after(1, 1))
                    dve.tensor_scalar(nb[g.par][:], mx[:], -0.5, None, ALU.mult).then_inc(f_ready, 1)
                g = k
                if g.within(GROUPS):
                    reach(dve, o_made, g.after(1, -1))
                    dve.tensor_tensor(vp[g.par][:].rearrange("p (b e) -> p b e", b=GB),
                                      psV[:].rearrange("p (b e) -> p b e", b=GB),
                                      w.b2[:].unsqueeze(1).to_broadcast([128, GB, 128]), ALU.add).then_inc(v_ready, 1)
                g = k - 2
                if g.within(GROUPS):
                    if g.known and g.n == 0:
                        for q in range(4):
                            dve.wait_ge(x_loaded[q], 16)
                    dve.wait_ge(o_made, g.after(1, 1))
                    dve.wait_ge(y_chain, g.after(3, 1))
                    reach(dve, x1_ready, g.after(1, -1))
                    for b in range(GB):
                        c = slice(b * 128, (b + 1) * 128)
                        ins = dve.scalar_tensor_tensor(out=y[g.par][:, b, :], in0=psO[:, c], scalar=rinv[:, b:b + 1],
                                                       in1=w.xres[:, bass.ds(g.n * 512 + b * 128, 128)],
                                                       op0=ALU.mult, op1=ALU.add)
                    ins.then_inc(y_chain, 1)
                    dve.wait_ge(y_chain, g.after(3, 2))
                    for b in range(GB):
                        ins = dve.bn_stats(stats[:, b, :], y[g.par][:, b, :])
                    ins.then_inc(y_chain, 1)
                    dve.wait_ge(y_chain, g.after(3, 3))
                    dve.memset(w.scratch[:], 0.0)
                    for b in range(GB):
                        ins = dve.bn_aggr(mv[g.par][:, b, :], stats[:, b, :])
                    ins.then_inc(mv_ready, 1)
            steps(dve, GROUPS, 3, step)


def attend_context(nc, io, w):
    PAIRS = B // 2
    HW = 4 * JP
    with ExitStack() as ctx:
        st = Store(nc, ctx, "cross")
        cg = [st.sb(f"cg{i}", [CD, 2 * JP]) for i in range(2)]
        qkh = [st.sb(f"qkh{i}", [128, 256 + 2 * JP], F32R) for i in range(2)]
        qkl = [st.sb(f"qkl{i}", [128, 256 + 2 * JP], F32R) for i in range(2)]
        fp = [st.sb(f"fp{i}", [128, 2, JP], BF16) for i in range(2)]
        kbh = [st.sb(f"kbh{i}", [128, 2, 4, JP], F32R) for i in range(2)]
        kbl = [st.sb(f"kbl{i}", [128, 2, 4, JP], F32R) for i in range(2)]
        v32 = st.sb("v32", [J, 256])
        vr = [st.sb(f"vr{i}", [J, 256]) for i in range(2)]
        vs = [st.sb(f"vs{i}", [J, 2, HEADS, 3, 9], BF16) for i in range(2)]
        mx = [st.sb(f"mx{i}", [128, 2, 4], F32R) for i in range(2)]
        p32 = [st.sb(f"p32{i}", [128, 2, HW]) for i in range(2)]
        ph = [st.sb(f"ph{i}", [128, 2, HW], F16) for i in range(2)]
        pl = [st.sb(f"pl{i}", [128, 2, HW], F16) for i in range(2)]
        pTh = [st.sb(f"pTh{i}", [J, 8, 128], F16) for i in range(2)]
        pTl = [st.sb(f"pTl{i}", [J, 8, 128], F16) for i in range(2)]
        o9 = st.sb("o9", [128, HEADS, 9])
        orec = st.sb("orec", [128, HEADS])
        on = st.sb("on", [128, 128])
        oT = st.sb("oT", [128, 128])
        y = [st.sb(f"y{i}", [128, 128]) for i in range(2)]
        stats = st.sb("stats", [128, 6])
        mv = [st.sb(f"mv{i}", [128, 2]) for i in range(2)]
        veps = st.sb("veps", [128, 1])
        rstd = [st.sb(f"rstd{i}", [128, 1]) for i in range(2)]
        xp = [st.sb(f"xp{i}", [128, 128]) for i in range(2)]
        psL = [st.ps(f"L{i}", [128, 2, 512]) for i in range(2)]
        psTh = st.ps("Th", [J, 8, 128], F16)
        psTl = st.ps("Tl", [J, 8, 128], F16)
        psA = st.ps("A", [128, 512])
        psM = st.ps("M", [128, 512])
        QUERY, KEY, BOTH = slice(0, 256), slice(256, 256 + 2 * JP), slice(0, 256 + 2 * JP)
        c_loaded = [st.sem("c_loaded0"), st.sem("c_loaded1")]
        (qk_made, qkh_ready, qkl_ready, kbh_ready, kbl_ready, v_made, v32_ready, high_ready, rest_ready, mid_ready,
         last_ready, vs_ready) = (
            st.sem(n) for n in ("qk_made", "qkh_ready", "qkl_ready", "kbh_ready", "kbl_ready", "v_made", "v32_ready",
                                "high_ready", "rest_ready", "mid_ready", "last_ready", "vs_ready"))
        s_made, mx_ready, shifted, ph_ready, p32_ready, pl_ready, t_made, pTh_ready, pTl_ready, av_made = (
            st.sem(n) for n in ("s_made", "mx_ready", "shifted", "ph_ready", "p32_ready", "pl_ready", "t_made",
                                "pTh_ready", "pTl_ready", "av_made"))
        (o_sum, o_rec, on_ready, oT_made, oT_ready, pj_made, y_done, st_done, mv_ready, ve_done, rstd_ready,
         x2_ready, xT_made, xh_ready, xl_ready) = (
            st.sem(n) for n in ("o_sum", "o_rec", "on_ready", "oT_made", "oT_ready", "pj_made", "y_done", "st_done",
                                "mv_ready", "ve_done", "rstd_ready", "x2_ready", "xT_made", "xh_ready", "xl_ready"))
        consts_set, fp_ready = st.sem("consts_set"), st.sem("fp_ready")
        block = ctx.enter_context(nc.Block())

        def earlier(r, j, s):
            return (r, j - s) if j >= s else (r - 1, j - s + 4)

        def part(r, c):
            return vs[r.par][:, :, :, c, 0:8]

        def as_heads(t):
            return t[:].rearrange("j (b h e) -> j b h e", b=2, h=HEADS)

        @block.sync
        def _(sync):
            sync.dma_start(w.phi[:], io["phi"].rearrange("(c r) d -> r c d", r=128)).then_inc(w.phi_loaded, 16)
            sync.dma_start(w.bias[:], io["phi_b"]).then_inc(w.phi_loaded, 16)

            def step(r):
                if r.within(PAIRS):
                    reach(sync, v_made, r.after(1, -1))
                    sync.dma_start(cg[r.par][:], io["ctxT"][:, bass.ds(r.n * 2 * JP, 2 * JP)])\
                        .then_inc(c_loaded[r.par], 16)
            steps(sync, PAIRS, 0, step)

        @block.tensor
        def _(pe):
            pe.wait_ge(consts_set, 1)

            def queries_keys(r, _):
                pe.wait_ge(c_loaded[r.par], r.turn(16, 16))
                pe.matmul(psM[:, QUERY], w.xqs[:], w.x1T[:, bass.ds(r.n * 256, 256)], start=True, stop=True)
                pe.matmul(psM[:, KEY], w.xk[:], cg[r.par][:], start=True, stop=True).then_inc(qk_made, 1)

            def own_values(r, _):
                for b in range(2):
                    ins = pe.matmul(psM[0:J, b * 128:(b + 1) * 128], cg[r.par][:, b * JP:b * JP + J], w.xv[:],
                                    start=True, stop=True)
                ins.then_inc(v_made, 1)

            def turn_out(r, b):
                pe.wait_ge(on_ready, r.after(2, b + 1))
                pe.transpose(psM[:, 0:128], on[:], w.ident).then_inc(oT_made, 1)

            def project(r, b):
                pe.wait_ge(oT_ready, r.after(2, b + 1))
                pe.matmul(psM[:, 0:128], oT[:], w.xo[:], start=True, stop=True).then_inc(pj_made, 1)

            def turn_x2(r, b):
                pe.wait_ge(x2_ready, r.after(2, b + 1))
                pe.transpose(psM[:, 0:128], xp[b][:], w.ident).then_inc(xT_made, 1)

            USES = [(queries_keys, qkl_ready, 0, None), (project, y_done, 3, 1), (own_values, v32_ready, 0, None),
                    (turn_out, oT_ready, 2, 0), (project, y_done, 2, 0), (turn_x2, xl_ready, 3, 1),
                    (turn_x2, xl_ready, 2, 0), (turn_out, oT_ready, 2, 1)]

            def use_bank(k, n):
                make, _, lag, b = USES[n]
                if not (k - lag).within(PAIRS):
                    return
                for back in range(1, 17):
                    m = n - back
                    _, read, lag_m, b_m = USES[m % 8]
                    r = k - lag_m + m // 8
                    if r.within(PAIRS):
                        pe.wait_ge(read, r.after(1, 1) if b_m is None else r.after(2, b_m + 1))
                        break
                make(k - lag, b)

            def scores(r, j):
                if j == 0:
                    pe.wait_ge(fp_ready, r.after(1, 1))
                    pe.wait_ge(kbh_ready, r.after(1, 1))
                    pe.wait_ge(kbl_ready, r.after(1, 1))
                reach(pe, p32_ready, r.after(4, j - 1))
                b, bc = j // 2, slice(j // 2 * 128, j // 2 * 128 + 128)
                for i in range(2):
                    g = 32 * (2 * (j % 2) + i)
                    gr = slice(g, g + 32)
                    out = psL[j % 2][:, i, 0:HW]
                    kh_, kl_ = kbh[r.par][gr, b, :, :], kbl[r.par][gr, b, :, :]
                    pe.matmul(out, qkh[r.par][gr, bc], kh_, start=True, stop=False)
                    pe.matmul(out, qkl[r.par][gr, bc], kh_, start=False, stop=False)
                    pe.matmul(out, qkh[r.par][gr, bc], kl_, start=False, stop=False)
                    fill = fp[r.par][g:g + 1, b, :].unsqueeze(1).to_broadcast([1, 4, JP])
                    ins = pe.matmul(out, w.ones16[g:g + 1, :], fill, start=False, stop=True)
                ins.then_inc(s_made, 1)

            def shift(r, j):
                pe.wait_ge(mx_ready, r.after(4, j + 1))
                for i in range(2):
                    ins = pe.matmul(psL[j % 2][:, i, 0:HW], w.neg_ident[:],
                                    mx[j % 2][:, i, :].unsqueeze(2).to_broadcast([128, 4, JP]),
                                    start=False, stop=True, skip_group_check=True)
                ins.then_inc(shifted, 1)

            def turn(r, j):
                pe.wait_ge(ph_ready, r.after(4, j + 1))
                pe.wait_ge(pl_ready, r.after(4, j + 1))
                reach(pe, pTh_ready, r.after(4, j))
                reach(pe, pTl_ready, r.after(4, j))
                for h in range(8):
                    c = slice(h % 4 * JP, h % 4 * JP + J)
                    pe.transpose(psTh[:, h, :], ph[j % 2][:, h // 4, c], w.ident16[:])
                    ins = pe.transpose(psTl[:, h, :], pl[j % 2][:, h // 4, c], w.ident16[:])
                ins.then_inc(t_made, 1)

            def values(r, j):
                if j == 0:
                    pe.wait_ge(vs_ready, r.after(1, 1))
                if j % 2 == 0:
                    reach(pe, o_sum, r.after(2, j // 2))
                pe.wait_ge(pTh_ready, r.after(4, j + 1))
                pe.wait_ge(pTl_ready, r.after(4, j + 1))
                for h in range(8):
                    head = 8 * (j % 2) + h
                    v = vs[r.par][:, j // 2, head, :, :]
                    pe.matmul(psA[:, head * 27:head * 27 + 27], pTh[j % 2][:, h, :], v, start=True, stop=True)
                    ins = pe.matmul(psA[:, head * 27:head * 27 + 18], pTl[j % 2][:, h, :], v[:, 0:2, :],
                                    start=False, stop=True, skip_group_check=True)
                ins.then_inc(av_made, 1)

            def step(k):
                r = k - 1
                for j in range(4):
                    if r.within(PAIRS):
                        scores(r, j)
                    if j < 2:
                        use_bank(k, 2 * j)
                    r3, j3 = earlier(r, j, 3)
                    if r3.within(PAIRS):
                        values(r3, j3)
                    if j >= 2:
                        use_bank(k, 2 * j)
                    r2, j2 = earlier(r, j, 2)
                    if r2.within(PAIRS):
                        turn(r2, j2)
                    if r.within(PAIRS):
                        shift(r, j)
                    use_bank(k, 2 * j + 1)
            steps(pe, PAIRS, 3, step)

        @block.scalar
        def _(act):
            def keep_out(r, b):
                act.wait_ge(oT_made, r.after(2, b + 1))
                reach(act, pj_made, r.after(2, b))
                act.copy(oT[:], psM[:, 0:128]).then_inc(oT_ready, 1)

            def keep_high(r, b):
                act.wait_ge(xT_made, r.after(2, b + 1))
                act.copy(w.xh[:, bass.ds(r.n * 256 + b * 128, 128)], psM[:, 0:128]).then_inc(xh_ready, 1)

            def step(k):
                r = k - 1
                for j in range(4):
                    if j == 0 and k.within(PAIRS):
                        act.wait_ge(qk_made, k.after(1, 1))
                        reach(act, shifted, (k - 1).after(4, 0))
                        act.copy(qkh[k.par][:], psM[:, BOTH]).then_inc(qkh_ready, 1)
                    if j == 3 and k.within(PAIRS):
                        act.wait_ge(v32_ready, k.after(1, 1))
                        reach(act, av_made, (k - 1).after(4, 0))
                        act.copy(part(k, 0), as_heads(v32)).then_inc(high_ready, 1)
                    if j == 2 and k.within(PAIRS):
                        act.copy(fp[k.par][:], w.fill[:, bass.ds(k.n * 2 * JP, 2 * JP)]
                                 .rearrange("p (b t) -> p b t", b=2)).then_inc(fp_ready, 1)
                    if j == 1 and k.within(PAIRS):
                        act.wait_ge(v_made, k.after(1, 1))
                        reach(act, rest_ready, k.after(1, 0))
                        act.copy(v32[:], psM[0:J, 0:256]).then_inc(v32_ready, 1)
                    if j == 3 and (k - 2).within(PAIRS):
                        keep_high(k - 2, 0)
                    r2, j2 = earlier(r, j, 2)
                    if r2.within(PAIRS):
                        act.wait_ge(t_made, r2.after(4, j2 + 1))
                        reach(act, av_made, r2.after(4, j2 - 1))
                        act.copy(pTl[j % 2][:], psTl[:]).then_inc(pTl_ready, 1)
                    if j == 2 and (k - 3).within(PAIRS):
                        keep_high(k - 3, 1)
                    if j % 2 and (k - 2).within(PAIRS):
                        keep_out(k - 2, j // 2)
                    if r.within(PAIRS):
                        act.wait_ge(shifted, r.after(4, j + 1))
                        reach(act, t_made, r.after(4, j - 1))
                        reach(act, pl_ready, r.after(4, j - 1))
                        act.activation(ph[j % 2][:], psL[j % 2][:, :, 0:HW], ACT.Exp).then_inc(ph_ready, 1)
                        act.activation(p32[j % 2][:], psL[j % 2][:, :, 0:HW], ACT.Exp).then_inc(p32_ready, 1)
            steps(act, PAIRS, 3, step)

        @block.vector
        def _(dve):
            for i in range(2):
                dve.memset(xp[i][:, 127:128], 1.0)
                dve.memset(vs[i][:, :, :, 0, 8], 1.0)
                ins = dve.memset(vs[i][:, :, :, 1:3, 8], 0.0)
            ins.then_inc(consts_set, 1)
            dve.wait_ge(consts_set, 1)

            def sum_parts(r, b):
                dve.wait_ge(av_made, r.after(4, 2 * b + 2))
                reach(dve, on_ready, r.after(2, b))
                dve.tensor_reduce(o9[:], psA[:, 0:432].rearrange("p (h c e) -> p h e c", h=HEADS, c=3), X, ALU.add)\
                    .then_inc(o_sum, 1)

            def invert_sums(r, b):
                dve.wait_ge(o_sum, r.after(2, b + 1))
                reach(dve, on_ready, r.after(2, b))
                dve.reciprocal(orec[:], o9[:, :, 8]).then_inc(o_rec, 1)

            def divide(r, b):
                dve.wait_ge(o_rec, r.after(2, b + 1))
                reach(dve, oT_made, r.after(2, b))
                dve.tensor_tensor(on[:].rearrange("p (h e) -> p h e", h=HEADS), o9[:, :, 0:8],
                                  orec[:].unsqueeze(2).to_broadcast([128, HEADS, 8]), ALU.mult).then_inc(on_ready, 1)

            def add_residual(r, b):
                dve.wait_ge(pj_made, r.after(2, b + 1))
                dve.tensor_tensor(y[b][:], psM[:, 0:128], w.xres[:, bass.ds(r.n * 256 + b * 128, 128)], ALU.add)\
                    .then_inc(y_done, 1)

            def statistics(r, b):
                dve.wait_ge(y_done, r.after(2, b + 1))
                dve.bn_stats(stats[:], y[b][:]).then_inc(st_done, 1)

            def aggregate(r, b):
                dve.wait_ge(st_done, r.after(2, b + 1))
                dve.memset(w.scratch[:], 0.0)
                dve.bn_aggr(mv[b][:], stats[:]).then_inc(mv_ready, 1)

            def normalise(r, b):
                dve.wait_ge(rstd_ready, r.after(2, b + 1))
                reach(dve, xT_made, (r - 1).after(2, b + 1))
                dve.tensor_scalar(xp[b][:, 0:127], y[b][:, 0:127], mv[b][:, 0:1], rstd[b][:],
                                  ALU.subtract, ALU.mult).then_inc(x2_ready, 1)

            def keep_residual(r, b):
                dve.tensor_scalar(w.xres[:, bass.ds(r.n * 256 + b * 128, 128)], y[b][:], mv[b][:, 0:1], rstd[b][:],
                                  ALU.subtract, ALU.mult)

            def low_part(r, b):
                at = bass.ds(r.n * 256 + b * 128, 128)
                dve.wait_ge(xh_ready, r.after(2, b + 1))
                dve.tensor_tensor(w.xl[:, at], psM[:, 0:128], w.xh[:, at], ALU.subtract).then_inc(xl_ready, 1)

            def step(k):
                r = k - 1
                for j in range(4):
                    if r.within(PAIRS):
                        dve.wait_ge(s_made, r.after(4, j + 1))
                        reach(dve, shifted, r.after(4, j - 1))
                        dve.tensor_reduce(mx[j % 2][:], psL[j % 2][:, :, 0:HW].rearrange("p i (h t) -> p i h t", h=4),
                                          X, ALU.max).then_inc(mx_ready, 1)
                    if j == 0 and k.within(PAIRS):
                        dve.wait_ge(qkh_ready, k.after(1, 1))
                        dve.tensor_tensor(qkl[k.par][:], psM[:, BOTH], qkh[k.par][:], ALU.subtract).then_inc(qkl_ready, 1)
                    if j % 2 and (k - 2).within(PAIRS):
                        invert_sums(k - 2, j // 2)
                    if j == 1 and (k - 3).within(PAIRS):
                        statistics(k - 3, 1)
                    if j == 3 and (k - 2).within(PAIRS):
                        low_part(k - 2, 0)
                    if j % 2 and (k - 2).within(PAIRS):
                        divide(k - 2, j // 2)
                    if j == 1 and (k - 3).within(PAIRS):
                        aggregate(k - 3, 1)
                    if j == 2 and (k - 2).within(PAIRS):
                        add_residual(k - 2, 0)
                        statistics(k - 2, 0)
                        sum_parts(k - 2, 1)
                        aggregate(k - 2, 0)
                    r2, j2 = earlier(r, j, 2)
                    if r2.within(PAIRS):
                        dve.wait_ge(t_made, r2.after(4, j2 + 1))
                        reach(dve, av_made, r2.after(4, j2 - 1))
                        dve.tensor_copy(pTh[j % 2][:], psTh[:]).then_inc(pTh_ready, 1)
                    if j == 3 and (k - 2).within(PAIRS):
                        keep_residual(k - 2, 0)
                    if j == 2 and r.within(PAIRS):
                        dve.wait_ge(last_ready, r.after(1, 1))
                        dve.tensor_copy(part(r, 2), as_heads(vr[1])).then_inc(vs_ready, 1)
                    if j == 0 and (k - 2).within(PAIRS):
                        sum_parts(k - 2, 0)
                    if j == 0 and (k - 3).within(PAIRS):
                        add_residual(k - 3, 1)
                    if j == 0 and r.within(PAIRS):
                        dve.wait_ge(rest_ready, r.after(1, 1))
                        dve.tensor_copy(part(r, 1), as_heads(vr[0])).then_inc(mid_ready, 1)
                    if j == 1 and (k - 3).within(PAIRS):
                        normalise(k - 3, 1)
                        keep_residual(k - 3, 1)
                    if j == 2 and (k - 2).within(PAIRS):
                        normalise(k - 2, 0)
                    if j == 2 and (k - 3).within(PAIRS):
                        low_part(k - 3, 1)
            steps(dve, PAIRS, 3, step)

        @block.gpsimd
        def _(pool):
            def keep_own(dst, src, r):
                keys = src[r.par][:, KEY].rearrange("p (b t) -> p b t", b=2).unsqueeze(2).to_broadcast([128, 2, 4, JP])
                own = w.head.unsqueeze(1).unsqueeze(3).to_broadcast([128, 2, 4, JP])
                return pool.tensor_tensor(dst[r.par][:], keys, own, ALU.mult)

            def inverse_deviation(r, b):
                pool.wait_ge(mv_ready, r.after(2, b + 1))
                pool.tensor_tensor(veps[:], mv[b][:, 1:2], w.eps[:, 0:1], ALU.add).then_inc(ve_done, 1)
                pool.wait_ge(ve_done, r.after(2, b + 1))
                pool.tensor_tensor(rstd[b][:], veps[:], w.neg_half[:, 0:1], ALU.pow).then_inc(rstd_ready, 1)

            def step(k):
                r = k - 1
                for j in range(4):
                    if j == 0 and k.within(PAIRS):
                        pool.wait_ge(qkh_ready, k.after(1, 1))
                        keep_own(kbh, qkh, k).then_inc(kbh_ready, 1)
                    if j == 1 and (k - 3).within(PAIRS):
                        inverse_deviation(k - 3, 1)
                    if j == 1 and r.within(PAIRS):
                        pool.wait_ge(mid_ready, r.after(1, 1))
                        reach(pool, vs_ready, r.after(1, 0))
                        pool.tensor_tensor(as_heads(vr[1]), as_heads(vr[0]), part(r, 1), ALU.subtract)\
                            .then_inc(last_ready, 1)
                    if j == 3 and k.within(PAIRS):
                        pool.wait_ge(high_ready, k.after(1, 1))
                        reach(pool, last_ready, k.after(1, 0))
                        pool.tensor_tensor(as_heads(vr[0]), as_heads(v32), part(k, 0), ALU.subtract)\
                            .then_inc(rest_ready, 1)
                    if j == 2 and (k - 2).within(PAIRS):
                        inverse_deviation(k - 2, 0)
                    if j == 2 and k.within(PAIRS):
                        pool.wait_ge(qkl_ready, k.after(1, 1))
                        keep_own(kbl, qkl, k).then_inc(kbl_ready, 1)
                    if r.within(PAIRS):
                        pool.wait_ge(p32_ready, r.after(4, j + 1))
                        reach(pool, t_made, r.after(4, j - 1))
                        pool.tensor_tensor(pl[j % 2][:], p32[j % 2][:], ph[j % 2][:], ALU.subtract).then_inc(pl_ready, 1)
            steps(pool, PAIRS, 3, step)


def prepare_slots(nc, w):
    with ExitStack() as ctx:
        st = Store(nc, ctx, "prep")
        diff = st.sb("diff", [128, 16, 128])
        psW = st.ps("W", [128, NP])
        diff_done, w_made, wh_done = (st.sem(n) for n in ("diff_done", "w_made", "wh_done"))
        block = ctx.enter_context(nc.Block())

        def by_quarter(t, c):
            return t[:].rearrange("d (q c g p) -> d c g q p", q=4, c=4, g=16)[:, c]

        def by_expert(t, c):
            return t[:, c * 512:(c + 1) * 512].rearrange("d (g q p) -> d g q p", g=16, q=4)

        @block.vector
        def _(dve):
            dve.wait_ge(w.phi_loaded, 32)
            dve.tensor_copy(diff[:, :, 127], w.bias[:])
            for c in range(4):
                p = slice(4 * c, 4 * c + 4)
                dve.tensor_tensor(diff[:, p, 0:127], w.phi[:, p, 0:127], w.phi[:, p, 127:128].to_broadcast([128, 4, 127]),
                                  ALU.subtract).then_inc(diff_done, 1)
            for c in range(4):
                b = slice(c * 512, (c + 1) * 512)
                dve.wait_ge(wh_done, c + 1)
                dve.tensor_tensor(w.w1l[:, b], psW[:, b], w.w1h[:, b], ALU.subtract)
                dve.tensor_tensor(by_quarter(w.w2l, c), by_expert(psW, c), by_quarter(w.w2h, c), ALU.subtract)

        @block.tensor
        def _(pe):
            for c in range(16):
                pe.wait_ge(diff_done, c // 4 + 1)
                ins = pe.transpose(psW[:, c * 128:(c + 1) * 128], diff[:, c, :], w.ident)
                if c % 4 == 3:
                    ins.then_inc(w_made, 1)

        @block.scalar
        def _(act):
            for c in range(4):
                b = slice(c * 512, (c + 1) * 512)
                act.wait_ge(w_made, c + 1)
                act.copy(w.w1h[:, b], psW[:, b])
                act.copy(by_quarter(w.w2h, c), by_expert(psW, c)).then_inc(wh_done, 1)


def gather_slots(nc, io, w, psX):
    TILES = TOKENS // 128
    with ExitStack() as ctx:
        st = Store(nc, ctx, "gather")
        xh = [st.sb(f"xh{i}", [128, 128], F32R) for i in range(2)]
        xl = [st.sb(f"xl{i}", [128, 128], F32R) for i in range(2)]
        x2 = [st.sb(f"x2{i}", [128, 128]) for i in range(2)]
        mx = [st.sb(f"mx{i}", [128, 2, 16], F32R) for i in range(2)]
        e = [st.sb(f"e{i}", [128, 2, 16, 32]) for i in range(2)]
        rsum = [st.sb(f"rsum{i}", [128, 32]) for i in range(2)]
        rinv = [st.sb(f"rinv{i}", [128, 32]) for i in range(2)]
        dd = [[st.sb(f"d{i}{j}", [128, 2, 512]) for j in range(2)] for i in range(2)]
        x2h = [st.sb(f"x2h{i}", [128, 128], F32R) for i in range(2)]
        x2l = [st.sb(f"x2l{i}", [128, 128], F32R) for i in range(2)]
        dh = [st.sb(f"dh{i}", [128, 512], F32R) for i in range(2)]
        dl = [st.sb(f"dl{i}", [128, 512], F32R) for i in range(2)]
        psL = [st.ps(f"L{i}", [128, 2, 512]) for i in range(2)]
        x_ready, x2_ready, x2l_ready = st.sem("x_ready"), st.sem("x2_ready"), st.sem("x2l_ready")
        (l_made, mx_ready, shifted, e_ready, sum_done, rinv_ready, d_ready, d_read, dh_ready, dl_ready,
         x_made) = (
            st.sem(n) for n in ("l_made", "mx_ready", "shifted", "e_ready", "sum_done", "rinv_ready", "d_ready",
                                "d_read", "dh_ready", "dl_ready", "x_made"))
        block = ctx.enter_context(nc.Block())

        def earlier(t, j, s):
            return (t, j - s) if j >= s else (t - (s - j + 1) // 2, (j - s) % 2)

        @block.sync
        def _(sync):
            sync.dma_start(w.we[:], io["expert_w"].rearrange("n d h -> d n h")).then_inc(w.we_loaded, 16)
            sync.dma_start(w.beT[:], io["expert_bT"]).then_inc(w.be_loaded, 16)

        @block.tensor
        def _(pe):
            def logits(t, j):
                pe.wait_ge(x_ready, t.after(1, 1))
                reach(pe, e_ready, t.after(2, j - 1))
                for n, (xs, ws) in enumerate(((xh, w.w1h), (xl, w.w1h), (xh, w.w1l))):
                    for i in range(2):
                        c = (2 * j + i) * 512
                        ins = pe.matmul(psL[j][:, i, :], xs[t.par][:], ws[:, c:c + 512], start=n == 0, stop=n == 2)
                ins.then_inc(l_made, 1)

            def gather(t, j):
                first, last = t.known and t.n == 0, t.known and t.n == TILES - 1
                if j == 0:
                    pe.wait_ge(x2_ready, t.after(1, 1))
                    pe.wait_ge(x2l_ready, t.after(1, 1))
                pe.wait_ge(d_ready, t.after(2, j + 1))
                pe.matmul(psX[:, 2 * j + 1, :], x2[t.par][:], dd[t.par][j][:, 1, :], start=first, stop=last)\
                    .then_inc(d_read, 1)
                pe.wait_ge(dl_ready, t.after(2, j + 1))
                out = psX[:, 2 * j, :]
                pe.matmul(out, x2h[t.par][:], dh[j][:], start=first, stop=False)
                pe.matmul(out, x2h[t.par][:], dl[j][:], start=False, stop=False)
                pe.matmul(out, x2l[t.par][:], dh[j][:], start=False, stop=last).then_inc(x_made, 1)

            def shift(t, j):
                pe.wait_ge(mx_ready, t.after(2, j + 1))
                for i in range(2):
                    ins = pe.matmul(psL[j][:, i, :], w.neg_ident[:],
                                    mx[j][:, i, :].unsqueeze(2).to_broadcast([128, 16, 32]), start=False, stop=True,
                                    skip_group_check=True)
                ins.then_inc(shifted, 1)

            def step(t):
                for j in range(2):
                    if t.within(TILES):
                        logits(t, j)
                    t1, j1 = earlier(t, j, 1)
                    if t1.within(TILES):
                        shift(t1, j1)
                    if (t - 2).within(TILES):
                        gather(t - 2, j)
            steps(pe, TILES, 2, step)

        @block.scalar
        def _(act):
            def copies(t):
                at = bass.ds(t.n * 128, 128)
                reach(act, l_made, t.after(2, -2))
                act.copy(xh[t.par][:], w.xh[:, at].bitcast(F32))
                act.copy(xl[t.par][:], w.xl[:, at].bitcast(F32)).then_inc(x_ready, 1)

            def step(t):
                for j in range(2):
                    if j == 0 and t.known and t.n == 0:
                        copies(t)
                    tu, ju = earlier(t, j, 1)
                    if tu.within(TILES):
                        act.wait_ge(shifted, tu.after(2, ju + 1))
                        reach(act, d_ready, tu.after(2, ju - 1))
                        act.activation(e[ju][:], psL[ju][:].rearrange("p i (n s) -> p i n s", n=16), ACT.Exp)\
                            .then_inc(e_ready, 1)
                    tp = t - 1
                    if j == 1 and tp.within(TILES):
                        reach(act, x_made, tp.after(2, -2))
                        act.copy(x2h[tp.par][:], w.xres[:, bass.ds(tp.n * 128, 128)])
                        act.copy(x2[tp.par][:], w.xres[:, bass.ds(tp.n * 128, 128)]).then_inc(x2_ready, 1)
                    if j == 0 and (t + 1).within(TILES):
                        copies(t + 1)
                    if tp.within(TILES):
                        act.wait_ge(d_ready, tp.after(2, j + 1))
                        reach(act, x_made, tp.after(2, j - 1))
                        act.copy(dh[j][:], dd[tp.par][j][:, 0, :]).then_inc(dh_ready, 1)
            steps(act, TILES, 2, step, ahead=1)

        @block.vector
        def _(dve):
            def step(t):
                for j in range(2):
                    if t.within(TILES):
                        dve.wait_ge(l_made, t.after(2, j + 1))
                        reach(dve, shifted, t.after(2, j - 1))
                        dve.tensor_reduce(mx[j][:], psL[j][:].rearrange("p i (n s) -> p i n s", n=16), X, ALU.max)\
                            .then_inc(mx_ready, 1)
                    tu, ju = earlier(t, j, 1)
                    if tu.within(TILES):
                        dve.wait_ge(e_ready, tu.after(2, ju + 1))
                        reach(dve, rinv_ready, tu.after(2, ju - 1))
                        dve.tensor_reduce(rsum[ju][:].rearrange("p (i n) -> p i n", i=2), e[ju][:], X, ALU.add)\
                            .then_inc(sum_done, 1)
                        dve.wait_ge(sum_done, tu.after(2, ju + 1))
                        reach(dve, d_ready, tu.after(2, ju - 1))
                        dve.reciprocal(rinv[ju][:], rsum[ju][:]).then_inc(rinv_ready, 1)
                    tp = t - 1
                    if j == 1 and tp.within(TILES):
                        dve.wait_ge(x2_ready, tp.after(1, 1))
                        reach(dve, x_made, tp.after(2, -2))
                        dve.tensor_tensor(x2l[tp.par][:], x2[tp.par][:], x2h[tp.par][:], ALU.subtract)\
                            .then_inc(x2l_ready, 1)
            steps(dve, TILES, 2, step)

        @block.gpsimd
        def _(pool):
            def step(t):
                for j in range(2):
                    t3, j3 = earlier(t, j, 3)
                    if t3.within(TILES):
                        pool.wait_ge(dh_ready, t3.after(2, j3 + 1))
                        reach(pool, x_made, t3.after(2, j3 - 1))
                        pool.tensor_tensor(dl[j3][:], dd[t3.par][j3][:, 0, :], dh[j3][:], ALU.subtract)\
                            .then_inc(dl_ready, 1)
                    tu, ju = earlier(t, j, 1)
                    if tu.within(TILES):
                        pool.wait_ge(rinv_ready, tu.after(2, ju + 1))
                        reach(pool, d_read, tu.after(2, ju - 3))
                        reach(pool, dl_ready, tu.after(2, ju - 3))
                        pool.tensor_tensor(
                            dd[tu.par][ju][:].rearrange("p i (n s) -> p i n s", n=16), e[ju][:],
                            rinv[ju][:].rearrange("p (i n) -> p i n", i=2).unsqueeze(3).to_broadcast([128, 2, 16, 32]),
                            ALU.mult).then_inc(d_ready, 1)
            steps(pool, TILES, 2, step)


def run_experts(nc, w, psX):
    with ExitStack() as ctx:
        st = Store(nc, ctx, "expert")
        xt = st.sb("xt", [128, 4, 512])
        stats = st.sb("stats", [128, 16, 6])
        mv = st.sb("mv", [128, 16, 2])
        veps = st.sb("veps", [128, 16])
        rstd = st.sb("rstd", [128, 16])
        n = st.sb("n", [128, 16, 128])
        z = st.sb("z", [128, 16, 128])
        zT = st.sb("zT", [128, 4, 512])
        y = n
        yT = xt
        psT = st.ps("T", [128, 16, 128])
        psY = psX
        (xt_ready, t_made, st_done, mv_ready, ve_done, rstd_ready, n_ready, z_ready, zT_made, zT_ready, y_made,
         y_ready, yT_made, yT_ready, yk_made) = (
            st.sem(n) for n in ("xt_ready", "t_made", "st_done", "mv_ready", "ve_done", "rstd_ready", "n_ready",
                                "z_ready", "zT_made", "zT_ready", "y_made", "y_ready", "yT_made", "yT_ready", "yk_made"))
        block = ctx.enter_context(nc.Block())
        PARTS = [range(4 * c, 4 * c + 4) for c in range(4)]

        @block.vector
        def _(dve):
            for c in range(4):
                dve.tensor_scalar(xt[:, c, :], psX[:, c, :], 65000.0, -33000.0, ALU.min, ALU.max).then_inc(xt_ready, 1)
            def statistics(c):
                dve.wait_ge(t_made, c + 1)
                for k in PARTS[c]:
                    ins = dve.bn_stats(stats[:, k, :], psT[:, k, :])
                ins.then_inc(st_done, 1)
                dve.wait_ge(st_done, c + 1)
                dve.memset(w.scratch[:], 0.0)
                for k in PARTS[c]:
                    ins = dve.bn_aggr(mv[:, k, :], stats[:, k, :])
                ins.then_inc(mv_ready, 1)

            def normalise(c):
                dve.wait_ge(rstd_ready, c + 1)
                for k in PARTS[c]:
                    ins = dve.tensor_scalar(n[:, k, :], psT[:, k, :], mv[:, k, 0:1], rstd[:, k:k + 1],
                                            ALU.subtract, ALU.mult)
                ins.then_inc(n_ready, 1)

            for c in range(4):
                statistics(c)
                if c > 0:
                    normalise(c - 1)
            normalise(3)
            dve.wait_ge(w.be_loaded, 16)
            for c in range(4):
                dve.wait_ge(yT_made, c + 1)
                bias = w.beT[:, 16 * c:16 * c + 16].unsqueeze(1).unsqueeze(3).to_broadcast([128, 4, 16, 8])
                dve.tensor_tensor(yT[:, c, :].rearrange("h (q g p) -> h q g p", q=4, g=16),
                                  psT[:, 4 * c:4 * c + 4, :].rearrange("h k (g q p) -> h q (k g) p", q=4, p=8), bias,
                                  ALU.add).then_inc(yT_ready, 1)

        @block.gpsimd
        def _(pool):
            for c in range(4):
                p = slice(4 * c, 4 * c + 4)
                pool.wait_ge(mv_ready, c + 1)
                pool.tensor_tensor(veps[:, p], mv[:, p, 1], w.eps[:, p], ALU.add).then_inc(ve_done, 1)
                pool.wait_ge(ve_done, c + 1)
                pool.tensor_tensor(rstd[:, p], veps[:, p], w.neg_half[:, p], ALU.pow).then_inc(rstd_ready, 1)

        @block.tensor
        def _(pe):
            def products(c):
                pe.wait_ge(zT_ready, c + 1)
                for g in range(16):
                    out = psY[g % 4 * 32:g % 4 * 32 + 32, c, g // 4 * 128:(g // 4 + 1) * 128]
                    ins = pe.matmul(out, zT[:, c, g * 32:(g + 1) * 32], w.we[:, 16 * c + g, :], start=True, stop=True)
                ins.then_inc(y_made, 1)

            def turn_products(c):
                pe.wait_ge(y_ready, c + 1)
                for k in PARTS[c]:
                    ins = pe.transpose(psT[:, k, :], y[:, k, :], w.ident)
                ins.then_inc(yT_made, 1)

            def turn_ordered(c):
                pe.wait_ge(yT_ready, c + 1)
                for q in range(4):
                    ins = pe.transpose(psT[:, 4 * c + q, :], yT[:, c, q * 128:(q + 1) * 128], w.ident)
                ins.then_inc(yk_made, 1)

            for c in range(4):
                pe.wait_ge(xt_ready, c + 1)
                for k in PARTS[c]:
                    ins = pe.transpose(psT[:, k, :], xt[:, c, k % 4 * 128:(k % 4 + 1) * 128], w.ident)
                ins.then_inc(t_made, 1)
            pe.wait_ge(w.we_loaded, 16)
            for c in range(4):
                pe.wait_ge(z_ready, c + 1)
                for k in PARTS[c]:
                    ins = pe.transpose(psT[:, k, :], z[:, k, :], w.ident)
                ins.then_inc(zT_made, 1)
                if c > 0:
                    products(c - 1)
                if c > 1:
                    turn_products(c - 2)
            products(3)
            turn_products(2)
            turn_ordered(0)
            turn_ordered(1)
            turn_products(3)
            turn_ordered(2)
            turn_ordered(3)

        @block.scalar
        def _(act):
            def keep_products(c):
                act.wait_ge(y_made, c + 1)
                act.copy(y[:, 4 * c:4 * c + 4, :], psY[:, c, :].rearrange("s (k h) -> s k h", k=4)).then_inc(y_ready, 1)

            for c in range(4):
                p = slice(4 * c, 4 * c + 4)
                act.wait_ge(n_ready, c + 1)
                act.activation(z[:, p, :], n[:, p, :], ACT.Tanh).then_inc(z_ready, 1)
                act.wait_ge(zT_made, c + 1)
                act.copy(zT[:, c, :], psT[:, p, :].rearrange("d k s -> d (k s)")).then_inc(zT_ready, 1)
                if c > 1:
                    keep_products(c - 2)
            keep_products(2)
            keep_products(3)
            for c in range(4):
                act.wait_ge(yk_made, c + 1)
                act.copy(w.yk[:].rearrange("s (q c) h -> s q c h", q=4)[:, :, c, :], psT[:, 4 * c:4 * c + 4, :])


def mix_slots(nc, w, out):
    TILES = TOKENS // 256
    with ExitStack() as ctx:
        st = Store(nc, ctx, "mix")
        mg = [st.sb(f"mg{i}", [128, 256]) for i in range(2)]
        m8 = st.sb("m8", [128, 2, 8])
        me = [st.sb(f"me{i}", [128, 2, 16, 8], F32R) for i in range(2)]
        e = [st.sb(f"e{i}", [128, 4, 256]) for i in range(4)]
        sg = [st.sb(f"sg{i}", [128, 256]) for i in range(2)]
        s8 = st.sb("s8", [128, 2, 8])
        r8 = st.sb("r8", [128, 2, 8])
        re = [st.sb(f"re{i}", [128, 2, 16, 8]) for i in range(2)]
        rinv = [st.sb(f"rinv{i}", [128, 256]) for i in range(2)]
        cc = [st.sb(f"c{i}", [128, 4, 256]) for i in range(4)]
        SPLIT = 2
        ch = [st.sb(f"ch{i}", [128, SPLIT, 256], F32R) for i in range(2)]
        cl = [st.sb(f"cl{i}", [128, SPLIT, 256], F32R) for i in range(2)]
        ykh, ykl = st.sb("ykh", [128, 16, 128], F32R), st.sb("ykl", [128, 16, 128], F32R)
        yT = st.sb("yT", [128, 256])
        y = [st.sb(f"y{i}", [128, 2, 128]) for i in range(2)]
        stats = st.sb("stats", [128, 2, 6])
        mv = [st.sb(f"mv{i}", [128, 2, 2]) for i in range(2)]
        veps = st.sb("veps", [128, 2])
        rstd = [st.sb(f"rstd{i}", [128, 2]) for i in range(2)]
        res = [st.sb(f"res{i}", [128, 2, 128]) for i in range(2)]
        psL = [st.ps(f"L{i}", [128, 2, 512]) for i in range(2)]
        psG = st.ps("G", [128, 4, 128])
        psR = st.ps("R", [128, 512])
        psY = st.ps("Y", [128, 256])
        psF = st.ps("F", [128, 2, 128])
        (l_made, mg_ready, g_made, m8_ready, me_ready, shifted, e_ready, sg_ready, sums_made, s8_done, r8_ready,
         re_ready, r_made,
         rinv_ready, c_ready, ch_ready, cl_ready, y_made) = (
            st.sem(n) for n in ("l_made", "mg_ready", "g_made", "m8_ready", "me_ready", "shifted", "e_ready", "sg_ready",
                                "sums_made", "s8_done", "r8_ready", "re_ready", "r_made", "rinv_ready", "c_ready", "ch_ready",
                                "cl_ready", "y_made"))
        yT_ready, f_made, y_done, st_done, mv_ready, ve_done, rstd_ready, res_ready = (
            st.sem(n) for n in ("yT_ready", "f_made", "y_done", "st_done", "mv_ready", "ve_done", "rstd_ready",
                                "res_ready"))
        ykh_ready, ykl_ready = st.sem("ykh_ready"), st.sem("ykl_ready")
        stored = [st.sem("stored0"), st.sem("stored1")]
        block = ctx.enter_context(nc.Block())

        def earlier(t, j, s):
            return t + (j - s) // 4, (j - s) % 4

        @block.sync
        def _(sync):
            def step(k):
                t = k - 3
                if t.within(TILES):
                    sync.wait_ge(res_ready, t.after(1, 1))
                    sync.dma_start(out[bass.ds(t.n * 256, 256), :].rearrange("(b s) d -> s b d", b=2), res[t.par][:])\
                        .then_inc(stored[t.par], 16)
            steps(sync, TILES, 3, step)
            for i in range(2):
                sync.wait_ge(stored[i], 16 * (TILES // 2))

        @block.tensor
        def _(pe):
            def logits(t, j):
                reach(pe, e_ready, t.after(4, j - 1))
                at = bass.ds(t.n * 256, 256)
                for c in range(4):
                    o = psL[j % 2][:, c // 2, c % 2 * 256:(c % 2 + 1) * 256]
                    k = slice((4 * j + c) * 128, (4 * j + c + 1) * 128)
                    pe.matmul(o, w.w2h[:, k], w.xh[:, at], start=(c % 2 == 0), stop=False, skip_group_check=True)
                    pe.matmul(o, w.w2h[:, k], w.xl[:, at], start=False, stop=False, skip_group_check=True)
                    ins = pe.matmul(o, w.w2l[:, k], w.xh[:, at], start=False, stop=True, skip_group_check=True)
                ins.then_inc(l_made, 1)

            def shift(t, j):
                pe.wait_ge(me_ready, t.after(4, j + 1))
                for b in range(2):
                    for i in range(2):
                        o = psL[j % 2][:, i, :].rearrange("p (c t) -> p c t", c=2)[:, :, b * 128:(b + 1) * 128]
                        ins = pe.matmul(o, me[j % 2][:, b, :, :],
                                        w.neg_ident[:].unsqueeze(1).to_broadcast([128, 2, 128]),
                                        start=False, stop=True, skip_group_check=True)
                ins.then_inc(shifted, 1)

            def repeat_inverses(t, j):
                pe.wait_ge(re_ready, t.after(4, j + 1))
                reach(pe, rinv_ready, t.after(4, j))
                for b in range(2):
                    ins = pe.transpose(psR[:, b * 128:(b + 1) * 128], re[j % 2][:, b, :, :], w.ident)
                ins.then_inc(r_made, 1)

            def spread(t, j, half):
                if half == 0:
                    pe.wait_ge(cl_ready, t.after(4, j + 1))
                    if j == 0:
                        reach(pe, yT_ready, t.after(1, 0))
                for c in range(2 * half, 2 * half + 2):
                    if c >= SPLIT:
                        ins = pe.matmul(psY[:], w.yk[:, 4 * j + c, :], cc[j][:, c, :], start=False,
                                        stop=(j == 3 and c == 3))
                        continue
                    y_h, y_l = ykh[:, 4 * j + c, :], ykl[:, 4 * j + c, :]
                    pe.matmul(psY[:], y_h, ch[j % 2][:, c, :], start=(j == 0 and c == 0), stop=False)
                    pe.matmul(psY[:], y_h, cl[j % 2][:, c, :], start=False, stop=False)
                    ins = pe.matmul(psY[:], y_l, ch[j % 2][:, c, :], start=False, stop=(j == 3 and c == 3))
                if half == 1:
                    ins.then_inc(y_made, 1)

            def turn_max(t, j):
                pe.wait_ge(mg_ready, t.after(4, j + 1))
                for b in range(2):
                    ins = pe.transpose(psG[:, b, :], mg[j % 2][:, b * 128:(b + 1) * 128], w.ident)
                ins.then_inc(g_made, 1)

            def turn_sums(t, j):
                pe.wait_ge(sg_ready, t.after(4, j + 1))
                for b in range(2):
                    ins = pe.transpose(psG[:, 2 + b, :], sg[j % 2][:, b * 128:(b + 1) * 128], w.ident)
                ins.then_inc(sums_made, 1)

            def step(k):
                for j in range(4):
                    if k.within(TILES):
                        logits(k, j)
                    t = k - 2
                    if j == 2 and t.within(TILES):
                        pe.wait_ge(yT_ready, t.after(1, 1))
                        reach(pe, y_done, t.after(1, 0))
                        for b in range(2):
                            ins = pe.transpose(psF[:, b, :], yT[:, b * 128:(b + 1) * 128], w.ident)
                        ins.then_inc(f_made, 1)
                    t1, j1 = earlier(k, j, 1)
                    if t1.within(TILES):
                        shift(t1, j1)
                    t6, j6 = earlier(k, j, 6)
                    if t6.within(TILES):
                        spread(t6, j6, 0)
                    t3, j3 = earlier(k, j, 3)
                    if t3.within(TILES):
                        repeat_inverses(t3, j3)
                    if t6.within(TILES):
                        spread(t6, j6, 1)
                    if t1.within(TILES):
                        pe.wait_ge(m8_ready, t1.after(4, j1 + 1))
                    if t3.within(TILES):
                        pe.wait_ge(s8_done, t3.after(4, j3 + 1))
                    if k.within(TILES):
                        turn_max(k, j)
                    t2, j2 = earlier(k, j, 2)
                    if t2.within(TILES):
                        turn_sums(t2, j2)
            pe.wait_ge(ykl_ready, 1)
            steps(pe, TILES, 2, step)

        @block.scalar
        def _(act):
            act.copy(ykh[:], w.yk[:]).then_inc(ykh_ready, 1)

            def step(k):
                for j in range(4):
                    t = k - 2
                    if j == 2 and t.within(TILES):
                        act.wait_ge(y_made, t.after(4, 4))
                        reach(act, f_made, t.after(1, 0))
                        act.copy(yT[:], psY[:]).then_inc(yT_ready, 1)
                    t1, j1 = earlier(k, j, 1)
                    t3, j3 = earlier(k, j, 3)
                    if t1.within(TILES):
                        act.wait_ge(m8_ready, t1.after(4, j1 + 1))
                        reach(act, shifted, t1.after(4, j1 - 1))
                        act.copy(me[j1 % 2][:], m8[:].unsqueeze(2).to_broadcast([128, 2, 16, 8])).then_inc(me_ready, 1)
                    if t3.within(TILES):
                        act.wait_ge(r8_ready, t3.after(4, j3 + 1))
                        reach(act, r_made, t3.after(4, j3 - 1))
                        act.copy(re[j3 % 2][:], r8[:].unsqueeze(2).to_broadcast([128, 2, 16, 8])).then_inc(re_ready, 1)
                    if t1.within(TILES):
                        act.wait_ge(shifted, t1.after(4, j1 + 1))
                        reach(act, c_ready, t1.after(4, j1 - 3))
                        act.activation(e[j1][:], psL[j1 % 2][:].rearrange("p i (c t) -> p (i c) t", c=2), ACT.Exp)\
                            .then_inc(e_ready, 1)
                    if t3.within(TILES):
                        act.wait_ge(r_made, t3.after(4, j3 + 1))
                        reach(act, c_ready, t3.after(4, j3 - 1))
                        act.copy(rinv[j3 % 2][:], psR[:, 0:256]).then_inc(rinv_ready, 1)
                    t4 = k - 1
                    if t4.within(TILES):
                        act.wait_ge(c_ready, t4.after(4, j + 1))
                        reach(act, y_made, t4.after(4, j - 1))
                        act.copy(ch[j % 2][:], cc[j][:, 0:SPLIT, :]).then_inc(ch_ready, 1)
            steps(act, TILES, 2, step)

        @block.vector
        def _(dve):
            dve.wait_ge(ykh_ready, 1)
            dve.tensor_tensor(ykl[:], w.yk[:], ykh[:], ALU.subtract).then_inc(ykl_ready, 1)

            def add_residual(t):
                dve.wait_ge(f_made, t.after(1, 1))
                reach(dve, res_ready, t.after(1, -1))
                dve.tensor_tensor(y[t.par][:], psF[:], w.xres[:, bass.ds(t.n * 256, 256)]
                                  .rearrange("s (b d) -> s b d", b=2), ALU.add).then_inc(y_done, 1)

            def statistics(t):
                dve.wait_ge(y_done, t.after(1, 1))
                for b in range(2):
                    ins = dve.bn_stats(stats[:, b, :], y[t.par][:, b, :])
                ins.then_inc(st_done, 1)
                dve.wait_ge(st_done, t.after(1, 1))
                dve.memset(w.scratch[:], 0.0)
                for b in range(2):
                    ins = dve.bn_aggr(mv[t.par][:, b, :], stats[:, b, :])
                ins.then_inc(mv_ready, 1)

            def normalise(t):
                dve.wait_ge(rstd_ready, t.after(1, 1))
                if not (t.known and t.n < 2):
                    dve.wait_ge(stored[t.par], t.turn(16, 0))
                for b in range(2):
                    ins = dve.tensor_scalar(res[t.par][:, b, :], y[t.par][:, b, :], mv[t.par][:, b, 0:1],
                                            rstd[t.par][:, b:b + 1], ALU.subtract, ALU.mult)
                ins.then_inc(res_ready, 1)

            def step(k):
                for j in range(4):
                    if k.within(TILES):
                        dve.wait_ge(l_made, k.after(4, j + 1))
                        reach(dve, g_made, k.after(4, j - 1))
                        dve.tensor_reduce(mg[j % 2][:], psL[j % 2][:].rearrange("p i (c t) -> p t (i c)", c=2), X,
                                          ALU.max).then_inc(mg_ready, 1)
                    if j == 3 and (k - 2).within(TILES):
                        add_residual(k - 2)
                    if j == 0 and (k - 3).within(TILES):
                        statistics(k - 3)
                    if j == 2 and (k - 3).within(TILES):
                        normalise(k - 3)
                    t1, j1 = earlier(k, j, 1)
                    if t1.within(TILES):
                        dve.wait_ge(e_ready, t1.after(4, j1 + 1))
                        reach(dve, sums_made, t1.after(4, j1 - 1))
                        dve.tensor_reduce(sg[j1 % 2][:], e[j1][:].rearrange("p c t -> p t c"), X, ALU.add)\
                            .then_inc(sg_ready, 1)
                    t2, j2 = earlier(k, j, 2)
                    if t2.within(TILES):
                        dve.wait_ge(sums_made, t2.after(4, j2 + 1))
                    if k.within(TILES):
                        dve.wait_ge(g_made, k.after(4, j + 1))
                        reach(dve, me_ready, k.after(4, j))
                        dve.tensor_reduce(m8[:], psG[:, 0:2, :].rearrange("t b (g p) -> t b p g", g=16), X,
                                          ALU.max).then_inc(m8_ready, 1)
                    if t2.within(TILES):
                        reach(dve, r8_ready, t2.after(4, j2))
                        dve.tensor_reduce(s8[:], psG[:, 2:4, :].rearrange("t b (g p) -> t b p g", g=16), X, ALU.add)\
                            .then_inc(s8_done, 1)
                        dve.wait_ge(s8_done, t2.after(4, j2 + 1))
                        reach(dve, re_ready, t2.after(4, j2))
                        dve.reciprocal(r8[:], s8[:]).then_inc(r8_ready, 1)
            steps(dve, TILES, 3, step)

        @block.gpsimd
        def _(pool):
            def step(k):
                for j in range(4):
                    t5, j5 = earlier(k, j, 5)
                    if t5.within(TILES):
                        pool.wait_ge(ch_ready, t5.after(4, j5 + 1))
                        pool.tensor_tensor(cl[j5 % 2][:], cc[j5][:, 0:SPLIT, :], ch[j5 % 2][:], ALU.subtract)\
                            .then_inc(cl_ready, 1)
                    t3, j3 = earlier(k, j, 3)
                    if t3.within(TILES):
                        pool.wait_ge(rinv_ready, t3.after(4, j3 + 1))
                        reach(pool, y_made, t3.after(4, j3 - 3))
                        pool.tensor_tensor(cc[j3][:], e[j3][:],
                                           rinv[j3 % 2][:].unsqueeze(1).to_broadcast([128, 4, 256]), ALU.mult)\
                            .then_inc(c_ready, 1)
                    t = k - 3
                    if j == 0 and t.within(TILES):
                        pool.wait_ge(mv_ready, t.after(1, 1))
                        pool.tensor_tensor(veps[:], mv[t.par][:, :, 1], w.eps[:, 0:2], ALU.add).then_inc(ve_done, 1)
                        pool.wait_ge(ve_done, t.after(1, 1))
                        pool.tensor_tensor(rstd[t.par][:], veps[:], w.neg_half[:, 0:2], ALU.pow).then_inc(rstd_ready, 1)
            steps(pool, TILES, 3, step)


class Weights:
    pass


def decoder_block(nc, io, out):
    with ExitStack() as ctx:
        st = Store(nc, ctx, "kept")
        w = Weights()
        w.xres = st.sb("xres", [128, TOKENS])
        w.xh = st.sb("xh", [128, TOKENS], F32R)
        w.xl = st.sb("xl", [128, TOKENS], F32R)
        w.consts = st.sb("consts", [128, C_END])
        w.ident = w.consts[:, C_IDENT:C_HEAD]
        w.head = w.consts[:, C_HEAD:C_END]
        w.ident16 = st.sb("ident16", [128, 128], F16)
        w.neg_ident = st.sb("neg_ident", [128, 128], F32R)
        w.neg_half = st.sb("neg_half", [128, 16])
        w.eps = st.sb("eps", [128, 16])
        w.scratch = st.sb("scratch", [128, 1])
        w.mask_loaded = st.sem("mask_loaded")
        w.phi_loaded, w.we_loaded, w.be_loaded = (st.sem(n) for n in ("phi_loaded", "we_loaded", "be_loaded"))
        w.phi = st.sb("phi", [128, 16, 128])
        w.bias = st.sb("bias", [128, 16])
        with ExitStack() as first:
            sf = Store(nc, first, "first")
            w.x1T = sf.sb("x1T", [128, TOKENS])
            w.m, w.w2, w.b2 = sf.sb("m", [128, 128]), sf.sb("w2", [128, 128]), sf.sb("b2", [128, 128])
            w.cvec, w.avec, w.beta = sf.sb("cvec", [128, 1]), sf.sb("avec", [128, 1]), sf.sb("beta", [128, 1])
            w.xq, w.xqs, w.xo = sf.sb("xq", [128, 128]), sf.sb("xqs", [128, 128]), sf.sb("xo", [128, 128])
            w.xk, w.xv = sf.sb("xk", [CD, 128]), sf.sb("xv", [CD, 128])
            w.mask = sf.sb("mask", [128, B * J], U8)
            w.fill = sf.sb("fill", [128, B * JP], BF16)
            w.ones16 = sf.sb("ones16", [128, 128], BF16)
            setup(nc, io, w)
            attention(nc, io, w)
            attend_context(nc, io, w)
        w.yk = w.phi
        w.w2h, w.w2l = st.sb("w2h", [128, NP], F32R), st.sb("w2l", [128, NP], F32R)
        with ExitStack() as banks:
            sl = Store(nc, banks, "slots")
            psX = sl.ps("X", [128, 4, 512])
            w.we = sl.sb("we", [128, EXPERTS, 128])
            w.beT = sl.sb("beT", [128, EXPERTS])
            with ExitStack() as second:
                ss = Store(nc, second, "second")
                w.w1h, w.w1l = ss.sb("w1h", [128, NP], F32R), ss.sb("w1l", [128, NP], F32R)
                prepare_slots(nc, w)
                gather_slots(nc, io, w, psX)
            run_experts(nc, w, psX)
        mix_slots(nc, w, out)


def kernel(**inputs):
    import concourse.bacc as bacc
    from concourse.bass_utils import run_bass_kernel_spmd

    get = lambda name: np.asarray(inputs[name])
    x = get("x").reshape(TOKENS, D)
    context = np.zeros((B, JP, CD), np.float32)
    context[:, :J] = get("ctx_768")
    host = {
        "x": x, "xT": x.T, "ctxT": context.reshape(B * JP, CD).T, "mask": get("mask_BxS2_bf1").reshape(1, B * J),
        "w_qkvT": get("L0_attn_W_qkv").T, "b_qkv": get("L0_attn_b_qkv").reshape(3, D).T,
        "w_proj": get("L0_attn_W_proj"), "b_proj": get("L0_attn_b_proj").reshape(1, D),
        "xq": get("L0_xattn_Wq"), "xk": get("L0_xattn_Wk"), "xv": get("L0_xattn_Wv"), "xo": get("L0_xattn_Wo"),
        "phi": get("L0_ffn_phi_w"), "phi_b": get("L0_ffn_phi_b").reshape(16, 128).T,
        "expert_w": get("L0_ffn_expert_w"), "expert_bT": get("L0_ffn_expert_b").T,
        "consts": constants(),
    }
    nc = bacc.Bacc("TRN2", target_bir_lowering=False, num_devices=1)
    arrays, io = {}, {}
    for name, a in host.items():
        a = np.ascontiguousarray(a)
        arrays[f"in_{name}"] = a
        io[name] = nc.dram_tensor(f"in_{name}", a.shape, mybir.dt.from_np(a.dtype), kind="ExternalInput").ap()
    out = nc.dram_tensor("out_0", (TOKENS, D), F32, kind="ExternalOutput").ap()
    decoder_block(nc, io, out)
    result = run_bass_kernel_spmd(nc, [arrays], core_ids=[0])
    return result.results[0]["out_0"].reshape(B, S, D)
```
